# Optimizing a Trainium2 kernel written in Bass

```python
import numpy as np
import jax
import jax.numpy as jnp

def _softmax(x, axis=-1):
    return jax.nn.softmax(x, axis=axis)

def _gelu(x):
    return jax.nn.gelu(x, approximate=True)

def _silu(x):
    return jax.nn.silu(x)

def _sigmoid(x):
    return jax.nn.sigmoid(x)

def _layernorm(x, axis=-1, eps=1e-05):
    m = jnp.mean(x, axis=axis, keepdims=True)
    v = jnp.var(x, axis=axis, keepdims=True)
    return (x - m) / jnp.sqrt(v + eps)

def _scatter_add(tgt, idx, src, axis=0):
    return tgt.at[idx].add(src)

def _segment_sum(src, seg, n):
    return jax.ops.segment_sum(src, seg, n)
kernel_name = 'mk_gps_d2_gnn_r32_b6d010'

def setup_inputs(seed: int=0):
    np.random.seed(seed)
    _w = jnp.asarray

    def _rec_inputs():
        import jax
        import jax.numpy as jnp
        _gk = jax.random.key(seed)
        x = -8.776e-05 + 1 * jax.random.normal(jax.random.fold_in(_gk, 1), (625, 256), jnp.float32)
        src = jax.random.randint(jax.random.fold_in(_gk, 2), (20000,), 0, 625, jnp.int32)
        dst = jax.random.randint(jax.random.fold_in(_gk, 3), (20000,), 0, 625, jnp.int32)
        _o = jnp.argsort(dst, stable=True)
        src = src[_o]
        dst = dst[_o]
        return (x, src, dst)
    x, src, dst = _rec_inputs()

    def _L0_gnn_setup():
        import jax, jax.numpy as jnp
        import numpy as np
        N = 625
        E = 10000
        D = 256
        NEG_SLOPE = 0.2
        BN_EPS = 1e-05

        def gat_layer(x, src, dst, W, a_s, a_d, b):
            h = x @ W
            alpha_s = h @ a_s
            alpha_d = h @ a_d
            e = jax.nn.leaky_relu(alpha_s[src] + alpha_d[dst], NEG_SLOPE)
            m = jax.ops.segment_max(e, dst, num_segments=N)
            m = jnp.where(jnp.isfinite(m), m, 0.0)
            p = jnp.exp(e - m[dst])
            denom = jax.ops.segment_sum(p, dst, num_segments=N)
            coef = p / (denom[dst] + 1e-16)
            out = jax.ops.segment_sum(coef[:, None] * h[src], dst, num_segments=N)
            return out + b

        def batchnorm(x, gamma, beta):
            mu = x.mean(axis=0)
            var = x.var(axis=0)
            return (x - mu) * jax.lax.rsqrt(var + BN_EPS) * gamma + beta
        key = jax.random.key(seed)
        ks = jax.random.split(key, 24)
        inp = {'x': jax.random.normal(ks[0], (N, D), dtype=jnp.float32), 'edge_src': jax.random.randint(ks[1], (E,), 0, N), 'edge_dst': jax.random.randint(ks[2], (E,), 0, N)}
        w_scale = 1.0 / np.sqrt(D)
        for l in range(3):
            inp[f'W{l}'] = jax.random.normal(ks[3 + 4 * l], (D, D), dtype=jnp.float32) * w_scale
            inp[f'a_src{l}'] = jax.random.normal(ks[4 + 4 * l], (D,), dtype=jnp.float32) * w_scale
            inp[f'a_dst{l}'] = jax.random.normal(ks[5 + 4 * l], (D,), dtype=jnp.float32) * w_scale
            inp[f'b{l}'] = jnp.zeros((D,), dtype=jnp.float32)
        for l in range(2):
            inp[f'gamma{l}'] = jnp.ones((D,), dtype=jnp.float32)
            inp[f'beta{l}'] = jnp.zeros((D,), dtype=jnp.float32)
        return inp
    _L0_gnn_all = _L0_gnn_setup()
    _L0_gnn_in = {k: v for k, v in _L0_gnn_all.items() if k in ('W0', 'a_src0', 'a_dst0', 'b0', 'W1', 'a_src1', 'a_dst1', 'b1', 'W2', 'a_src2', 'a_dst2', 'b2', 'gamma0', 'beta0', 'gamma1', 'beta1')}
    del _L0_gnn_all

    def _L0_mix_setup():
        import jax, jax.numpy as jnp
        import numpy as np
        EMB, HEADS, DEPTH, SEQ, BATCH = (256, 8, 4, 256, 4)
        DH = EMB // HEADS
        FF = 4 * EMB
        EPS = 1e-05

        def _layernorm(x, g, b):
            mu = x.mean(-1, keepdims=True)
            var = ((x - mu) ** 2).mean(-1, keepdims=True)
            return (x - mu) * jax.lax.rsqrt(var + EPS) * g + b

        def _linear_attn(x, Wq, Wk, Wv, Wo, bo):
            b, n, dm = x.shape
            split = lambda t: t.reshape(b, n, HEADS, DH).transpose(0, 2, 1, 3)
            scale = DH ** (-0.25)
            q = jax.nn.softmax(split(x @ Wq) * scale, axis=-1)
            k = jax.nn.softmax(split(x @ Wk) * scale, axis=-2)
            v = split(x @ Wv)
            context = jnp.einsum('bhnd,bhne->bhde', k, v)
            out = jnp.einsum('bhnd,bhde->bhne', q, context)
            out = out.transpose(0, 2, 1, 3).reshape(b, n, dm)
            return out @ Wo + bo

        def _forward(x, Wq, Wk, Wv, Wo, bo, ln1_g, ln1_b, W1, b1, W2, b2, ln2_g, ln2_b):
            for i in range(DEPTH):
                h = _layernorm(x, ln1_g[i], ln1_b[i])
                x = x + _linear_attn(h, Wq[i], Wk[i], Wv[i], Wo[i], bo[i])
                h = _layernorm(x, ln2_g[i], ln2_b[i])
                x = x + (jax.nn.gelu(h @ W1[i] + b1[i], approximate=False) @ W2[i] + b2[i])
            return x
        key = jax.random.key(seed)
        ks = jax.random.split(key, 8)
        w = lambda k, shape: jax.random.normal(k, shape, dtype=jnp.float32) * 0.02
        D = DEPTH
        return {'x': jax.random.normal(ks[0], (BATCH, SEQ, EMB), dtype=jnp.float32), 'Wq': w(ks[1], (D, EMB, EMB)), 'Wk': w(ks[2], (D, EMB, EMB)), 'Wv': w(ks[3], (D, EMB, EMB)), 'Wo': w(ks[4], (D, EMB, EMB)), 'bo': jnp.zeros((D, EMB), jnp.float32), 'ln1_g': jnp.ones((D, EMB), jnp.float32), 'ln1_b': jnp.zeros((D, EMB), jnp.float32), 'W1': w(ks[5], (D, EMB, FF)), 'b1': jnp.zeros((D, FF), jnp.float32), 'W2': w(ks[6], (D, FF, EMB)), 'b2': jnp.zeros((D, EMB), jnp.float32), 'ln2_g': jnp.ones((D, EMB), jnp.float32), 'ln2_b': jnp.zeros((D, EMB), jnp.float32)}
    _L0_mix_all = _L0_mix_setup()
    _L0_mix_in = {k: v for k, v in _L0_mix_all.items() if k in ('Wq', 'Wk', 'Wv', 'Wo', 'bo', 'ln1_g', 'ln1_b', 'W1', 'b1', 'W2', 'b2', 'ln2_g', 'ln2_b')}
    del _L0_mix_all

    def _L0_ffn_setup():
        import jax, jax.numpy as jnp
        import numpy as np
        B, S, D, H, E, K = (8, 256, 256, 1024, 8, 2)
        key = jax.random.key(seed)
        ks = jax.random.split(key, 7)
        s_in = 1.0 / np.sqrt(D)
        s_hid = 1.0 / np.sqrt(H)
        return {'x': jax.random.normal(ks[0], (B, S, D), dtype=jnp.float32), 'Wg': jax.random.uniform(ks[1], (E, D), jnp.float32, -s_in, s_in), 'bg': jax.random.uniform(ks[2], (E,), jnp.float32, -s_in, s_in), 'W1': jax.random.uniform(ks[3], (E, H, D), jnp.float32, -s_in, s_in), 'b1': jax.random.uniform(ks[4], (E, H), jnp.float32, -s_in, s_in), 'W2': jax.random.uniform(ks[5], (E, D, H), jnp.float32, -s_hid, s_hid), 'b2': jax.random.uniform(ks[6], (E, D), jnp.float32, -s_hid, s_hid)}
    _L0_ffn_all = _L0_ffn_setup()
    _L0_ffn_in = {k: v for k, v in _L0_ffn_all.items() if k in ('Wg', 'bg', 'W1', 'b1', 'W2', 'b2')}
    del _L0_ffn_all

    def _L1_gnn_setup():
        import jax, jax.numpy as jnp
        import numpy as np
        N_NODES = 50000
        N_EDGES = 25000
        DIM = 256
        NUM_HEADS = 8
        key = jax.random.key(seed)
        k_x, k_wu, k_bu, k_wv, k_src, k_dst = jax.random.split(key, 6)
        x = jax.random.normal(k_x, (N_NODES, DIM), dtype=jnp.float32)
        W_u = jax.random.normal(k_wu, (NUM_HEADS, DIM), dtype=jnp.float32) * (1.0 / np.sqrt(DIM))
        b_u = jax.random.normal(k_bu, (NUM_HEADS,), dtype=jnp.float32) * 0.01
        W_v = jax.random.normal(k_wv, (NUM_HEADS, DIM), dtype=jnp.float32) * (1.0 / np.sqrt(DIM))
        src = jax.random.randint(k_src, (N_EDGES,), 0, N_NODES, dtype=jnp.int32)
        dst = jax.random.randint(k_dst, (N_EDGES,), 0, N_NODES, dtype=jnp.int32)
        return {'x': x, 'W_u': W_u, 'b_u': b_u, 'W_v': W_v, 'src': src, 'dst': dst}
    _L1_gnn_all = _L1_gnn_setup()
    _L1_gnn_in = {k: v for k, v in _L1_gnn_all.items() if k in ('W_u', 'b_u', 'W_v')}
    del _L1_gnn_all

    def _L1_mix_setup():
        import jax, jax.numpy as jnp
        import numpy as np
        NHEAD = 8
        ATT_EPS = 1e-06
        LN_EPS = 1e-05

        def _layernorm(x, g, b):
            mu = jnp.mean(x, axis=-1, keepdims=True)
            var = jnp.mean(jnp.square(x - mu), axis=-1, keepdims=True)
            return (x - mu) * jax.lax.rsqrt(var + LN_EPS) * g + b
        key = jax.random.key(seed)
        ks = jax.random.split(key, 7)
        N, L, C = (4, 512, 256)
        s = 1.0 / np.sqrt(C)
        return {'x': jax.random.normal(ks[0], (N, L, C), jnp.float32), 'Wq': jax.random.normal(ks[1], (C, C), jnp.float32) * s, 'Wk': jax.random.normal(ks[2], (C, C), jnp.float32) * s, 'Wv': jax.random.normal(ks[3], (C, C), jnp.float32) * s, 'Wm': jax.random.normal(ks[4], (C, C), jnp.float32) * s, 'W1': jax.random.normal(ks[5], (2 * C, 2 * C), jnp.float32) * (1.0 / np.sqrt(2 * C)), 'W2': jax.random.normal(ks[6], (2 * C, C), jnp.float32) * (1.0 / np.sqrt(2 * C)), 'g1': jnp.ones((C,), jnp.float32), 'b1': jnp.zeros((C,), jnp.float32), 'g2': jnp.ones((C,), jnp.float32), 'b2': jnp.zeros((C,), jnp.float32)}
    _L1_mix_all = _L1_mix_setup()
    _L1_mix_in = {k: v for k, v in _L1_mix_all.items() if k in ('Wq', 'Wk', 'Wv', 'Wm', 'W1', 'W2', 'g1', 'b1', 'g2', 'b2')}
    del _L1_mix_all

    def _L1_ffn_setup():
        import jax, jax.numpy as jnp
        import numpy as np
        B, S, H, F, E, K = (8, 128, 256, 512, 16, 2)
        EPS = 1e-05
        key = jax.random.key(seed)
        ks = jax.random.split(key, 9)
        sc = 0.02
        return {'x': jax.random.normal(ks[0], (B, S, H), dtype=jnp.float32), 'gate_w': jax.random.normal(ks[1], (H, E), dtype=jnp.float32) * sc, 'gate_b': jnp.zeros((E,), dtype=jnp.float32), 'w1': jax.random.normal(ks[2], (E, H, F), dtype=jnp.float32) * sc, 'b1': jnp.zeros((E, F), dtype=jnp.float32), 'w2': jax.random.normal(ks[3], (E, F, H), dtype=jnp.float32) * sc, 'b2': jnp.zeros((E, H), dtype=jnp.float32), 'gamma': jnp.ones((H,), dtype=jnp.float32), 'beta': jnp.zeros((H,), dtype=jnp.float32)}
    _L1_ffn_all = _L1_ffn_setup()
    _L1_ffn_in = {k: v for k, v in _L1_ffn_all.items() if k in ('gate_w', 'gate_b', 'w1', 'b1', 'w2', 'b2', 'gamma', 'beta')}
    del _L1_ffn_all
    return {'x': x, 'src': src, 'dst': dst, 'L0_gnn_W0': _L0_gnn_in['W0'], 'L0_gnn_a_src0': _L0_gnn_in['a_src0'], 'L0_gnn_a_dst0': _L0_gnn_in['a_dst0'], 'L0_gnn_b0': _L0_gnn_in['b0'], 'L0_gnn_W1': _L0_gnn_in['W1'], 'L0_gnn_a_src1': _L0_gnn_in['a_src1'], 'L0_gnn_a_dst1': _L0_gnn_in['a_dst1'], 'L0_gnn_b1': _L0_gnn_in['b1'], 'L0_gnn_W2': _L0_gnn_in['W2'], 'L0_gnn_a_src2': _L0_gnn_in['a_src2'], 'L0_gnn_a_dst2': _L0_gnn_in['a_dst2'], 'L0_gnn_b2': _L0_gnn_in['b2'], 'L0_gnn_gamma0': _L0_gnn_in['gamma0'], 'L0_gnn_beta0': _L0_gnn_in['beta0'], 'L0_gnn_gamma1': _L0_gnn_in['gamma1'], 'L0_gnn_beta1': _L0_gnn_in['beta1'], 'L0_mix_Wq': _L0_mix_in['Wq'], 'L0_mix_Wk': _L0_mix_in['Wk'], 'L0_mix_Wv': _L0_mix_in['Wv'], 'L0_mix_Wo': _L0_mix_in['Wo'], 'L0_mix_bo': _L0_mix_in['bo'], 'L0_mix_ln1_g': _L0_mix_in['ln1_g'], 'L0_mix_ln1_b': _L0_mix_in['ln1_b'], 'L0_mix_W1': _L0_mix_in['W1'], 'L0_mix_b1': _L0_mix_in['b1'], 'L0_mix_W2': _L0_mix_in['W2'], 'L0_mix_b2': _L0_mix_in['b2'], 'L0_mix_ln2_g': _L0_mix_in['ln2_g'], 'L0_mix_ln2_b': _L0_mix_in['ln2_b'], 'L0_ffn_Wg': _L0_ffn_in['Wg'], 'L0_ffn_bg': _L0_ffn_in['bg'], 'L0_ffn_W1': _L0_ffn_in['W1'], 'L0_ffn_b1': _L0_ffn_in['b1'], 'L0_ffn_W2': _L0_ffn_in['W2'], 'L0_ffn_b2': _L0_ffn_in['b2'], 'L1_gnn_W_u': _L1_gnn_in['W_u'], 'L1_gnn_b_u': _L1_gnn_in['b_u'], 'L1_gnn_W_v': _L1_gnn_in['W_v'], 'L1_mix_Wq': _L1_mix_in['Wq'], 'L1_mix_Wk': _L1_mix_in['Wk'], 'L1_mix_Wv': _L1_mix_in['Wv'], 'L1_mix_Wm': _L1_mix_in['Wm'], 'L1_mix_W1': _L1_mix_in['W1'], 'L1_mix_W2': _L1_mix_in['W2'], 'L1_mix_g1': _L1_mix_in['g1'], 'L1_mix_b1': _L1_mix_in['b1'], 'L1_mix_g2': _L1_mix_in['g2'], 'L1_mix_b2': _L1_mix_in['b2'], 'L1_ffn_gate_w': _L1_ffn_in['gate_w'], 'L1_ffn_gate_b': _L1_ffn_in['gate_b'], 'L1_ffn_w1': _L1_ffn_in['w1'], 'L1_ffn_b1': _L1_ffn_in['b1'], 'L1_ffn_w2': _L1_ffn_in['w2'], 'L1_ffn_b2': _L1_ffn_in['b2'], 'L1_ffn_gamma': _L1_ffn_in['gamma'], 'L1_ffn_beta': _L1_ffn_in['beta']}

def reference(x, src, dst, L0_gnn_W0, L0_gnn_a_src0, L0_gnn_a_dst0, L0_gnn_b0, L0_gnn_W1, L0_gnn_a_src1, L0_gnn_a_dst1, L0_gnn_b1, L0_gnn_W2, L0_gnn_a_src2, L0_gnn_a_dst2, L0_gnn_b2, L0_gnn_gamma0, L0_gnn_beta0, L0_gnn_gamma1, L0_gnn_beta1, L0_mix_Wq, L0_mix_Wk, L0_mix_Wv, L0_mix_Wo, L0_mix_bo, L0_mix_ln1_g, L0_mix_ln1_b, L0_mix_W1, L0_mix_b1, L0_mix_W2, L0_mix_b2, L0_mix_ln2_g, L0_mix_ln2_b, L0_ffn_Wg, L0_ffn_bg, L0_ffn_W1, L0_ffn_b1, L0_ffn_W2, L0_ffn_b2, L1_gnn_W_u, L1_gnn_b_u, L1_gnn_W_v, L1_mix_Wq, L1_mix_Wk, L1_mix_Wv, L1_mix_Wm, L1_mix_W1, L1_mix_W2, L1_mix_g1, L1_mix_b1, L1_mix_g2, L1_mix_b2, L1_ffn_gate_w, L1_ffn_gate_b, L1_ffn_w1, L1_ffn_b1, L1_ffn_w2, L1_ffn_b2, L1_ffn_gamma, L1_ffn_beta):
    import jax
    import jax.numpy as jnp

    def _L0_gnn_ref(x, edge_src, edge_dst, W0, a_src0, a_dst0, b0, W1, a_src1, a_dst1, b1, W2, a_src2, a_dst2, b2, gamma0, beta0, gamma1, beta1):
        import jax, jax.numpy as jnp
        import numpy as np
        N = 625
        E = 10000
        D = 256
        NEG_SLOPE = 0.2
        BN_EPS = 1e-05

        def gat_layer(x, src, dst, W, a_s, a_d, b):
            h = x @ W
            alpha_s = h @ a_s
            alpha_d = h @ a_d
            e = jax.nn.leaky_relu(alpha_s[src] + alpha_d[dst], NEG_SLOPE)
            m = jax.ops.segment_max(e, dst, num_segments=N)
            m = jnp.where(jnp.isfinite(m), m, 0.0)
            p = jnp.exp(e - m[dst])
            denom = jax.ops.segment_sum(p, dst, num_segments=N)
            coef = p / (denom[dst] + 1e-16)
            out = jax.ops.segment_sum(coef[:, None] * h[src], dst, num_segments=N)
            return out + b

        def batchnorm(x, gamma, beta):
            mu = x.mean(axis=0)
            var = x.var(axis=0)
            return (x - mu) * jax.lax.rsqrt(var + BN_EPS) * gamma + beta
        h = gat_layer(x, edge_src, edge_dst, W0, a_src0, a_dst0, b0)
        h = jax.nn.relu(batchnorm(h, gamma0, beta0))
        h = gat_layer(h, edge_src, edge_dst, W1, a_src1, a_dst1, b1)
        h = jax.nn.relu(batchnorm(h, gamma1, beta1))
        out = gat_layer(h, edge_src, edge_dst, W2, a_src2, a_dst2, b2)
        return out

    def _L0_mix_ref(x, Wq, Wk, Wv, Wo, bo, ln1_g, ln1_b, W1, b1, W2, b2, ln2_g, ln2_b):
        import jax, jax.numpy as jnp
        import numpy as np
        EMB, HEADS, DEPTH, SEQ, BATCH = (256, 8, 4, 256, 4)
        DH = EMB // HEADS
        FF = 4 * EMB
        EPS = 1e-05

        def _layernorm(x, g, b):
            mu = x.mean(-1, keepdims=True)
            var = ((x - mu) ** 2).mean(-1, keepdims=True)
            return (x - mu) * jax.lax.rsqrt(var + EPS) * g + b

        def _linear_attn(x, Wq, Wk, Wv, Wo, bo):
            b, n, dm = x.shape
            split = lambda t: t.reshape(b, n, HEADS, DH).transpose(0, 2, 1, 3)
            scale = DH ** (-0.25)
            q = jax.nn.softmax(split(x @ Wq) * scale, axis=-1)
            k = jax.nn.softmax(split(x @ Wk) * scale, axis=-2)
            v = split(x @ Wv)
            context = jnp.einsum('bhnd,bhne->bhde', k, v)
            out = jnp.einsum('bhnd,bhde->bhne', q, context)
            out = out.transpose(0, 2, 1, 3).reshape(b, n, dm)
            return out @ Wo + bo

        def _forward(x, Wq, Wk, Wv, Wo, bo, ln1_g, ln1_b, W1, b1, W2, b2, ln2_g, ln2_b):
            for i in range(DEPTH):
                h = _layernorm(x, ln1_g[i], ln1_b[i])
                x = x + _linear_attn(h, Wq[i], Wk[i], Wv[i], Wo[i], bo[i])
                h = _layernorm(x, ln2_g[i], ln2_b[i])
                x = x + (jax.nn.gelu(h @ W1[i] + b1[i], approximate=False) @ W2[i] + b2[i])
            return x
        return _forward(x, Wq, Wk, Wv, Wo, bo, ln1_g, ln1_b, W1, b1, W2, b2, ln2_g, ln2_b)

    def _L0_ffn_ref(x, Wg, bg, W1, b1, W2, b2):
        import jax, jax.numpy as jnp
        import numpy as np
        B, S, D, H, E, K = (8, 256, 256, 1024, 8, 2)
        gate_scores = jnp.einsum('bsd,ed->bse', x, Wg) + bg
        topk_scores, topk_idx = jax.lax.top_k(gate_scores, K)
        topk_probs = jax.nn.softmax(topk_scores, axis=-1)
        combine = jnp.sum(topk_probs[..., None] * jax.nn.one_hot(topk_idx, E, dtype=x.dtype), axis=-2)
        out = jnp.zeros_like(x)
        for e in range(E):
            h = jax.nn.relu(jnp.einsum('bsd,hd->bsh', x, W1[e]) + b1[e])
            y = jnp.einsum('bsh,dh->bsd', h, W2[e]) + b2[e]
            out = out + combine[..., e:e + 1] * y
        return out

    def _L1_gnn_ref(x, W_u, b_u, W_v, src, dst):
        import jax, jax.numpy as jnp
        import numpy as np
        N_NODES = 50000
        N_EDGES = 25000
        DIM = 256
        NUM_HEADS = 8
        n_nodes, dim = x.shape
        num_heads = W_u.shape[0]
        head_dim = dim // num_heads
        s_u = x @ W_u.T + b_u
        s_v = x @ W_v.T
        e = s_u[src] + s_v[dst]
        e = jnp.where(e >= 0, e, 0.2 * e)
        m = jax.ops.segment_max(e, dst, num_segments=n_nodes)
        e_exp = jnp.exp(e - m[dst])
        denom = jax.ops.segment_sum(e_exp, dst, num_segments=n_nodes)
        probs = e_exp / denom[dst]
        xh = x.reshape(n_nodes, head_dim, num_heads)
        msg = xh[src] * probs[:, None, :]
        out = jax.ops.segment_sum(msg, dst, num_segments=n_nodes)
        return out.reshape(n_nodes, dim)

    def _L1_mix_ref(x, Wq, Wk, Wv, Wm, W1, W2, g1, b1, g2, b2):
        import jax, jax.numpy as jnp
        import numpy as np
        NHEAD = 8
        ATT_EPS = 1e-06
        LN_EPS = 1e-05

        def _layernorm(x, g, b):
            mu = jnp.mean(x, axis=-1, keepdims=True)
            var = jnp.mean(jnp.square(x - mu), axis=-1, keepdims=True)
            return (x - mu) * jax.lax.rsqrt(var + LN_EPS) * g + b
        N, L, C = x.shape
        H = NHEAD
        D = C // H
        q = (x @ Wq).reshape(N, L, H, D)
        k = (x @ Wk).reshape(N, L, H, D)
        v = (x @ Wv).reshape(N, L, H, D)
        Q = jax.nn.elu(q) + 1.0
        K = jax.nn.elu(k) + 1.0
        v = v / L
        KV = jnp.einsum('nshd,nshv->nhdv', K, v)
        Z = 1.0 / (jnp.einsum('nlhd,nhd->nlh', Q, K.sum(axis=1)) + ATT_EPS)
        msg = jnp.einsum('nlhd,nhdv,nlh->nlhv', Q, KV, Z) * L
        msg = msg.reshape(N, L, C) @ Wm
        msg = _layernorm(msg, g1, b1)
        h = jnp.concatenate([x, msg], axis=-1) @ W1
        h = jax.nn.relu(h) @ W2
        msg = _layernorm(h, g2, b2)
        return x + msg

    def _L1_ffn_ref(x, gate_w, gate_b, w1, b1, w2, b2, gamma, beta):
        import jax, jax.numpy as jnp
        import numpy as np
        B, S, H, F, E, K = (8, 128, 256, 512, 16, 2)
        EPS = 1e-05
        gate_logits = x @ gate_w + gate_b
        topk_vals, topk_idx = jax.lax.top_k(gate_logits, K)
        topk_w = jax.nn.softmax(topk_vals, axis=-1)
        h = jax.nn.relu(jnp.einsum('bsh,ehf->bsef', x, w1) + b1)
        expert_out = jnp.einsum('bsef,efh->bseh', h, w2) + b2
        sel = jnp.take_along_axis(expert_out, topk_idx[:, :, :, None], axis=2)
        moe = jnp.sum(topk_w[..., None] * sel, axis=2)
        y = x + moe
        mu = jnp.mean(y, axis=-1, keepdims=True)
        var = jnp.var(y, axis=-1, keepdims=True)
        return (y - mu) / jnp.sqrt(var + EPS) * gamma + beta
    xn = _layernorm(x, axis=-1)
    x = x + _L0_gnn_ref(xn, src, dst, L0_gnn_W0, L0_gnn_a_src0, L0_gnn_a_dst0, L0_gnn_b0, L0_gnn_W1, L0_gnn_a_src1, L0_gnn_a_dst1, L0_gnn_b1, L0_gnn_W2, L0_gnn_a_src2, L0_gnn_a_dst2, L0_gnn_b2, L0_gnn_gamma0, L0_gnn_beta0, L0_gnn_gamma1, L0_gnn_beta1) + _L0_mix_ref(xn[None], L0_mix_Wq, L0_mix_Wk, L0_mix_Wv, L0_mix_Wo, L0_mix_bo, L0_mix_ln1_g, L0_mix_ln1_b, L0_mix_W1, L0_mix_b1, L0_mix_W2, L0_mix_b2, L0_mix_ln2_g, L0_mix_ln2_b)[0]
    x = x + _L0_ffn_ref(_layernorm(x, axis=-1)[None], L0_ffn_Wg, L0_ffn_bg, L0_ffn_W1, L0_ffn_b1, L0_ffn_W2, L0_ffn_b2)[0]
    xn = _layernorm(x, axis=-1)
    x = x + _L1_gnn_ref(xn, L1_gnn_W_u, L1_gnn_b_u, L1_gnn_W_v, src, dst) + _L1_mix_ref(xn[None], L1_mix_Wq, L1_mix_Wk, L1_mix_Wv, L1_mix_Wm, L1_mix_W1, L1_mix_W2, L1_mix_g1, L1_mix_b1, L1_mix_g2, L1_mix_b2)[0]
    x = x + _L1_ffn_ref(_layernorm(x, axis=-1)[None], L1_ffn_gate_w, L1_ffn_gate_b, L1_ffn_w1, L1_ffn_b1, L1_ffn_w2, L1_ffn_b2, L1_ffn_gamma, L1_ffn_beta)[0]
    return x

_drawn_inputs = setup_inputs


def setup_inputs(seed=0):
    import zlib

    import numpy as np

    out = dict(_drawn_inputs(seed))
    spreads = {'L0_gnn_b0': (0.0, 2.0),
     'L0_gnn_b1': (0.0, 2.0),
     'L0_gnn_b2': (0.0, 0.1),
     'L0_gnn_gamma0': (1.0, 0.6),
     'L0_gnn_beta0': (0.0, 0.8),
     'L0_gnn_gamma1': (1.0, 0.2),
     'L0_gnn_beta1': (0.0, 0.1),
     'L0_mix_bo': (0.0, 0.1),
     'L0_mix_ln1_g': (1.0, 0.6),
     'L0_mix_ln1_b': (0.0, 0.489),
     'L0_mix_b1': (0.0, 0.1),
     'L0_mix_b2': (0.0, 0.1),
     'L0_mix_ln2_g': (1.0, 0.6),
     'L0_mix_ln2_b': (0.0, 0.465),
     'L1_mix_g1': (1.0, 0.2),
     'L1_mix_b1': (0.0, 0.327),
     'L1_mix_g2': (1.0, 0.2),
     'L1_mix_b2': (0.0, 0.267),
     'L1_ffn_gate_b': (0.0, 0.584),
     'L1_ffn_b1': (0.0, 0.8),
     'L1_ffn_b2': (0.0, 0.481),
     'L1_ffn_gamma': (1.0, 0.2),
     'L1_ffn_beta': (0.0, 0.367)}
    factors = {'L0_gnn_a_dst1': 3.556,
     'L0_gnn_a_dst2': 4.884,
     'L0_mix_Wq': 22.015,
     'L0_mix_Wk': 8.0,
     'L0_ffn_bg': 3.411,
     'L0_ffn_b1': 8.0,
     'L0_ffn_b2': 7.746,
     'L1_gnn_b_u': 64.0,
     'L1_gnn_W_v': 4.101,
     'L1_mix_Wq': 8.0,
     'L1_mix_Wk': 6.522,
     'L1_ffn_w1': 3.992,
     'L1_ffn_w2': 3.191}
    for name, (base, spread) in spreads.items():
        noise = np.random.default_rng([zlib.crc32(name.encode()), seed]).standard_normal(out[name].shape)
        drawn = base * np.exp(spread * noise) if base else spread * noise
        out[name] = jnp.asarray(drawn.astype(out[name].dtype))
    for name, factor in factors.items():
        out[name] = (out[name] * factor).astype(out[name].dtype)
    return out
```

```python
from contextlib import ExitStack

import concourse.bass as bass
from concourse import mybir

F32 = mybir.dt.float32
BF16 = mybir.dt.bfloat16
F16 = mybir.dt.float16
I32 = mybir.dt.int32
U32 = mybir.dt.uint32
ALU = mybir.AluOpType
ACT = mybir.ActivationFunctionType
AX = mybir.AxisListType

P = 128
N = 625
NT = 5
NP = NT * P
LAST = N - (NT - 1) * P
D = 256
KD = D // P
EDGES = 20000
EP = 125
ET = EDGES // EP
EG = 4
EGN = ET // EG
GAT = 3
DEPTH = 4
HEADS = 8
DH = D // HEADS
FF = 1024
E0, H0 = 8, 1024
E1, H1 = 16, 512
EPS = 1e-5
QK_SCALE = float(DH) ** -0.25
NOEDGE = -1.0e30
ATT_EPS = 1e-6

COLS = {}
_at = 0
for _l in range(GAT):
    COLS["gat_b", _l] = _at; _at += KD
for _l in range(GAT - 1):
    COLS["gamma", _l] = _at; _at += KD
    COLS["beta", _l] = _at; _at += KD
for _l in range(DEPTH):
    for _n in ("ln1_g", "ln1_b", "ln2_g", "ln2_b"):
        COLS[_n, _l] = _at; _at += KD
    COLS["ff_b1", _l] = _at; _at += FF // P
COLS["m_g1", 0] = _at; _at += KD
COLS["m_b1", 0] = _at; _at += KD
NCOL = _at
ROWS = {}
_at = 0
for _l in range(DEPTH):
    ROWS["bo", _l] = _at; _at += D
    ROWS["ff_b2", _l] = _at; _at += D
for _n, _k in (("gat_b2", D), ("bg", E0), ("b_u", HEADS), ("m_g2", D), ("m_b2", D), ("gate_b", E1),
               ("gamma_out", D), ("beta_out", D)):
    ROWS[_n, 0] = _at; _at += _k
NROW = _at


def build(nc, t):
    ctx = ExitStack()
    with ctx:
        def sb(name, shape, dt=F32):
            return ctx.enter_context(nc.sbuf_tensor(name, shape, dt))

        def sem(name):
            return ctx.enter_context(nc.semaphore(name))

        ident = sb("ident", [P, P])
        ones = sb("ones", [P, P])
        iota = sb("iota", [P, NP], F16)
        iota_f = sb("iota_f", [P, E1])
        headmask = sb("headmask", [P, P])
        minus_half = sb("minus_half", [P, 16])
        cols = sb("cols", [P, NCOL])
        rows = sb("rows", [P, NROW])
        x_res = sb("x_res", [P, NT, D])
        x_mix = sb("x_mix", [P, NT, D])
        x_bias = sb("x_bias", [P, NT, D])
        normed = sb("normed", [P, NT, D])
        normed_T = sb("normed_T", [P, KD, NP])
        stats = sb("stats", [P, NT, 6])
        mv = sb("mv", [P, NT, 2])
        var_eps = sb("var_eps", [P, NT])
        rstd = sb("rstd", [P, NT])
        edge_i = sb("edge_i", [EP, 2, ET], I32)
        edge_f = sb("edge_f", [EP, 2, ET])
        present = sb("present", [1, NT * EGN])
        span_f = sb("span_f", [1, 2, NT])
        span_g = sb("span_g", [1, 1, NT])
        marked = sb("marked", [1, NT * EGN])
        group_f = sb("group_f", [1, EGN])
        group_r = sb("group_r", [1, EGN])
        zero_b = sb("zero_b", [EP, 512], BF16)
        span_i = sb("span_i", [1, 2, NT], I32)
        count_src = sb("count_src", [P, NT, NP])
        no_edge = sb("no_edge", [P, NT, NP])
        gat_w = sb("gat_w", [P, GAT, KD, D + 2])
        gat_in = sb("gat_in", [P, KD, NP])
        gat_h = sb("gat_h", [P, NT, D + 1])
        score = sb("score", [P, NT, 2])
        gat_out = sb("gat_out", [P, NT, D])
        score_max = sb("score_max", [P, NT])
        shift = sb("shift", [P, 2, NT])
        score2 = sb("score2", [P, NT])
        tiny = sb("tiny", [P, 8 * NT])
        tiny2 = sb("tiny2", [P, 8 * NT])
        row1 = sb("row1", [P, NP])
        row2 = sb("row2", [P, NP])
        prob = sb("prob", [P, NT, NP])
        prob2 = sb("prob2", [P, 2, NP])
        junk = sb("junk", [P, NP])
        bn_st = sb("bn_st", [P, KD, 2, 6])
        bn_mv = sb("bn_mv", [P, KD, 2])
        bn_rstd = sb("bn_rstd", [P, KD])
        bn_eps = sb("bn_eps", [P, KD])
        bn_scale = sb("bn_scale", [P, KD])
        bn_shift = sb("bn_shift", [P, KD])
        WQKVO = KD * D
        mix_w = sb("mix_w", [P, 4 * WQKVO])
        ff_w1 = sb("ff_w1", [P, 2, KD * FF])
        ff_w2 = sb("ff_w2", [P, 2, KD * FF])
        q_max = sb("q_max", [P, NT * HEADS])
        v_tok = sb("v_tok", [P, NT, KD, P + 1])
        k_exp = sb("k_exp", [P, KD, NP])
        q_T = sb("q_T", [P, KD, NP])
        k_max = sb("k_max", [P, KD])
        k_top = sb("k_top", [P, KD])
        k_inv = sb("k_inv", [P, KD])
        q_inv = sb("q_inv", [P, NT * HEADS])
        k_sum = sb("k_sum", [P, KD])
        context = sb("context", [P, KD, P + 4])
        att_T = sb("att_T", [P, KD, NP])
        hidden = sb("hidden", [P, FF // P, NP])
        gate_w = sb("gate_w", [P, KD, E0 + E1])
        gates = sb("gates", [P, NT, E1])
        top = sb("top", [P, NT, 8])
        top_i = sb("top_i", [P, NT, 8], U32)
        top_f = sb("top_f", [P, NT, 8])
        pair = sb("pair", [P, NT, 4])
        comb = sb("comb", [P, NT, E1])
        comb2 = sb("comb2", [P, NT, E1])
        moe_b2 = sb("moe_b2", [E1, 2, D])
        moe_b1 = sb("moe_b1", [P, 2, 64])
        uv_w = sb("uv_w", [P, KD, 2 * HEADS])
        su = sb("su", [P, NT, HEADS])
        su2 = sb("su2", [P, NT, HEADS])
        sv = sb("sv", [P, NT, HEADS])
        hmax = sb("hmax", [P, NT, HEADS])
        hm_ = sb("hm_", [P, NT, HEADS])
        hs1 = sb("hs1", [P, NT, HEADS])
        hs2 = sb("hs2", [P, NT, HEADS])
        hout = sb("hout", [P, NT, DH])
        flat = lambda ap: ap.rearrange("p a b -> p (a b)")
        count_dst = hidden[:, 0:NT, :]
        a_rows = flat(hidden[:, NT:, :])[:, 0:GAT * 2 * D]
        hot_src = flat(q_T[0:EP]).bitcast(BF16).rearrange("p (u s n) -> p u s n", u=2, s=EG // 2)
        in_block = flat(att_T[0:EP])[:, 0:NT * ET].rearrange("p (b t) -> p b t", b=NT)
        hot_dst = flat(att_T[0:EP])[:, NT * ET:NT * ET + EG * P // 2].bitcast(BF16).rearrange("p (u s n) -> p u s n", u=2, s=EG // 2)
        gat_pre = prob[:, 0:KD, :]
        xn_tok = gat_out
        q_tok = normed
        k_tok = flat(att_T[:]).rearrange("p (t d) -> p t d", t=NT)
        comb_T = junk
        head_T = k_exp[0:DH + 1, 0, :]
        xh = mix_w[:, 0:NT * HEADS * (DH + 1)].rearrange("p (t h c) -> p t h c", t=NT, h=HEADS)
        mps = ctx.enter_context(nc.psum_tensor("mps", [P, 6 * 512], F32))
        gps = ctx.enter_context(nc.psum_tensor("gps", [P, 2 * 512], F32))

        def bank(b, n=NP):
            return mps[:, b * 512:b * 512 + n]

        def down_slot(n):
            return (mps[:, (4 + n % 4) * 512:] if n % 4 < 2 else gps[:, (n % 4 - 2) * 512:])[:, 0:D]

        def col(name, l, k):
            c = COLS[name, l] + k
            return cols[:, c:c + 1]

        def row(name, l, n=D):
            return rows[:, ROWS[name, l]:ROWS[name, l] + n]

        def tiles(ap):
            return ap.rearrange("p (t c) -> p t c", t=NT)

        def halves(ap):
            return ap.rearrange("p (t k c) -> p t k c", t=NT, k=KD)

        def expert_up(e, h, u):
            return ff_w1[:, u, 0:KD * h].rearrange("p (k h) -> p k h", k=KD)

        def expert_down(e, h, u):
            return ff_w2[:, u, 0:h // P * D].rearrange("p (j d) -> p j d", j=h // P)

        names = ("x_loaded xpad_zero consts_ready cols_loaded rows_loaded edges_loaded gatw_loaded mixw_loaded "
                 "arows_loaded ffw_loaded0 ffw_loaded1 small_loaded var_ready rstd_ready norm_ready normT_filled "
                 "normT_dve normT_act edge_float in_block_ready block_counts present_ready span_ready hot_ready "
                 "hot_free count_filled count_kept countT_filled countT_kept gatw_ready "
                 "h_filled h_kept srow_filled max_done shift_ready r_filled r_kept exp_ready exp_used "
                 "prob_ready agg_filled agg_kept gatT_filled gatT_kept bnvar_ready bnrstd_ready bn_ready gatin_ready "
                 "qv_filled q_shifted q_exped q_normed v_kept k_filled kmax_ready k_exped qT_filled qT_dve qT_act "
                 "kT_filled kT_dve kT_act ctx_filled ctx_kept att_filled att_dve att_act proj_filled xbias_ready "
                 "x_updated up_filled up_kept down_filled down_used ff_used gate_filled gdiff_ready gexp_ready "
                 "comb_ready combT_filled combT_kept moe_bias_filled moe_ready dve_step act_step pool_step "
                 "uv_filled uv_ready hrow_filled hmax_done hshift_ready hr_filled hexp_ready hexp_used hprob_ready "
                 "hagg_filled hagg_kept hT_filled hT_kept heads_ready qk_min qk_exp qk_ready qk_filled num_filled "
                 "num_kept hr_kept moe_bias_kept moe_down_filled stored").split()
        S = {n: sem("s_" + n) for n in names}

        block = ctx.enter_context(nc.Block())

        @block.sync
        def _(sp):
            sp.wait_ge(S["xpad_zero"], 1)
            sp.dma_start(x_res[:, 0:NT - 1, :], t["x"][0:(NT - 1) * P].rearrange("(t p) d -> p t d", p=P)).then_inc(S["x_loaded"], 16)
            sp.dma_start(x_res[0:LAST, NT - 1, :], t["x"][(NT - 1) * P:N]).then_inc(S["x_loaded"], 16)
            sp.dma_start(edge_i[:, 0, :], t["src"]).then_inc(S["edges_loaded"], 16)
            sp.dma_start(edge_i[:, 1, :], t["dst"]).then_inc(S["edges_loaded"], 16)
            sp.dma_start(cols[:], t["cols"]).then_inc(S["cols_loaded"], 16)

            def load_mix(i):
                if i >= 1:
                    sp.wait_ge(S["proj_filled"], i)
                sp.dma_start(mix_w[:], t["mix1_qkvm"] if i == DEPTH else t["mix_w"][i]).then_inc(S["mixw_loaded"], 16)

            def load_ff(n, up, down):
                if 2 <= n < 2 + DEPTH:
                    sp.wait_ge(S["down_filled"], n - 1)
                elif n == DEPTH + E0 + 2:
                    sp.wait_ge(S["down_filled"], DEPTH + 1)
                elif n >= 2:
                    sp.wait_ge(S["moe_down_filled"], NT * (n - 1 - DEPTH - (n > DEPTH + E0 + 2)))
                sp.dma_start(ff_w1[:, n % 2, 0:up.shape[1]], up).then_inc(S["ffw_loaded%d" % (n % 2)], 16)
                sp.dma_start(ff_w2[:, n % 2, 0:down.shape[1]], down).then_inc(S["ffw_loaded%d" % (n % 2)], 16)

            load_mix(0)
            sp.dma_start(rows[:], t["rows"].broadcast_to([P, NROW])).then_inc(S["rows_loaded"], 16)
            sp.dma_start(gat_w[:, :, :, 0:D], t["gat_w"]).then_inc(S["gatw_loaded"], 16)
            load_ff(0, t["ff_w1"][0], t["ff_w2"][0])
            sp.dma_start(a_rows, t["a_rows"].broadcast_to([P, GAT * 2 * D])).then_inc(S["arows_loaded"], 16)
            load_ff(1, t["ff_w1"][1], t["ff_w2"][1])
            sp.dma_start(gate_w[:], t["gate_w"]).then_inc(S["small_loaded"], 16)
            sp.dma_start(uv_w[:], t["uv_w"]).then_inc(S["small_loaded"], 16)
            sp.dma_start(moe_b2[0:E0, 0, :], t["moe0_b2"]).then_inc(S["small_loaded"], 16)
            sp.dma_start(moe_b2[0:E1, 1, :], t["moe1_b2"]).then_inc(S["small_loaded"], 16)
            sp.dma_start(moe_b1[:], t["moe_b1"]).then_inc(S["small_loaded"], 16)
            load_mix(1)
            for i in range(2, DEPTH):
                load_mix(i)
                load_ff(i, t["ff_w1"][i], t["ff_w2"][i])
            load_mix(DEPTH)
            for e in range(2):
                load_ff(DEPTH + e, t["moe0_w1"][e], t["moe0_w2"][e])
            for e in range(2, E0):
                load_ff(DEPTH + e, t["moe0_w1"][e], t["moe0_w2"][e])
            load_ff(DEPTH + E0, t["mix1_w1"], t["mix1_w2"])
            for e in range(E1):
                load_ff(DEPTH + E0 + 1 + e, t["moe1_w1"][e], t["moe1_w2"][e])
            sp.wait_ge(S["moe_ready"], 2)
            sp.dma_start(t["out"][0:(NT - 1) * P].rearrange("(t p) d -> p t d", p=P), normed[:, 0:NT - 1, :]).then_inc(S["stored"], 16)
            sp.dma_start(t["out"][(NT - 1) * P:N], normed[0:LAST, NT - 1, :]).then_inc(S["stored"], 16)
            sp.wait_ge(S["stored"], 32)

        @block.gpsimd
        def _(pool):
            steps = [0]

            def link(ins):
                steps[0] += 1
                ins.then_inc(S["pool_step"], 1)
                pool.wait_ge(S["pool_step"], steps[0])

            def rsqrt(dst, var, eps, n, ready, count):
                pool.wait_ge(S[ready], count)
                link(pool.tensor_scalar(eps, var, EPS, None, ALU.add))
                return pool.tensor_tensor(dst, eps, minus_half[:, 0:n], ALU.pow)

            def norm(n):
                rsqrt(rstd[:], mv[:, :, 1], var_eps[:], NT, "var_ready", n).then_inc(S["rstd_ready"], 1)

            link(pool.memset(x_res[:, NT - 1, :], 0.0))
            pool.sem_inc(S["xpad_zero"], 1)
            pool.memset(ones[:], 1.0)
            pool.memset(minus_half[:], -0.5)
            link(pool.memset(ident[:], 0.0))
            pool.affine_select(out=ident[:], in_=ident[:], compare_op=ALU.not_equal, fill=1.0, base=0,
                               pattern=[[-1, P]], channel_multiplier=1)
            pool.iota(iota[:], pattern=[[1, NP]], base=0, channel_multiplier=0, allow_small_or_imprecise_dtypes=True)
            pool.iota(iota_f[:], pattern=[[1, E1]], base=0, channel_multiplier=0, allow_small_or_imprecise_dtypes=True)
            pool.iota(group_f[0:1, :], pattern=[[1, EGN]], base=1, channel_multiplier=0, allow_small_or_imprecise_dtypes=True)
            link(pool.memset(headmask[:], 1.0))
            hm = headmask[:].rearrange("p (h e) -> p h e", e=DH)
            link(pool.affine_select(out=hm, in_=hm, compare_op=ALU.is_ge, fill=0.0, base=0,
                                    pattern=[[-DH, P // DH], [0, DH]], channel_multiplier=1))
            link(pool.affine_select(out=hm, in_=hm, compare_op=ALU.is_ge, fill=0.0, base=DH - 1,
                                    pattern=[[DH, P // DH], [0, DH]], channel_multiplier=-1))
            pool.memset(gat_h[:, :, D:D + 1], 1.0)
            pool.memset(k_exp[:, :, N:NP], 0.0)
            pool.memset(zero_b[:], 0.0)
            link(pool.memset(v_tok[:, :, :, P:P + 1], 1.0))
            key_sum = v_tok[:, NT - 1, :, P]
            pool.affine_select(out=key_sum, in_=key_sum, compare_op=ALU.is_ge,
                               fill=0.0, base=LAST - 1, pattern=[[0, KD]], channel_multiplier=-1).then_inc(S["consts_ready"], 1)
            norm(1)
            nth = 1
            for i in range(DEPTH):
                nth += 1
                norm(nth)
                if i == 0:
                    pool.wait_ge(S["rows_loaded"], 16)
                if i > 0:
                    pool.wait_ge(S["x_updated"], 2 * i)
                pool.tensor_tensor(x_bias[:], x_mix[:], row("bo", i)[:, None, :].broadcast_to([P, NT, D]),
                                   ALU.add).then_inc(S["xbias_ready"], 1)
                pool.wait_ge(S["x_updated"], 2 * i + 1)
                pool.tensor_tensor(x_bias[:], x_mix[:], row("ff_b2", i)[:, None, :].broadcast_to([P, NT, D]),
                                   ALU.add).then_inc(S["xbias_ready"], 1)
                nth += 1
                norm(nth)
                if i < GAT - 1:
                    rsqrt(bn_rstd[:], bn_mv[:, :, 1], bn_eps[:], KD, "bnvar_ready", i + 1).then_inc(S["bnrstd_ready"], 1)
            for _ in range(5):
                nth += 1
                norm(nth)
            nth += 1
            norm(nth)

        @block.scalar
        def _(act):
            steps = [0]

            def link(ins):
                steps[0] += 1
                ins.then_inc(S["act_step"], 1)
                act.wait_ge(S["act_step"], steps[0])

            def normT_half(n, dst, g=None, b=None):
                act.wait_ge(S["normT_filled"], 2 * n)
                if g is None:
                    ins = act.activation(dst, bank(2), ACT.Copy)
                else:
                    ins = act.activation(dst, bank(2), ACT.Identity, bias=b, scale=g)
                ins.then_inc(S["normT_act"], 1)

            def up_tile(u, dst, func, bias):
                act.wait_ge(S["up_filled"], u + 1)
                act.activation(dst, bank(2 * (u % 2)), func, bias=bias).then_inc(S["up_kept"], 1)

            act.wait_ge(S["consts_ready"], 1)
            act.wait_ge(S["cols_loaded"], 16)
            for l in range(NT):
                act.wait_ge(S["countT_filled"], l + 1)
                act.activation(count_src[:, l, :], bank(2 * (l % 2)), ACT.Copy).then_inc(S["countT_kept"], 1)
            normT_half(1, gat_in[:, 1, :])

            def gat_rows(l):
                for i in range(NT):
                    act.wait_ge(S["h_filled"], NT * l + i + 1)
                    if i == 0 and l > 0:
                        act.wait_ge(S["agg_filled"], NT * l)
                    ps = gps[:, (i % 2) * 512:(i % 2) * 512 + D + 2]
                    act.activation(gat_h[:, i, 0:D], ps[:, 0:D], ACT.Copy)
                    act.activation(score[:, i, :], ps[:, D:D + 2], ACT.Copy).then_inc(S["h_kept"], 1)
                for n, dst in enumerate((row1, row2)):
                    act.wait_ge(S["r_filled"], 2 * l + n + 1)
                    act.activation(dst[:], gps[:, 0:NP], ACT.Copy).then_inc(S["r_kept"], 1)

            def exponentials(n, s1, s2):
                act.wait_ge(S["r_kept" if n < GAT else "hr_kept"], 2 * (n if n < GAT else n - GAT) + 2)
                for i in range(NT):
                    c = NT * n + i
                    act.activation(prob[:, i, :], row1[:], ACT.Exp, bias=s1[:, i:i + 1])
                    if c >= 2:
                        act.wait_ge(S["prob_ready"], c - 1)
                    act.activation(prob2[:, c % 2, :], row2[:], ACT.Exp, bias=s2[:, i:i + 1]).then_inc(S["exp_ready"], 1)

            def gat_turn(l):
                for k in range(KD):
                    act.wait_ge(S["gatT_filled"], KD * l + k + 1)
                    act.activation(gat_pre[:, k, :], gps[:, 0:NP], ACT.Identity, bias=col("gat_b", l, k)).then_inc(S["gatT_kept"], 1)
                act.wait_ge(S["bn_ready"], l + 1)
                for k in range(KD):
                    act.activation(gat_in[:, k, :], gat_pre[:, k, :], ACT.Relu, bias=bn_shift[:, k:k + 1],
                                   scale=bn_scale[:, k:k + 1]).then_inc(S["gatin_ready"], 1)

            nth = 1
            for i in range(DEPTH):
                nth += 1
                normT_half(nth, normed_T[:, 1, :], col("ln1_g", i, 1), col("ln1_b", i, 1))
                act.wait_ge(S["qv_filled"], 2 * i + 2)
                act.activation(v_tok[:, :, :, 0:P], halves(bank(3, NT * D)), ACT.Copy).then_inc(S["v_kept"], 1)
                act.wait_ge(S["q_shifted"], i + 1)
                act.activation(q_tok[:], q_tok[:], ACT.Exp, scale=QK_SCALE).then_inc(S["q_exped"], 1)
                for k in range(KD):
                    act.wait_ge(S["kmax_ready"], KD * i + k + 1)
                    act.activation(k_exp[:, k, 0:N], bank(2 * k, N), ACT.Exp, bias=k_max[:, k:k + 1], scale=QK_SCALE,
                                   accum_out=k_sum[:, k:k + 1]).then_inc(S["k_exped"], 1)
                if i < GAT:
                    gat_rows(i)
                act.wait_ge(S["qT_filled"], 2 * i + 2)
                act.activation(q_T[:, 1, :], bank(0), ACT.Copy).then_inc(S["qT_act"], 1)
                act.wait_ge(S["kT_filled"], 2 * i + 2)
                act.activation(k_tok[:, :, P:D], tiles(bank(4)), ACT.Copy).then_inc(S["kT_act"], 1)
                act.wait_ge(S["att_filled"], 2 * i + 2)
                act.activation(att_T[:, 1, :], bank(4), ACT.Copy).then_inc(S["att_act"], 1)
                nth += 1
                normT_half(nth, normed_T[:, 1, :], col("ln2_g", i, 1), col("ln2_b", i, 1))
                if i < GAT:
                    exponentials(i, score[:, :, 0], score2)
                for j in range(FF // P):
                    up_tile(FF // P * i + j, hidden[:, j, :], ACT.Gelu, cols[:, COLS["ff_b1", i] + j:COLS["ff_b1", i] + j + 1])
                if i < GAT - 1:
                    gat_turn(i)

            def moe(m, experts, width, u0):
                nonlocal nth
                nth += 1
                normT_half(nth, normed_T[:, 1, :])
                act.wait_ge(S["gdiff_ready"], m + 1)
                act.activation(pair[:, :, 1], pair[:, :, 0], ACT.Exp).then_inc(S["gexp_ready"], 1)
                act.wait_ge(S["combT_filled"], m + 1)
                act.activation(comb_T[0:experts, :], gps[0:experts, 0:NP], ACT.Copy).then_inc(S["combT_kept"], 1)
                act.wait_ge(S["small_loaded"], 16 * 5)
                J = width // P
                for e in range(experts):
                    if e > 0:
                        act.wait_ge(S["moe_down_filled"], NT * (m * E0 + e))
                    for j in range(J):
                        b = e * J + j
                        up_tile(u0 + b, hidden[:, j, :], ACT.Relu, moe_b1[:, m, b:b + 1])

            moe(0, E0, H0, DEPTH * FF // P)
            nth += 1
            normT_half(nth, normed_T[:, 1, :])
            act.wait_ge(S["qk_min"], 1)
            act.activation(q_T[:], q_T[:], ACT.Exp).then_inc(S["qk_exp"], 1)
            act.wait_ge(S["qk_min"], 2)
            act.activation(k_tok[:], k_tok[:], ACT.Exp).then_inc(S["qk_exp"], 1)
            act.wait_ge(S["qv_filled"], 2 * DEPTH + 2)
            act.activation(v_tok[:, :, :, 0:P], halves(bank(3, NT * D)), ACT.Copy, scale=1.0 / N).then_inc(S["v_kept"], 1)
            act.wait_ge(S["qT_filled"], 2 * DEPTH + 2)
            act.activation(att_T[:, 1, :], bank(2), ACT.Copy).then_inc(S["att_act"], 1)
            nth += 1
            normT_half(nth, att_T[:, 1, :], col("m_g1", 0, 1), col("m_b1", 0, 1))
            for j in range(4):
                up_tile(DEPTH * 8 + 64 + j, hidden[:, j, :], ACT.Relu, 0.0)
            for h in range(HEADS):
                for n, dst in enumerate((row1, row2)):
                    act.wait_ge(S["hr_filled"], 2 * h + n + 1)
                    ins = act.activation(dst[:], gps[:, 0:NP], ACT.Copy)
                    ins.then_inc(S["hr_kept"], 1)
                exponentials(GAT + h, su[:, :, h], su2[:, :, h])
                act.wait_ge(S["hagg_filled"], h + 1)
                act.activation(head_T[:], gps[0:DH + 1, 0:NP], ACT.Copy).then_inc(S["hagg_kept"], 1)
            moe(1, E1, H1, DEPTH * 8 + 64 + 4)

        @block.vector
        def _(dve):
            steps = [0]

            def link(ins):
                steps[0] += 1
                ins.then_inc(S["dve_step"], 1)
                dve.wait_ge(S["dve_step"], steps[0])

            norms, turns = [0], [0]

            def normalise(src, dst):
                norms[0] += 1
                for i in range(NT):
                    ins = dve.bn_stats(stats[:, i, :], src[:, i, :])
                link(ins)
                for i in range(NT):
                    ins = dve.bn_aggr(mv[:, i, :], stats[:, i, :])
                ins.then_inc(S["var_ready"], 1)
                dve.wait_ge(S["rstd_ready"], norms[0])
                for i in range(NT):
                    ins = dve.tensor_scalar(dst[:, i, :], src[:, i, :], mv[:, i, 0:1], rstd[:, i:i + 1],
                                            ALU.subtract, ALU.mult)
                return ins

            def normT_half(dst, g=None, b=None):
                turns[0] += 1
                dve.wait_ge(S["normT_filled"], 2 * turns[0] - 1)
                if g is None:
                    ins = dve.tensor_copy(dst, bank(4))
                else:
                    ins = dve.tensor_scalar(dst, bank(4), g, b, ALU.mult, ALU.add)
                ins.then_inc(S["normT_dve"], 1)

            dve.wait_ge(S["consts_ready"], 1)
            dve.wait_ge(S["edges_loaded"], 32)
            link(dve.tensor_copy(edge_f[:], edge_i[:]))
            for b in range(NT):
                link(dve.tensor_scalar(in_block[:, b, :], edge_f[:, 1, :], float(P * b), None, ALU.is_ge))
                ins = dve.scalar_tensor_tensor(out=in_block[:, b, :], in0=edge_f[:, 1, :], scalar=float(P * (b + 1)),
                                               in1=in_block[:, b, :], op0=ALU.is_lt, op1=ALU.mult)
            link(ins)
            dve.sem_inc(S["in_block_ready"], 1)
            dve.wait_ge(S["block_counts"], 1)
            for h in range(2):
                c = NT * ET // 2
                ins = dve.tensor_reduce(present[0:1, h * c // EG:(h + 1) * c // EG],
                                        gps[0:1, 512 * h:512 * h + c].rearrange("p (g s) -> p g s", s=EG), AX.X, ALU.add)
            link(ins)
            pr = present[:].rearrange("p (b g) -> p b g", b=NT)
            gr = group_f[0:1, None, :].broadcast_to([1, NT, EGN])
            link(dve.tensor_scalar(present[:], present[:], 0.0, None, ALU.is_gt))
            link(dve.tensor_tensor(marked[:].rearrange("p (b g) -> p b g", b=NT), pr, gr, ALU.mult))
            link(dve.tensor_reduce(span_f[:, 1, :], marked[:].rearrange("p (b g) -> p b g", b=NT), AX.X, ALU.max))
            link(dve.tensor_scalar(group_r[:], group_f[:], -1.0, float(EGN + 1), ALU.mult, ALU.add))
            link(dve.tensor_tensor(marked[:].rearrange("p (b g) -> p b g", b=NT), pr,
                                   group_r[0:1, None, :].broadcast_to([1, NT, EGN]), ALU.mult))
            link(dve.tensor_reduce(span_f[:, 0, :], marked[:].rearrange("p (b g) -> p b g", b=NT), AX.X, ALU.max))
            link(dve.tensor_scalar(span_f[:, 0, :], span_f[:, 0, :], -1.0, float(EGN), ALU.mult, ALU.add))
            link(dve.tensor_scalar(span_f[:, 0, :], span_f[:, 0, :], float(EGN - 1), None, ALU.min))
            link(dve.tensor_scalar(span_g[:, 0, :], span_f[:, 0, :], 1.0, None, ALU.add))
            link(dve.tensor_tensor(span_f[:, 1, :], span_f[:, 1, :], span_g[:, 0, :], ALU.max))
            link(dve.tensor_copy(span_i[:], span_f[:]))
            dve.sem_inc(S["span_ready"], 1)

            turn_no = dve.alloc_register("dve_hot_turn")
            dve.reg_mov(turn_no, 0)
            for b in range(NT):
                first = dve.value_load(span_i[0:1, 0, b:b + 1], min_val=0, max_val=EGN - 1)
                last = dve.value_load(span_i[0:1, 1, b:b + 1], min_val=1, max_val=EGN)
                with dve.Fori(first, last) as g:
                    for u in range(2):
                        dve.reg_add(turn_no, turn_no, 1)
                        dve.wait_ge(S["hot_free"], dve.snap(turn_no))
                        for s in range(EG // 2):
                            c = bass.ds(g * EG + u * (EG // 2) + s, 1)
                            dve.tensor_scalar(hot_src[:, u, s, :], iota[0:EP, :], edge_f[:, 0, c], None, ALU.is_equal)
                            ins = dve.tensor_scalar(hot_dst[:, u, s, :], iota[0:EP, P * b:P * (b + 1)], edge_f[:, 1, c],
                                                    None, ALU.is_equal)
                        ins.then_inc(S["hot_ready"], 1)
                dve.wait_ge(S["count_filled"], b + 1)
                dve.tensor_copy(count_dst[:, b, :], bank(2 * (b % 2)))
                dve.tensor_scalar(no_edge[:, b, :], bank(2 * (b % 2)), 0.0, NOEDGE, ALU.is_equal, ALU.mult).then_inc(S["count_kept"], 1)

            dve.wait_ge(S["rows_loaded"], 16)
            dve.wait_ge(S["arows_loaded"], 16)
            dve.wait_ge(S["gatw_loaded"], 16)
            for l in range(GAT):
                for n in range(2):
                    for k in range(KD):
                        s0 = ((l * 2 + n) * KD + k) * D
                        ins = dve.tensor_tensor_reduce(flat(prob[:])[:, s0:s0 + D], gat_w[:, l, k, 0:D], a_rows[:, (2 * l + n) * D:(2 * l + n + 1) * D], 1.0, 0.0, ALU.mult,
                                                       ALU.add, gat_w[:, l, k, D + n:D + n + 1])
            ins.then_inc(S["gatw_ready"], 1)

            dve.wait_ge(S["x_loaded"], 32)
            link(normalise(x_res, x_mix))
            dve.sem_inc(S["norm_ready"], 1)
            normT_half(gat_in[:, 0, :])

            def gat_shift(l):
                dve.wait_ge(S["srow_filled"], l + 1)
                for i in range(NT):
                    ins = dve.tensor_tensor_reduce(prob[:, i, :], gps[:, 0:NP], no_edge[:, i, :], 1.0, NOEDGE * 2, ALU.add,
                                                   ALU.max, score_max[:, i:i + 1])
                ins.then_inc(S["max_done"], 1)
                dve.wait_ge(S["max_done"], l + 1)
                link(dve.scalar_tensor_tensor(out=score_max[:], in0=score_max[:], scalar=NOEDGE / 2, in1=score_max[:],
                                              op0=ALU.is_gt, op1=ALU.mult))
                link(dve.tensor_tensor(tiny[:, 0:NT], score_max[:], score[:, :, 1], ALU.add))
                link(dve.scalar_tensor_tensor(out=tiny2[:, 0:NT], in0=tiny[:, 0:NT], scalar=0.2, in1=tiny[:, 0:NT],
                                              op0=ALU.mult, op1=ALU.max))
                dve.tensor_tensor(shift[:, 0, :], score[:, :, 1], tiny2[:, 0:NT], ALU.subtract)
                dve.tensor_scalar(score2[:], score[:, :, 0], 0.2, None, ALU.mult)
                dve.scalar_tensor_tensor(out=shift[:, 1, :], in0=score[:, :, 1], scalar=0.2, in1=tiny2[:, 0:NT],
                                         op0=ALU.mult, op1=ALU.subtract).then_inc(S["shift_ready"], 1)

            def probabilities(n):
                for i in range(NT):
                    dve.wait_ge(S["exp_ready"], NT * n + i + 1)
                    link(dve.tensor_tensor(prob[:, i, :], prob[:, i, :], prob2[:, (NT * n + i) % 2, :], ALU.max))
                    dve.scalar_tensor_tensor(out=prob[:, i, :], in0=prob[:, i, :], scalar=1.0, in1=count_src[:, i, :],
                                             op0=ALU.min, op1=ALU.mult).then_inc(S["prob_ready"], 1)

            def gat_aggregate(l):
                probabilities(l)
                for i in range(NT):
                    dve.wait_ge(S["agg_filled"], NT * l + i + 1)
                    ps = gps[:, (i % 2) * 512:(i % 2) * 512 + D + 1]
                    link(dve.tensor_scalar(tiny[:, 0:1], ps[:, D:D + 1], 1e-16, None, ALU.add))
                    link(dve.reciprocal(tiny[:, 1:2], tiny[:, 0:1]))
                    dve.tensor_scalar(gat_out[:, i, :], ps[:, 0:D], tiny[:, 1:2], None, ALU.mult).then_inc(S["agg_kept"], 1)

            def gat_batchnorm(l):
                for k in range(KD):
                    dve.wait_ge(S["gatT_kept"], KD * l + k + 1)
                    dve.bn_stats(bn_st[:, k, 0, :], gat_pre[:, k, 0:512])
                    ins = dve.bn_stats(bn_st[:, k, 1, :], gat_pre[:, k, 512:N])
                link(ins)
                for k in range(KD):
                    ins = dve.bn_aggr(bn_mv[:, k, :], bn_st[:, k, :, :])
                ins.then_inc(S["bnvar_ready"], 1)
                dve.wait_ge(S["bnrstd_ready"], l + 1)
                c = COLS["gamma", l]
                link(dve.tensor_tensor(bn_scale[:], bn_rstd[:], cols[:, c:c + KD], ALU.mult))
                link(dve.tensor_tensor(bn_shift[:], bn_mv[:, :, 0], bn_scale[:], ALU.mult))
                c = COLS["beta", l]
                dve.tensor_tensor(bn_shift[:], cols[:, c:c + KD], bn_shift[:], ALU.subtract).then_inc(S["bn_ready"], 1)

            def residual(n, ps):
                dve.wait_ge(S["xbias_ready"], n)
                link(dve.tensor_tensor(x_mix[:], ps, x_bias[:], ALU.add))
                dve.sem_inc(S["x_updated"], 1)

            for i in range(DEPTH):
                link(normalise(x_mix, normed))
                dve.sem_inc(S["norm_ready"], 1)
                normT_half(normed_T[:, 0, :], col("ln1_g", i, 0), col("ln1_b", i, 0))
                dve.wait_ge(S["qv_filled"], 2 * i + 1)
                heads = mps[:, 0:NT * D].rearrange("p (g c) -> p g c", c=DH)
                link(dve.tensor_reduce(q_max[:], heads, AX.X, ALU.max))
                qh = q_tok[:].rearrange("p t (g c) -> p (t g) c", c=DH)
                dve.tensor_tensor(qh, heads, q_max[:, :, None].broadcast_to([P, NT * HEADS, DH]),
                                  ALU.subtract).then_inc(S["q_shifted"], 1)
                for k in range(KD):
                    dve.wait_ge(S["k_filled"], KD * i + k + 1)
                    link(dve.tensor_reduce(k_top[:, k:k + 1], bank(2 * k, N), AX.X, ALU.max))
                    dve.tensor_scalar(k_max[:, k:k + 1], k_top[:, k:k + 1], -QK_SCALE, None, ALU.mult).then_inc(S["kmax_ready"], 1)
                dve.wait_ge(S["q_exped"], i + 1)
                link(dve.tensor_reduce(q_max[:], qh, AX.X, ALU.add))
                link(dve.reciprocal(q_inv[:], q_max[:]))
                dve.tensor_tensor(qh, qh, q_inv[:, :, None].broadcast_to([P, NT * HEADS, DH]), ALU.mult).then_inc(S["q_normed"], 1)
                if i < GAT:
                    gat_shift(i)
                dve.wait_ge(S["qT_filled"], 2 * i + 1)
                dve.tensor_copy(q_T[:, 0, :], bank(4)).then_inc(S["qT_dve"], 1)
                dve.wait_ge(S["kT_filled"], 2 * i + 1)
                dve.tensor_copy(k_tok[:, :, 0:P], tiles(bank(2))).then_inc(S["kT_dve"], 1)
                dve.wait_ge(S["k_exped"], KD * i + 2)
                link(dve.reciprocal(k_inv[:], k_sum[:]))
                dve.wait_ge(S["ctx_filled"], i + 1)
                for k in range(KD):
                    ins = dve.scalar_tensor_tensor(out=context[:, k, 0:P], in0=mps[:, k * 256:k * 256 + P], scalar=k_inv[:, k:k + 1],
                                                   in1=headmask[:], op0=ALU.mult, op1=ALU.mult)
                ins.then_inc(S["ctx_kept"], 1)
                dve.wait_ge(S["att_filled"], 2 * i + 1)
                dve.tensor_copy(att_T[:, 0, :], bank(2)).then_inc(S["att_dve"], 1)
                dve.wait_ge(S["proj_filled"], i + 1)
                residual(2 * i + 1, tiles(mps[:, 0:NT * D]))
                link(normalise(x_mix, normed))
                dve.sem_inc(S["norm_ready"], 1)
                normT_half(normed_T[:, 0, :], col("ln2_g", i, 0), col("ln2_b", i, 0))
                if i < GAT:
                    gat_aggregate(i)
                if i < GAT - 1:
                    gat_batchnorm(i)
                dve.wait_ge(S["down_filled"], i + 1)
                residual(2 * i + 2, tiles(mps[:, 0:NT * D]))
            link(dve.tensor_tensor(x_res[:], x_res[:], gat_out[:], ALU.add))
            link(dve.tensor_tensor(x_res[:], x_res[:], row("gat_b2", 0)[:, None, :].broadcast_to([P, NT, D]), ALU.add))
            link(dve.tensor_tensor(x_res[:], x_res[:], x_mix[:], ALU.add))

            down = [0]

            def moe(m, experts, bias, post):
                link(normalise(x_res, normed))
                dve.sem_inc(S["norm_ready"], 1)
                normT_half(normed_T[:, 0, :])
                dve.wait_ge(S["gate_filled"], m + 1)
                g = gates[:, :, 0:experts]
                link(dve.tensor_tensor(g, gps[:, 0:NT * experts].rearrange("p (t e) -> p t e", t=NT),
                                       row(bias, 0, experts)[:, None, :].broadcast_to([P, NT, experts]), ALU.add))
                for i in range(NT):
                    ins = dve.max(top[:, i, :], gates[:, i, 0:experts])
                link(ins)
                for i in range(NT):
                    ins = dve.max_index(top_i[:, i, :], top[:, i, :], gates[:, i, 0:experts])
                link(ins)
                dve.tensor_copy(top_f[:], top_i[:])
                dve.tensor_tensor(pair[:, :, 0], top[:, :, 1], top[:, :, 0], ALU.subtract).then_inc(S["gdiff_ready"], 1)
                dve.wait_ge(S["gexp_ready"], m + 1)
                link(dve.tensor_scalar(pair[:, :, 0], pair[:, :, 1], 1.0, None, ALU.add))
                link(dve.reciprocal(pair[:, :, 2], pair[:, :, 0]))
                link(dve.tensor_tensor(pair[:, :, 3], pair[:, :, 1], pair[:, :, 2], ALU.mult))
                for i in range(NT):
                    dve.tensor_scalar(comb[:, i, 0:experts], iota_f[:, 0:experts], top_f[:, i, 0:1], pair[:, i, 2:3],
                                      ALU.is_equal, ALU.mult)
                    ins = dve.tensor_scalar(comb2[:, i, 0:experts], iota_f[:, 0:experts], top_f[:, i, 1:2], pair[:, i, 3:4],
                                            ALU.is_equal, ALU.mult)
                link(ins)
                link(dve.tensor_tensor(comb[:, :, 0:experts], comb[:, :, 0:experts], comb2[:, :, 0:experts], ALU.add))
                dve.sem_inc(S["comb_ready"], 1)
                dve.wait_ge(S["moe_bias_filled"], m + 1)
                base = x_res if m == 0 else normed
                link(dve.tensor_tensor(x_mix[:], tiles(mps[:, 0:NT * D]), base[:], ALU.add))
                dve.sem_inc(S["moe_bias_kept"], 1)
                for e in range(experts):
                    for i in range(NT):
                        n = down[0]
                        dve.wait_ge(S["moe_down_filled"], n + 1)
                        ins = dve.scalar_tensor_tensor(out=x_mix[:, i, :], in0=down_slot(n),
                                                       scalar=comb[:, i, e:e + 1], in1=x_mix[:, i, :], op0=ALU.mult, op1=ALU.add)
                        down[0] += 1
                        ins.then_inc(S["down_used"], 1)
                    dve.wait_ge(S["down_used"], down[0])

            moe(0, E0, "bg", None)

            link(normalise(x_mix, xn_tok))
            dve.sem_inc(S["norm_ready"], 1)
            normT_half(normed_T[:, 0, :])
            for k in range(KD):
                dve.wait_ge(S["qk_filled"], k + 1)
                dve.tensor_scalar(q_T[:, k, :], bank(2 * k), 0.0, None, ALU.min)
                ins = dve.tensor_scalar(att_T[:, k, :], bank(2 * k), 0.0, None, ALU.max)
            link(ins)
            dve.sem_inc(S["qk_min"], 1)
            dve.wait_ge(S["qk_exp"], 1)
            dve.tensor_tensor(q_T[:], q_T[:], att_T[:], ALU.add).then_inc(S["qk_ready"], 1)
            dve.wait_ge(S["qk_ready"], 1)
            dve.wait_ge(S["qv_filled"], 2 * DEPTH + 1)
            dve.tensor_scalar(k_tok[:], tiles(mps[:, 0:NT * D]), 0.0, None, ALU.min)
            link(dve.tensor_scalar(q_tok[:], tiles(mps[:, 0:NT * D]), 0.0, None, ALU.max))
            dve.sem_inc(S["qk_min"], 1)
            dve.wait_ge(S["qk_exp"], 2)
            link(dve.tensor_tensor(k_tok[:], k_tok[:], q_tok[:], ALU.add))
            dve.tensor_scalar(k_tok[:, NT - 1, :], k_tok[:, NT - 1, :], v_tok[:, NT - 1, 0, P:P + 1], None,
                              ALU.mult).then_inc(S["qk_ready"], 1)
            dve.wait_ge(S["ctx_filled"], DEPTH + 1)
            for k in range(KD):
                dve.tensor_tensor(context[:, k, 0:P], mps[:, k * 256:k * 256 + P], headmask[:], ALU.mult)
                ins = dve.tensor_scalar(context[:, k, P:P + 4], headmask[:, 0:P:DH], mps[:, k * 256 + P:k * 256 + P + 1],
                                        None, ALU.mult)
            ins.then_inc(S["ctx_kept"], 1)
            for i in range(NT):
                dve.wait_ge(S["num_filled"], i + 1)
                ps = mps[:, i * 512:i * 512 + KD * (P + 4)].rearrange("p (k c) -> p k c", k=KD)
                den, inv = tiny[:, i * HEADS:(i + 1) * HEADS], tiny2[:, i * HEADS:(i + 1) * HEADS]
                link(dve.tensor_scalar(den.rearrange("p (k h) -> p k h", k=KD), ps[:, :, P:P + 4], ATT_EPS, None, ALU.add))
                link(dve.reciprocal(inv, den))
                link(dve.tensor_scalar(den, inv, float(N), None, ALU.mult))
                for k in range(KD):
                    ins = dve.tensor_tensor(q_tok[:, i, k * P:(k + 1) * P].rearrange("p (h c) -> p h c", c=DH),
                                            ps[:, k, 0:P].rearrange("p (h c) -> p h c", c=DH),
                                            den[:, k * 4:k * 4 + 4, None].broadcast_to([P, 4, DH]), ALU.mult)
                ins.then_inc(S["num_kept"], 1)
            dve.wait_ge(S["qT_filled"], 2 * DEPTH + 1)
            dve.tensor_copy(att_T[:, 0, :], bank(4)).then_inc(S["att_dve"], 1)
            dve.wait_ge(S["proj_filled"], DEPTH + 1)
            link(dve.tensor_copy(q_tok[:], tiles(mps[:, 0:NT * D])))
            link(normalise(q_tok, normed))
            dve.sem_inc(S["norm_ready"], 1)
            normT_half(att_T[:, 0, :], col("m_g1", 0, 0), col("m_b1", 0, 0))
            dve.wait_ge(S["down_filled"], DEPTH + 1)
            link(dve.tensor_copy(q_tok[:], tiles(mps[:, 0:NT * D])))
            link(normalise(q_tok, normed))
            def wide(name):
                return row(name, 0)[:, None, :].broadcast_to([P, NT, D])
            link(dve.tensor_tensor(normed[:], normed[:], wide("m_g2"), ALU.mult))
            link(dve.tensor_tensor(normed[:], normed[:], wide("m_b2"), ALU.add))
            link(dve.tensor_tensor(x_mix[:], x_mix[:], xn_tok[:], ALU.add))
            link(dve.tensor_tensor(x_res[:], x_mix[:], normed[:], ALU.add))

            dve.memset(xh[:, :, :, DH:DH + 1], 1.0)
            for h in range(HEADS):
                ins = dve.tensor_copy(xh[:, :, h, 0:DH], xn_tok[:].rearrange("p t (c h) -> p t c h", h=HEADS)[:, :, :, h])
            link(ins)
            dve.wait_ge(S["uv_filled"], 1)
            uv = gps[:, 0:NT * 2 * HEADS].rearrange("p (t c) -> p t c", t=NT)
            dve.tensor_tensor(su[:], uv[:, :, 0:HEADS], row("b_u", 0, HEADS)[:, None, :].broadcast_to([P, NT, HEADS]), ALU.add)
            link(dve.tensor_copy(sv[:], uv[:, :, HEADS:2 * HEADS]))
            dve.sem_inc(S["uv_ready"], 1)
            for h in range(HEADS):
                dve.wait_ge(S["hrow_filled"], h + 1)
                for i in range(NT):
                    ins = dve.tensor_tensor_reduce(prob[:, i, :], gps[:, 0:NP], no_edge[:, i, :], 1.0, NOEDGE * 2, ALU.add,
                                                   ALU.max, hmax[:, i, h:h + 1])
                ins.then_inc(S["hmax_done"], 1)
            dve.wait_ge(S["hmax_done"], HEADS)
            link(dve.scalar_tensor_tensor(out=hmax[:], in0=hmax[:], scalar=NOEDGE / 2, in1=hmax[:], op0=ALU.is_gt, op1=ALU.mult))
            link(dve.tensor_tensor(hmax[:], hmax[:], sv[:], ALU.add))
            link(dve.scalar_tensor_tensor(out=hm_[:], in0=hmax[:], scalar=0.2, in1=hmax[:], op0=ALU.mult, op1=ALU.max))
            dve.tensor_tensor(hs1[:], sv[:], hm_[:], ALU.subtract)
            dve.tensor_scalar(su2[:], su[:], 0.2, None, ALU.mult)
            dve.scalar_tensor_tensor(out=hs2[:], in0=sv[:], scalar=0.2, in1=hm_[:], op0=ALU.mult, op1=ALU.subtract)\
               .then_inc(S["hshift_ready"], 1)
            for h in range(HEADS):
                probabilities(GAT + h)
                dve.wait_ge(S["hT_filled"], h + 1)
                ps = gps[:, 0:NT * (DH + 1)].rearrange("p (t c) -> p t c", t=NT)
                link(dve.tensor_scalar(tiny[:, 0:NT], ps[:, :, DH], 1e-30, None, ALU.max))
                link(dve.reciprocal(tiny2[:, 0:NT], tiny[:, 0:NT]))
                link(dve.tensor_tensor(hout[:], ps[:, :, 0:DH], tiny2[:, 0:NT, None].broadcast_to([P, NT, DH]), ALU.mult))
                dve.sem_inc(S["hT_kept"], 1)
                xr = x_res[:].rearrange("p t (c h) -> p t c h", h=HEADS)[:, :, :, h]
                link(dve.tensor_tensor(xr, xr, hout[:], ALU.add))
            moe(1, E1, "gate_b", None)
            link(normalise(x_mix, normed))
            link(dve.tensor_tensor(normed[:], normed[:], wide("gamma_out"), ALU.mult))
            link(dve.tensor_tensor(normed[:], normed[:], wide("beta_out"), ALU.add))
            dve.tensor_tensor(normed[:], normed[:], x_res[:], ALU.add).then_inc(S["moe_ready"], 2)

        @block.tensor
        def _(pe):
            turns = [0]

            def product(out, pairs):
                ins = None
                width = out.shape[-1]
                for c in range(0, width, 512):
                    w = min(512, width - c)
                    for n, (lhsT, rhs) in enumerate(pairs):
                        ins = pe.matmul(out[:, c:c + w], lhsT, rhs[:, c:c + w], start=(n == 0), stop=(n == len(pairs) - 1))
                return ins

            def turn(src, k, out):
                for i in range(NT):
                    ins = pe.transpose(out[:, i * P:(i + 1) * P], src[:, i, k * P:(k + 1) * P], ident[:])
                return ins

            def turn_norm(src):
                turns[0] += 1
                n = turns[0]
                pe.wait_ge(S["norm_ready"], n)
                if n > 1:
                    pe.wait_ge(S["normT_dve"], n - 1)
                    pe.wait_ge(S["normT_act"], n - 1)
                turn(src, 0, bank(4)).then_inc(S["normT_filled"], 1)
                turn(src, 1, bank(2)).then_inc(S["normT_filled"], 1)

            def norm_turned():
                pe.wait_ge(S["normT_dve"], turns[0])
                pe.wait_ge(S["normT_act"], turns[0])

            def part(src, k, i):
                return src[:, k, i * P:(i + 1) * P]

            def spread(column, out):
                for i in range(NT):
                    ins = pe.matmul(out[:, i * P:(i + 1) * P], column(i).broadcast_to([P, P]), ident[:], start=True, stop=True)
                return ins

            pe.wait_ge(S["consts_ready"], 1)
            pe.wait_ge(S["in_block_ready"], 1)
            blocks = in_block.rearrange("p b t -> p (b t)")
            for h in range(2):
                c = NT * ET // 2
                ins = pe.matmul(gps[0:1, 512 * h:512 * h + c], ones[0:EP, 0:1], blocks[:, h * c:(h + 1) * c], start=True, stop=True)
            ins.then_inc(S["block_counts"], 1)
            pe.wait_ge(S["span_ready"], 1)
            pe.sem_inc(S["hot_free"], 2)

            turn_no = pe.alloc_register("pe_hot_turn")
            pe.reg_mov(turn_no, 0)
            for b in range(NT):
                first = pe.value_load(span_i[0:1, 0, b:b + 1], min_val=0, max_val=EGN - 1)
                last = pe.value_load(span_i[0:1, 1, b:b + 1], min_val=1, max_val=EGN)
                if b >= 2:
                    pe.wait_ge(S["count_kept"], b - 1)
                out = bank(2 * (b % 2))
                for c, w in ((0, 512), (512, P)):
                    pe.matmul(out[:, c:c + w], zero_b[:, 0:P], zero_b[:, 0:w], start=True, stop=False, skip_group_check=True)
                with pe.Fori(first, last) as g:
                    for u in range(2):
                        pe.reg_add(turn_no, turn_no, 1)
                        pe.wait_ge(S["hot_ready"], pe.snap(turn_no))
                        for s in range(EG // 2):
                            for c, w in ((0, 512), (512, P)):
                                ins = pe.matmul(out[:, c:c + w], hot_dst[:, u, s, :], hot_src[:, u, s, c:c + w],
                                                start=False, stop=False, skip_group_check=True)
                        ins.then_inc(S["hot_free"], 1)
                for c, w in ((0, 512), (512, P)):
                    ins = pe.matmul(out[:, c:c + w], zero_b[:, 0:P], zero_b[:, 0:w], start=False, stop=True, skip_group_check=True)
                ins.then_inc(S["count_filled"], 1)
            pe.wait_ge(S["count_kept"], NT)
            for l in range(NT):
                if l >= 2:
                    pe.wait_ge(S["countT_kept"], l - 1)
                for b in range(NT):
                    ins = pe.transpose(mps[:, 1024 * (l % 2) + b * P:1024 * (l % 2) + (b + 1) * P],
                                       count_dst[:, b, l * P:(l + 1) * P], ident[:])
                ins.then_inc(S["countT_filled"], 1)
            pe.wait_ge(S["countT_kept"], NT)
            turn_norm(x_mix)
            norm_turned()
            pe.wait_ge(S["gatw_ready"], 1)

            def gat_scores(l):
                if l > 0:
                    pe.wait_ge(S["gatin_ready"], KD * l)
                for i in range(NT):
                    if i >= 2:
                        pe.wait_ge(S["h_kept"], NT * l + i - 1)
                    c = (i % 2) * 512
                    product(gps[:, c:c + D + 2], [(part(gat_in, k, i), gat_w[:, l, k, :]) for k in range(KD)])\
                        .then_inc(S["h_filled"], 1)
                pe.wait_ge(S["h_kept"], NT * (l + 1))
                spread(lambda i: score[:, i, 0:1], gps[:, 0:NP]).then_inc(S["srow_filled"], 1)
                pe.wait_ge(S["shift_ready"], l + 1)
                for n in range(2):
                    if n:
                        pe.wait_ge(S["r_kept"], 2 * l + 1)
                    spread(lambda i: shift[:, n, i:i + 1], gps[:, 0:NP]).then_inc(S["r_filled"], 1)

            def gat_sum(l):
                pe.wait_ge(S["r_kept"], 2 * l + 2)
                pe.wait_ge(S["prob_ready"], NT * (l + 1))
                for i in range(NT):
                    if i >= 2:
                        pe.wait_ge(S["agg_kept"], NT * l + i - 1)
                    c = (i % 2) * 512
                    product(gps[:, c:c + D + 1], [(part(prob, s, i), gat_h[:, s, :]) for s in range(NT)])\
                        .then_inc(S["agg_filled"], 1)
                if l < GAT - 1:
                    pe.wait_ge(S["agg_kept"], NT * (l + 1))
                    for k in range(KD):
                        if k:
                            pe.wait_ge(S["gatT_kept"], KD * l + 1)
                        turn(gat_out, k, gps[:, 0:NP]).then_inc(S["gatT_filled"], 1)

            def weight(w, n):
                return w[:, n * KD * D:(n + 1) * KD * D].rearrange("p (k d) -> p k d", k=KD)

            def tokens_by(src, w, c0):
                for i in range(NT):
                    ins = product(mps[:, c0 + i * D:c0 + (i + 1) * D], [(part(src, k, i), w[:, k, :]) for k in range(KD)])
                return ins

            def up(u0, tiles_, srcs, w):
                for j in range(tiles_):
                    u = u0 + j
                    if u >= 2:
                        pe.wait_ge(S["up_kept"], u - 1)
                    product(bank(2 * (u % 2)), [(w[:, k, j * P:(j + 1) * P], src) for k, src in enumerate(srcs)])\
                        .then_inc(S["up_filled"], 1)

            for i in range(DEPTH):
                turn_norm(normed)
                norm_turned()
                pe.wait_ge(S["mixw_loaded"], 16 * (i + 1))
                w = mix_w
                tokens_by(normed_T, weight(w, 0), 0).then_inc(S["qv_filled"], 1)
                tokens_by(normed_T, weight(w, 2), 3 * 512).then_inc(S["qv_filled"], 1)
                for m in range(KD):
                    pe.wait_ge(S["q_shifted" if m == 0 else "v_kept"], i + 1)
                    product(bank(2 * m), [(weight(w, 1)[:, k, m * P:(m + 1) * P], normed_T[:, k, :]) for k in range(KD)])\
                        .then_inc(S["k_filled"], 1)
                if i < GAT:
                    gat_scores(i)
                pe.wait_ge(S["q_normed"], i + 1)
                turn(q_tok, 0, bank(4)).then_inc(S["qT_filled"], 1)
                pe.wait_ge(S["k_exped"], KD * i + 1)
                turn(q_tok, 1, bank(0)).then_inc(S["qT_filled"], 1)
                pe.wait_ge(S["k_exped"], KD * i + 2)
                for m, b in ((0, 2), (1, 4)):
                    if m:
                        pe.wait_ge(S["qT_dve"], i + 1)
                    for j in range(NT):
                        ins = pe.transpose(mps[:, b * 512 + j * P:b * 512 + (j + 1) * P], part(k_exp, m, j), ident[:])
                    ins.then_inc(S["kT_filled"], 1)
                pe.wait_ge(S["qT_act"], i + 1)
                pe.wait_ge(S["kT_dve"], i + 1)
                pe.wait_ge(S["kT_act"], i + 1)
                for m in range(KD):
                    ins = product(mps[:, m * 256:m * 256 + P],
                                  [(k_tok[:, j, m * P:(m + 1) * P], v_tok[:, j, m, 0:P]) for j in range(NT)])
                ins.then_inc(S["ctx_filled"], 1)
                pe.wait_ge(S["ctx_kept"], i + 1)
                for m, b in ((0, 2), (1, 4)):
                    product(bank(b), [(context[:, m, 0:P], q_T[:, m, :])]).then_inc(S["att_filled"], 1)
                pe.wait_ge(S["att_dve"], i + 1)
                pe.wait_ge(S["att_act"], i + 1)
                tokens_by(att_T, weight(w, 3), 0).then_inc(S["proj_filled"], 1)
                turn_norm(normed)
                norm_turned()
                pe.wait_ge(S["ffw_loaded%d" % (i % 2)], 32 * (i // 2 + 1))
                up(8 * i, FF // P, [normed_T[:, k, :] for k in range(KD)], expert_up(i, FF, i % 2))
                if i < GAT:
                    gat_sum(i)
                pe.wait_ge(S["up_kept"], 8 * (i + 1))
                wd = expert_down(i, FF, i % 2)
                for j in range(NT):
                    ins = product(mps[:, j * D:(j + 1) * D], [(part(hidden, h, j), wd[:, h, :]) for h in range(FF // P)])
                ins.then_inc(S["down_filled"], 1)

            def moe(m, experts, width, u0):
                turn_norm(normed)
                norm_turned()
                if m == 0:
                    pe.wait_ge(S["agg_kept"], NT * GAT)
                else:
                    pe.wait_ge(S["hT_kept"], HEADS)
                pe.wait_ge(S["small_loaded"], 16 * 5)
                w = gate_w[:, :, 0:E0] if m == 0 else gate_w[:, :, E0:E0 + E1]
                for i in range(NT):
                    ins = product(gps[:, i * experts:(i + 1) * experts], [(part(normed_T, k, i), w[:, k, :]) for k in range(KD)])
                ins.then_inc(S["gate_filled"], 1)
                pe.wait_ge(S["comb_ready"], m + 1)
                for i in range(NT):
                    ins = pe.transpose(gps[0:experts, i * P:(i + 1) * P], comb[:, i, 0:experts], ident[:])
                ins.then_inc(S["combT_filled"], 1)
                pe.wait_ge(S["combT_kept"], m + 1)
                for i in range(NT):
                    ins = pe.matmul(mps[:, i * D:(i + 1) * D], comb_T[0:experts, i * P:(i + 1) * P], moe_b2[0:experts, m, :],
                                    start=True, stop=True)
                ins.then_inc(S["moe_bias_filled"], 1)
                pe.wait_ge(S["moe_bias_kept"], m + 1)
                J = width // P
                for e in range(experts):
                    n = m * E0 + e
                    r = DEPTH + n + m
                    pe.wait_ge(S["ffw_loaded%d" % (r % 2)], 32 * (r // 2 + 1))
                    up(u0 + e * J, J, [normed_T[:, k, :] for k in range(KD)], expert_up(e, width, r % 2))
                    pe.wait_ge(S["up_kept"], u0 + (e + 1) * J)
                    wd = expert_down(e, width, r % 2)
                    for i in range(NT):
                        c = NT * n + i
                        if c >= 4:
                            pe.wait_ge(S["down_used"], c - 3)
                        product(down_slot(c), [(part(hidden, j, i), wd[:, j, :]) for j in range(J)])\
                            .then_inc(S["moe_down_filled"], 1)

            moe(0, E0, H0, DEPTH * 8)

            turn_norm(xn_tok)
            norm_turned()
            pe.wait_ge(S["mixw_loaded"], 16 * (DEPTH + 1))
            w = mix_w
            for m in range(KD):
                product(bank(2 * m), [(weight(w, 0)[:, k, m * P:(m + 1) * P], normed_T[:, k, :]) for k in range(KD)])\
                    .then_inc(S["qk_filled"], 1)
            pe.wait_ge(S["qk_min"], 1)
            tokens_by(normed_T, weight(w, 1), 0).then_inc(S["qv_filled"], 1)
            tokens_by(normed_T, weight(w, 2), 3 * 512).then_inc(S["qv_filled"], 1)
            pe.wait_ge(S["qk_ready"], 2)
            pe.wait_ge(S["v_kept"], DEPTH + 1)
            for m in range(KD):
                ins = product(mps[:, m * 256:m * 256 + P + 1],
                              [(k_tok[:, j, m * P:(m + 1) * P], v_tok[:, j, m, :]) for j in range(NT)])
            ins.then_inc(S["ctx_filled"], 1)
            pe.wait_ge(S["ctx_kept"], DEPTH + 1)
            for i in range(NT):
                for m in range(KD):
                    c = i * 512 + m * (P + 4)
                    ins = product(mps[:, c:c + P + 4], [(part(q_T, m, i), context[:, m, :])])
                ins.then_inc(S["num_filled"], 1)
            pe.wait_ge(S["num_kept"], NT)
            turn(q_tok, 0, bank(4)).then_inc(S["qT_filled"], 1)
            turn(q_tok, 1, bank(2)).then_inc(S["qT_filled"], 1)
            pe.wait_ge(S["att_dve"], DEPTH + 1)
            pe.wait_ge(S["att_act"], DEPTH + 1)
            tokens_by(att_T, weight(w, 3), 0).then_inc(S["proj_filled"], 1)
            turn_norm(normed)
            norm_turned()
            pe.wait_ge(S["ffw_loaded0"], 32 * ((DEPTH + E0) // 2 + 1))
            w1 = ff_w1[:, 0, :].rearrange("p (k h) -> p k h", k=4)
            w2 = ff_w2[:, 0, 0:4 * D].rearrange("p (k d) -> p k d", k=4)
            u0 = DEPTH * 8 + 64
            up(u0, 4, [normed_T[:, 0, :], normed_T[:, 1, :], att_T[:, 0, :], att_T[:, 1, :]], w1)
            pe.wait_ge(S["up_kept"], u0 + 4)
            for j in range(NT):
                ins = product(mps[:, j * D:(j + 1) * D], [(part(hidden, h, j), w2[:, h, :]) for h in range(4)])
            ins.then_inc(S["down_filled"], 1)

            pe.wait_ge(S["down_used"], NT * E0)
            for i in range(NT):
                ins = product(gps[:, i * 16:(i + 1) * 16], [(part(normed_T, k, i), uv_w[:, k, :]) for k in range(KD)])
            ins.then_inc(S["uv_filled"], 1)
            pe.wait_ge(S["uv_ready"], 1)
            for h in range(HEADS):
                if h:
                    pe.wait_ge(S["hmax_done"], h)
                spread(lambda i: su[:, i, h:h + 1], gps[:, 0:NP]).then_inc(S["hrow_filled"], 1)
            pe.wait_ge(S["hshift_ready"], 1)
            for h in range(HEADS):
                if h:
                    pe.wait_ge(S["hT_kept"], h)
                for n, sh in enumerate((hs1, hs2)):
                    if n:
                        pe.wait_ge(S["hr_kept"], 2 * h + 1)
                    spread(lambda i: sh[:, i, h:h + 1], gps[:, 0:NP]).then_inc(S["hr_filled"], 1)
                pe.wait_ge(S["hr_kept"], 2 * h + 2)
                pe.wait_ge(S["prob_ready"], NT * (GAT + h + 1))
                product(gps[0:DH + 1, 0:NP], [(xh[:, s, h, :], prob[:, s, :]) for s in range(NT)]).then_inc(S["hagg_filled"], 1)
                pe.wait_ge(S["hagg_kept"], h + 1)
                for i in range(NT):
                    ins = pe.transpose(gps[:, i * (DH + 1):(i + 1) * (DH + 1)], head_T[:, i * P:(i + 1) * P],
                                       ident[0:DH + 1, 0:DH + 1])
                ins.then_inc(S["hT_filled"], 1)
            moe(1, E1, H1, u0 + 4)


def kernel(**inputs):
    import numpy as np
    import concourse.bacc as bacc
    from concourse.bass_utils import run_bass_kernel_spmd as run

    a = {k: np.asarray(v) for k, v in inputs.items()}

    def halves(w):
        *lead, r, c = w.shape
        w = w.reshape(*lead, r // P, P, c)
        return np.ascontiguousarray(np.swapaxes(w, -3, -2)).reshape(*lead, P, r // P * c)

    def column(v):
        return v.reshape(-1, P).T

    arrays = {"x": a["x"], "src": a["src"].reshape(ET, EP).T, "dst": a["dst"].reshape(ET, EP).T}
    cols = np.zeros((P, NCOL), np.float32)
    names = {"gat_b": "L0_gnn_b%d", "gamma": "L0_gnn_gamma%d", "beta": "L0_gnn_beta%d"}
    stacked = {"ln1_g": "L0_mix_ln1_g", "ln1_b": "L0_mix_ln1_b", "ln2_g": "L0_mix_ln2_g", "ln2_b": "L0_mix_ln2_b",
               "ff_b1": "L0_mix_b1"}
    for (n, l), c in COLS.items():
        if n in names:
            v = a[names[n] % l]
        elif n in stacked:
            v = a[stacked[n]][l]
        else:
            v = a["L1_mix_" + n[2:]]
        cols[:, c:c + v.size // P] = column(v)
    arrays["cols"] = cols
    rows = np.zeros((1, NROW), np.float32)
    plain = {"gat_b2": "L0_gnn_b2", "bg": "L0_ffn_bg", "b_u": "L1_gnn_b_u", "m_g2": "L1_mix_g2", "m_b2": "L1_mix_b2",
             "gate_b": "L1_ffn_gate_b", "gamma_out": "L1_ffn_gamma", "beta_out": "L1_ffn_beta"}
    for (n, l), c in ROWS.items():
        if n in ("bo", "ff_b2"):
            v = a["L0_mix_" + n[-2:]][l]
        else:
            v = a[plain[n]]
        rows[0, c:c + v.size] = v
    arrays["rows"] = rows
    arrays["gat_w"] = np.stack([halves(a["L0_gnn_W%d" % l]).reshape(P, KD, D) for l in range(GAT)], 1)
    arrays["mix_w"] = np.concatenate([halves(a["L0_mix_" + n]) for n in ("Wq", "Wk", "Wv", "Wo")], -1)
    arrays["ff_w1"], arrays["ff_w2"] = halves(a["L0_mix_W1"]), halves(a["L0_mix_W2"])
    arrays["moe0_w1"] = halves(a["L0_ffn_W1"].transpose(0, 2, 1))
    arrays["moe0_w2"] = halves(a["L0_ffn_W2"].transpose(0, 2, 1))
    arrays["moe1_w1"], arrays["moe1_w2"] = halves(a["L1_ffn_w1"]), halves(a["L1_ffn_w2"])
    arrays["moe0_b2"], arrays["moe1_b2"] = a["L0_ffn_b2"], a["L1_ffn_b2"]
    arrays["moe_b1"] = np.stack([column(a["L0_ffn_b1"].reshape(-1)), column(a["L1_ffn_b1"].reshape(-1))], 1)
    arrays["gate_w"] = np.concatenate([halves(a["L0_ffn_Wg"].T).reshape(P, KD, E0), halves(a["L1_ffn_gate_w"]).reshape(P, KD, E1)], -1)
    arrays["uv_w"] = np.concatenate([halves(a["L1_gnn_W_u"].T).reshape(P, KD, HEADS), halves(a["L1_gnn_W_v"].T).reshape(P, KD, HEADS)], -1)
    arrays["mix1_qkvm"] = np.concatenate([halves(a["L1_mix_" + n]) for n in ("Wq", "Wk", "Wv", "Wm")], -1)
    arrays["mix1_w1"] = halves(a["L1_mix_W1"])
    arrays["mix1_w2"] = halves(a["L1_mix_W2"])
    arrays["a_rows"] = np.concatenate([a["L0_gnn_a_%s%d" % (n, l)] for l in range(GAT) for n in ("src", "dst")])[None, :]

    nc = bacc.Bacc("TRN2", target_bir_lowering=False, num_devices=1)
    t, feed = {}, {}
    for name, v in arrays.items():
        v = np.ascontiguousarray(v)
        feed["in_" + name] = v
        t[name] = nc.dram_tensor("in_" + name, v.shape, mybir.dt.from_np(v.dtype), kind="ExternalInput").ap()
    t["out"] = nc.dram_tensor("out", (N, D), F32, kind="ExternalOutput").ap()
    build(nc, t)
    r = run(nc, [feed], core_ids=[0])
    return r.results[0]["out"]
```

```python
from contextlib import ExitStack

import concourse.bass as bass
from concourse import mybir

F32 = mybir.dt.float32
BF16 = mybir.dt.bfloat16
F16 = mybir.dt.float16
I32 = mybir.dt.int32
U32 = mybir.dt.uint32
ALU = mybir.AluOpType
ACT = mybir.ActivationFunctionType
AX = mybir.AxisListType

P = 128
N = 625
NT = 5
NP = NT * P
LAST = N - (NT - 1) * P
D = 256
KD = D // P
EDGES = 20000
EP = 125
ET = EDGES // EP
EG = 4
EGN = ET // EG
GAT = 3
DEPTH = 4
HEADS = 8
DH = D // HEADS
FF = 1024
E0, H0 = 8, 1024
E1, H1 = 16, 512
EPS = 1e-5
QK_SCALE = float(DH) ** -0.25
NOEDGE = -1.0e30
ATT_EPS = 1e-6
CHUNKS = (2 * N - E1) // P + E1
HEAD = NT

def chunks_of(experts):
    return (2 * N - experts) // P + experts


COLS = {}
_at = 0
for _l in range(GAT):
    COLS["gat_b", _l] = _at; _at += KD
for _l in range(GAT - 1):
    COLS["gamma", _l] = _at; _at += KD
    COLS["beta", _l] = _at; _at += KD
for _l in range(DEPTH):
    for _n in ("ln1_g", "ln1_b", "ln2_g", "ln2_b"):
        COLS[_n, _l] = _at; _at += KD
    COLS["ff_b1", _l] = _at; _at += FF // P
COLS["m_g1", 0] = _at; _at += KD
COLS["m_b1", 0] = _at; _at += KD
NCOL = _at
ROWS = {}
_at = 0
for _l in range(DEPTH):
    ROWS["bo", _l] = _at; _at += D
    ROWS["ff_b2", _l] = _at; _at += D
for _n, _k in (("gat_b2", D), ("bg", E0), ("b_u", HEADS), ("m_g2", D), ("m_b2", D), ("gate_b", E1),
               ("gamma_out", D), ("beta_out", D)):
    ROWS[_n, 0] = _at; _at += _k
NROW = _at


def build(nc, t):
    ctx = ExitStack()
    with ctx:
        def sb(name, shape, dt=F32):
            return ctx.enter_context(nc.sbuf_tensor(name, shape, dt))

        def sem(name):
            return ctx.enter_context(nc.semaphore(name))

        ident = sb("ident", [P, P])
        ones = sb("ones", [P, P])
        iota = sb("iota", [P, NP], F16)
        iota_f = sb("iota_f", [P, E1])
        headmask = sb("headmask", [P, P])
        minus_half = sb("minus_half", [P, 16])
        cols = sb("cols", [P, NCOL])
        rows = sb("rows", [P, NROW])
        x_res = sb("x_res", [P, NT, D])
        x_mix = sb("x_mix", [P, NT, D])
        x_bias = sb("x_bias", [P, NT, D])
        normed = sb("normed", [P, NT, D])
        normed_T = sb("normed_T", [P, KD, NP])
        stats = sb("stats", [P, NT, 6])
        mv = sb("mv", [P, NT, 2])
        var_eps = sb("var_eps", [P, NT])
        rstd = sb("rstd", [P, NT])
        edge_i = sb("edge_i", [EP, 2, ET], I32)
        edge_f = sb("edge_f", [EP, 2, ET])
        present = sb("present", [1, NT * EGN])
        span_f = sb("span_f", [1, 2, NT])
        span_g = sb("span_g", [1, 1, NT])
        marked = sb("marked", [1, NT * EGN])
        group_f = sb("group_f", [1, EGN])
        group_r = sb("group_r", [1, EGN])
        zero_b = sb("zero_b", [EP, 512], BF16)
        span_i = sb("span_i", [1, 2, NT], I32)
        graph = sb("graph", [P, 2, NT, NP])
        count_src = graph[:, 0]
        no_edge = graph[:, 1]
        gat_w = sb("gat_w", [P, GAT, KD, D + 2])
        gat_in = sb("gat_in", [P, KD, NP])
        gat_h = sb("gat_h", [P, NT, D + 1])
        score = sb("score", [P, NT, 2])
        gat_out = sb("gat_out", [P, NT, D])
        score_max = sb("score_max", [P, NT])
        shift = sb("shift", [P, 2, NT])
        score2 = sb("score2", [P, NT])
        tiny = sb("tiny", [P, 8 * NT])
        tiny2 = sb("tiny2", [P, 8 * NT])
        row1 = sb("row1", [P, NP])
        row2 = sb("row2", [P, NP])
        arena = sb("arena", [P, NT + 2 + FF // P, NP])
        prob = arena[:, 0:NT, :]
        prob2 = arena[:, NT:NT + 2, :]
        bn_st = sb("bn_st", [P, KD, 2, 6])
        bn_mv = sb("bn_mv", [P, KD, 2])
        bn_rstd = sb("bn_rstd", [P, KD])
        bn_eps = sb("bn_eps", [P, KD])
        bn_scale = sb("bn_scale", [P, KD])
        bn_shift = sb("bn_shift", [P, KD])
        WQKVO = KD * D
        mix_w = sb("mix_w", [P, 4 * WQKVO])
        ff_w1 = sb("ff_w1", [P, 2, KD * FF])
        ff_w2 = sb("ff_w2", [P, 2, KD * FF])
        q_max = sb("q_max", [P, NT * HEADS])
        v_tok = sb("v_tok", [P, NT, KD, P + 1])
        k_exp = sb("k_exp", [P, KD, NP])
        q_T = sb("q_T", [P, KD, NP])
        k_max = sb("k_max", [P, KD])
        k_top = sb("k_top", [P, KD])
        k_inv = sb("k_inv", [P, KD])
        q_inv = sb("q_inv", [P, NT * HEADS])
        k_sum = sb("k_sum", [P, KD])
        context = sb("context", [P, KD, P + 4])
        att_T = sb("att_T", [P, KD, NP])
        hidden = arena[:, NT + 2:, :]
        gate_w = sb("gate_w", [P, KD, E0 + E1])
        gates = sb("gates", [P, NT, E1])
        top = sb("top", [P, NT, 8])
        top_i = sb("top_i", [P, NT, 8], U32)
        top_f = sb("top_f", [P, NT, 8])
        pair = sb("pair", [P, NT, 4])
        comb = sb("comb", [P, NT, E1])
        first_hot = sb("first_hot", [P, NT, E1])
        chosen = sb("chosen", [P, NT, E1])
        both = sb("both", [P, NT, E1])
        before = sb("before", [P, NT + 1, E1])
        chunk_n = sb("chunk_n", [P, E1])
        scan_a = sb("scan_a", [P, E1])
        scan_b = sb("scan_b", [P, E1])
        chunk_i = sb("chunk_i", [P, E1], I32)
        slot = sb("slot", [P, NT, E1])
        slot_f = sb("slot_f", [P, 2, NT])
        slot_i = sb("slot_i", [P, 2, NT], I32)
        below = sb("below", [P, P])
        moe_b2 = sb("moe_b2", [E1, 2, D])
        moe_b1 = sb("moe_b1", [P, 2, 64])
        uv_w = sb("uv_w", [P, KD, 2 * HEADS])
        su = sb("su", [P, NT, HEADS])
        su2 = sb("su2", [P, NT, HEADS])
        sv = sb("sv", [P, NT, HEADS])
        hmax = sb("hmax", [P, NT, HEADS])
        hm_ = sb("hm_", [P, NT, HEADS])
        hs1 = sb("hs1", [P, NT, HEADS])
        hs2 = sb("hs2", [P, NT, HEADS])
        flat = lambda ap: ap.rearrange("p a b -> p (a b)")
        count_dst = hidden[:, 0:NT, :]
        a_rows = flat(hidden[:, NT:, :])[:, 0:GAT * 2 * D]
        hot_src = flat(q_T[0:EP]).bitcast(BF16).rearrange("p (u s n) -> p u s n", u=2, s=EG // 2)
        in_block = flat(att_T[0:EP])[:, 0:NT * ET].rearrange("p (b t) -> p b t", b=NT)
        hot_dst = flat(att_T[0:EP])[:, NT * ET:NT * ET + EG * P // 2].bitcast(BF16).rearrange("p (u s n) -> p u s n", u=2, s=EG // 2)
        gat_pre = prob[:, 0:KD, :]
        xn_tok = gat_out
        zero_x = x_bias[:, 0, :]
        q_tok = normed
        k_tok = flat(att_T[:]).rearrange("p (t d) -> p t d", t=NT)
        comb_T = row1
        head_T = k_exp[0:DH + 1, 0, :]
        x_chunk = flat(q_T[:])[:, 0:D]
        xT_chunk = flat(q_T[:])[:, D:2 * D].rearrange("p (k n) -> p k n", k=KD)
        hid_chunk = flat(att_T[:])[:, 0:FF].rearrange("p (j n) -> p j n", n=P)
        x_all = [flat(hidden[:]), flat(graph[:].rearrange("p a b c -> p (a b) c"))]
        y_all = [flat(arena[:]), flat(arena[:])]
        picked = [a[:, 0:2 * NT * D].rearrange("p (s t d) -> p s t d", s=2, t=NT) for a in x_all]
        head_prob = [arena[:, 0:NT, :], arena[:, NT:2 * NT, :]]
        head_prob2 = arena[:, 2 * NT:3 * NT, :]
        hidden2 = arena[:, NT:NT + 4, :]
        heads = lambda ap: ap[:, 0:NT * HEADS * (DH + 1)].rearrange("p (t h c) -> p t h c", t=NT, h=HEADS)
        xh = heads(gat_w[:].rearrange("p l k d -> p (l k d)"))
        head_sum = heads(mix_w)
        mps = ctx.enter_context(nc.psum_tensor("mps", [P, 6 * 512], F32))
        gps = ctx.enter_context(nc.psum_tensor("gps", [P, 2 * 512], F32))

        def bank(b, n=NP):
            return mps[:, b * 512:b * 512 + n]

        def col(name, l, k):
            c = COLS[name, l] + k
            return cols[:, c:c + 1]

        def row(name, l, n=D):
            return rows[:, ROWS[name, l]:ROWS[name, l] + n]

        def tiles(ap):
            return ap.rearrange("p (t c) -> p t c", t=NT)

        def halves(ap):
            return ap.rearrange("p (t k c) -> p t k c", t=NT, k=KD)

        def expert_up(h, u):
            c = u // 2 * KD * h
            return ff_w1[:, u % 2, c:c + KD * h].rearrange("p (k h) -> p k h", k=KD)

        def expert_down(h, u):
            c = u // 2 * KD * h
            return ff_w2[:, u % 2, c:c + h // P * D].rearrange("p (j d) -> p j d", j=h // P)

        LAYER2_NORM = 2 * DEPTH + 3

        xs = nc.dram_tensor("expert_in", (CHUNKS * P, D), F32, kind="Internal").ap()
        ys = nc.dram_tensor("expert_out", (CHUNKS * P, D), F32, kind="Internal").ap()

        names = ("x_loaded xpad_zero consts_ready cols_loaded rows_loaded edges_loaded gatw_loaded mixw_loaded "
                 "arows_loaded ffw_loaded0 ffw_loaded1 small_loaded var_ready rstd_ready norm_ready normT_filled "
                 "normT_dve normT_act edge_float in_block_ready block_counts present_ready span_ready hot_ready "
                 "hot_free count_filled count_kept countT_filled countT_kept gatw_ready "
                 "h_filled h_kept srow_filled max_done shift_ready r_filled r_kept exp_ready exp_used "
                 "prob_ready agg_filled agg_kept gatT_filled gatT_kept bnvar_ready bnrstd_ready bn_ready gatin_ready "
                 "qv_filled q_shifted q_exped q_normed v_kept k_filled kmax_ready k_exped qT_filled qT_dve qT_act "
                 "kT_filled kT_dve kT_act ctx_filled ctx_kept att_filled att_dve att_act proj_filled xbias_ready "
                 "x_updated up_filled up_kept down_filled down_used ff_used gate_filled gdiff_ready gexp_ready "
                 "comb_ready combT_filled combT_kept moe_bias_filled out_ready dve_step act_step pool_step "
                 "uv_filled uv_ready hrow_filled hmax_done hshift_ready hr1_filled hr2_filled hr1_used xh_ready prob2_taken "
                 "mix1_kept mix1_added hagg_filled hagg_kept hT_filled hT_kept qk_min qk_exp qk_ready qk_filled num_filled "
                 "num_kept moe_bias_kept "
                 "chosen_ready ranks_filled slots_ready scattered x_head_loaded x_rest_loaded x_copied x_turned xT_kept half_filled "
                 "half_act half_dve y_filled y_kept slots_written expert_done expert_loaded0 expert_loaded1 expert_loaded2 expert_loaded3 x_beta_ready gathered0 gathered1 gathered2 gathered3 gathered4 stored").split()
        S = {n: sem("s_" + n) for n in names}

        block = ctx.enter_context(nc.Block())

        @block.sync
        def _(sp):
            sp.wait_ge(S["xpad_zero"], 1)
            sp.dma_start(x_res[:, 0:NT - 1, :], t["x"][0:(NT - 1) * P].rearrange("(t p) d -> p t d", p=P)).then_inc(S["x_loaded"], 16)
            sp.dma_start(x_res[0:LAST, NT - 1, :], t["x"][(NT - 1) * P:N]).then_inc(S["x_loaded"], 16)
            sp.dma_start(edge_i[:, 0, :], t["src"]).then_inc(S["edges_loaded"], 16)
            sp.dma_start(edge_i[:, 1, :], t["dst"]).then_inc(S["edges_loaded"], 16)
            sp.dma_start(cols[:], t["cols"]).then_inc(S["cols_loaded"], 16)

            sp.dma_start(xs.rearrange("(c p) d -> p c d", p=P), zero_x[:, None, :].broadcast_to([P, CHUNKS, D]))\
              .then_inc(S["slots_written"], 16)
            sp.dma_start(ys.rearrange("(c p) d -> p c d", p=P), zero_x[:, None, :].broadcast_to([P, CHUNKS, D]))\
              .then_inc(S["slots_written"], 16)

            def load_mix(i):
                if i >= 1:
                    sp.wait_ge(S["proj_filled"], i)
                sp.dma_start(mix_w[:], t["mix1_qkvm"] if i == DEPTH else t["mix_w"][i]).then_inc(S["mixw_loaded"], 16)

            def load_ff(n, up, down):
                if 2 <= n < 2 + DEPTH:
                    sp.wait_ge(S["down_filled"], n - 1)
                sp.dma_start(ff_w1[:, n % 2, 0:up.shape[1]], up).then_inc(S["ffw_loaded%d" % (n % 2)], 16)
                sp.dma_start(ff_w2[:, n % 2, 0:down.shape[1]], down).then_inc(S["ffw_loaded%d" % (n % 2)], 16)

            load_mix(0)
            sp.dma_start(rows[:], t["rows"].broadcast_to([P, NROW])).then_inc(S["rows_loaded"], 16)
            sp.dma_start(gat_w[:, :, :, 0:D], t["gat_w"]).then_inc(S["gatw_loaded"], 16)
            load_ff(0, t["ff_w1"][0], t["ff_w2"][0])
            sp.dma_start(a_rows, t["a_rows"].broadcast_to([P, GAT * 2 * D])).then_inc(S["arows_loaded"], 16)
            load_ff(1, t["ff_w1"][1], t["ff_w2"][1])
            sp.dma_start(gate_w[:], t["gate_w"]).then_inc(S["small_loaded"], 16)
            sp.dma_start(uv_w[:], t["uv_w"]).then_inc(S["small_loaded"], 16)
            sp.dma_start(moe_b2[0:E0, 0, :], t["moe0_b2"]).then_inc(S["small_loaded"], 16)
            sp.dma_start(moe_b2[0:E1, 1, :], t["moe1_b2"]).then_inc(S["small_loaded"], 16)
            sp.dma_start(moe_b1[:], t["moe_b1"]).then_inc(S["small_loaded"], 16)
            load_mix(1)
            for i in range(2, DEPTH):
                load_mix(i)
                load_ff(i, t["ff_w1"][i], t["ff_w2"][i])
            load_mix(DEPTH)
            for e in range(2):
                load_ff(DEPTH + e, t["moe0_w1"][e], t["moe0_w2"][e])

            def load_expert(e):
                half = slice(e % 4 // 2 * KD * H1, (e % 4 // 2 + 1) * KD * H1)
                sp.dma_start(ff_w1[:, e % 2, half], t["moe1_w1"][e]).then_inc(S["expert_loaded%d" % (e % 4)], 16)
                sp.dma_start(ff_w2[:, e % 2, half], t["moe1_w2"][e]).then_inc(S["expert_loaded%d" % (e % 4)], 16)

            no, written = (sp.alloc_register("sp_" + n) for n in ("chunk", "written"))
            sp.reg_mov(no, 0)
            sp.reg_mov(written, 32)

            def moe(m, experts):
                sp.wait_ge(S["scattered"], 16 * 2 * NT * (m + 1))
                n = chunks_of(experts)
                for c0, c1, name in ((0, HEAD, "x_head_loaded"), (HEAD, n, "x_rest_loaded")):
                    sp.dma_start(x_all[m][:, c0 * D:c1 * D].rearrange("p (c d) -> p c d", d=D),
                                 xs[c0 * P:c1 * P].rearrange("(c p) d -> p c d", p=P)).then_inc(S[name], 16)
                at = sp.alloc_register("sp_slot%d" % m)
                sp.reg_mov(at, 0)
                for e in range(experts):
                    n = sp.value_load(chunk_i[0:1, e:e + 1], min_val=1, max_val=NT)
                    with sp.Fori(0, n):
                        sp.reg_add(no, no, 1)
                        sp.reg_add(written, written, 16)
                        sp.wait_ge(S["y_kept"], sp.snap(no))
                        here = sp.snap(at, min_val=0, max_val=(CHUNKS - 1) * P)
                        sp.dma_start(ys[bass.ds(here, P), :], y_all[m][:, bass.ds(here * (D // P), D)]).then_inc(S["slots_written"], 16)
                        sp.reg_add(at, at, P)
                    if m == 0 and e + 2 < E0:
                        load_ff(DEPTH + e + 2, t["moe0_w1"][e + 2], t["moe0_w2"][e + 2])
                    elif m == 0 and e + 2 == E0:
                        load_ff(DEPTH + E0, t["mix1_w1"], t["mix1_w2"])
                    elif m == 1 and e + 4 < E1:
                        load_expert(e + 4)
                sp.wait_ge(S["slots_written"], sp.snap(written))
                sp.sem_inc(S["expert_done"], 1)

            moe(0, E0)
            load_expert(1)
            load_expert(3)
            sp.wait_ge(S["down_filled"], DEPTH + 1)
            load_expert(0)
            load_expert(2)
            moe(1, E1)
            sp.wait_ge(S["out_ready"], NT - 1)
            sp.dma_start(t["out"][0:(NT - 1) * P].rearrange("(t p) d -> p t d", p=P), normed[:, 0:NT - 1, :]).then_inc(S["stored"], 16)
            sp.wait_ge(S["out_ready"], NT)
            sp.dma_start(t["out"][(NT - 1) * P:N], normed[0:LAST, NT - 1, :]).then_inc(S["stored"], 16)
            sp.wait_ge(S["stored"], 32)

        @block.gpsimd
        def _(pool):
            steps = [0]

            def link(ins):
                steps[0] += 1
                ins.then_inc(S["pool_step"], 1)
                pool.wait_ge(S["pool_step"], steps[0])

            def rsqrt(dst, var, eps, n, ready, count):
                pool.wait_ge(S[ready], count)
                link(pool.tensor_scalar(eps, var, EPS, None, ALU.add))
                return pool.tensor_tensor(dst, eps, minus_half[:, 0:n], ALU.pow)

            def norm(n):
                rsqrt(rstd[:], mv[:, :, 1], var_eps[:], NT, "var_ready", n).then_inc(S["rstd_ready"], 1)

            pool.memset(zero_x, 0.0)
            link(pool.memset(x_res[:, NT - 1, :], 0.0))
            pool.sem_inc(S["xpad_zero"], 1)
            pool.memset(ones[:], 1.0)
            pool.memset(minus_half[:], -0.5)
            link(pool.memset(ident[:], 0.0))
            pool.affine_select(out=ident[:], in_=ident[:], compare_op=ALU.not_equal, fill=1.0, base=0,
                               pattern=[[-1, P]], channel_multiplier=1)
            pool.iota(iota[:], pattern=[[1, NP]], base=0, channel_multiplier=0, allow_small_or_imprecise_dtypes=True)
            pool.iota(iota_f[:], pattern=[[1, E1]], base=0, channel_multiplier=0, allow_small_or_imprecise_dtypes=True)
            pool.iota(group_f[0:1, :], pattern=[[1, EGN]], base=1, channel_multiplier=0, allow_small_or_imprecise_dtypes=True)
            link(pool.memset(below[:], 1.0))
            pool.affine_select(out=below[:], in_=below[:], compare_op=ALU.is_gt, fill=0.0, base=0,
                               pattern=[[1, P]], channel_multiplier=-1)
            link(pool.memset(headmask[:], 1.0))
            hm = headmask[:].rearrange("p (h e) -> p h e", e=DH)
            link(pool.affine_select(out=hm, in_=hm, compare_op=ALU.is_ge, fill=0.0, base=0,
                                    pattern=[[-DH, P // DH], [0, DH]], channel_multiplier=1))
            link(pool.affine_select(out=hm, in_=hm, compare_op=ALU.is_ge, fill=0.0, base=DH - 1,
                                    pattern=[[DH, P // DH], [0, DH]], channel_multiplier=-1))
            pool.memset(gat_h[:, :, D:D + 1], 1.0)
            pool.memset(k_exp[:, :, N:NP], 0.0)
            pool.memset(zero_b[:], 0.0)
            link(pool.memset(v_tok[:, :, :, P:P + 1], 1.0))
            key_sum = v_tok[:, NT - 1, :, P]
            pool.affine_select(out=key_sum, in_=key_sum, compare_op=ALU.is_ge,
                               fill=0.0, base=LAST - 1, pattern=[[0, KD]], channel_multiplier=-1).then_inc(S["consts_ready"], 1)
            norm(1)
            nth = 1
            for i in range(DEPTH):
                nth += 1
                norm(nth)
                if i == 0:
                    pool.wait_ge(S["rows_loaded"], 16)
                    pool.wait_ge(S["slots_written"], 32)
                if i > 0:
                    pool.wait_ge(S["x_updated"], 2 * i)
                pool.tensor_tensor(x_bias[:], x_mix[:], row("bo", i)[:, None, :].broadcast_to([P, NT, D]),
                                   ALU.add).then_inc(S["xbias_ready"], 1)
                pool.wait_ge(S["x_updated"], 2 * i + 1)
                pool.tensor_tensor(x_bias[:], x_mix[:], row("ff_b2", i)[:, None, :].broadcast_to([P, NT, D]),
                                   ALU.add).then_inc(S["xbias_ready"], 1)
                nth += 1
                norm(nth)
                if i < GAT - 1:
                    rsqrt(bn_rstd[:], bn_mv[:, :, 1], bn_eps[:], KD, "bnvar_ready", i + 1).then_inc(S["bnrstd_ready"], 1)
            def exchange(m):
                pool.wait_ge(S["slots_written"], 32)
                pool.wait_ge(S["slots_ready"], m + 1)
                for s in range(2):
                    for i in range(NT):
                        n = P if i < NT - 1 else LAST
                        pool.indirect_dma_start(xs, bass.IndirectOffsetOnAxis(ap=slot_i[0:n, s, i:i + 1], axis=0), normed[0:n, i, :],
                                                None).then_inc(S["scattered"], 16)
                if m == 1:
                    pool.tensor_tensor(x_res[:], x_res[:], row("beta_out", 0)[:, None, :].broadcast_to([P, NT, D]), ALU.add)\
                        .then_inc(S["x_beta_ready"], 1)
                pool.wait_ge(S["expert_done"], m + 1)
                for i in range(NT):
                    for s in range(2):
                        n = P if i < NT - 1 else LAST
                        pool.indirect_dma_start(picked[m][0:n, s, i, :], None, ys,
                                                bass.IndirectOffsetOnAxis(ap=slot_i[0:n, s, i:i + 1], axis=0)).then_inc(S["gathered%d" % i], 16)

            nth += 1
            norm(nth)
            exchange(0)
            nth += 1
            norm(nth)
            pool.wait_ge(S["norm_ready"], LAYER2_NORM)
            pool.memset(xh[:, :, :, DH:DH + 1], 1.0)
            pool.tensor_copy(xh[:, :, :, 0:DH], xn_tok[:].rearrange("p t (c h) -> p t h c", h=HEADS)).then_inc(S["xh_ready"], 1)
            for _ in range(2):
                nth += 1
                norm(nth)
            pool.wait_ge(S["mix1_kept"], 1)
            link(pool.tensor_tensor(normed[:], normed[:], row("m_g2", 0)[:, None, :].broadcast_to([P, NT, D]), ALU.mult))
            link(pool.tensor_tensor(normed[:], normed[:], row("m_b2", 0)[:, None, :].broadcast_to([P, NT, D]), ALU.add))
            link(pool.tensor_tensor(normed[:], normed[:], xn_tok[:], ALU.add))
            pool.tensor_tensor(normed[:], normed[:], x_mix[:], ALU.add).then_inc(S["mix1_added"], 1)
            nth += 1
            norm(nth)
            exchange(1)
            nth += 1
            norm(nth)

        @block.scalar
        def _(act):
            steps = [0]

            def link(ins):
                steps[0] += 1
                ins.then_inc(S["act_step"], 1)
                act.wait_ge(S["act_step"], steps[0])

            def normT_half(n, dst, g=None, b=None):
                act.wait_ge(S["normT_filled"], 2 * n)
                if g is None:
                    ins = act.activation(dst, bank(2), ACT.Copy)
                else:
                    ins = act.activation(dst, bank(2), ACT.Identity, bias=b, scale=g)
                ins.then_inc(S["normT_act"], 1)

            def up_tile(u, dst, func, bias):
                act.wait_ge(S["up_filled"], u + 1)
                act.activation(dst, bank(2 * (u % 2)), func, bias=bias).then_inc(S["up_kept"], 1)

            act.wait_ge(S["consts_ready"], 1)
            act.wait_ge(S["cols_loaded"], 16)
            for l in range(NT):
                act.wait_ge(S["countT_filled"], l + 1)
                act.activation(count_src[:, l, :], bank(2 * (l % 2)), ACT.Copy).then_inc(S["countT_kept"], 1)
            normT_half(1, gat_in[:, 1, :])

            def gat_rows(l):
                for i in range(NT):
                    act.wait_ge(S["h_filled"], NT * l + i + 1)
                    if i == 0 and l > 0:
                        act.wait_ge(S["agg_filled"], NT * l)
                    ps = gps[:, (i % 2) * 512:(i % 2) * 512 + D + 2]
                    act.activation(gat_h[:, i, 0:D], ps[:, 0:D], ACT.Copy)
                    act.activation(score[:, i, :], ps[:, D:D + 2], ACT.Copy).then_inc(S["h_kept"], 1)
                for n, dst in enumerate((row1, row2)):
                    act.wait_ge(S["r_filled"], 2 * l + n + 1)
                    act.activation(dst[:], gps[:, 0:NP], ACT.Copy).then_inc(S["r_kept"], 1)

            def exponentials(l):
                act.wait_ge(S["r_kept"], 2 * l + 2)
                for i in range(NT):
                    c = NT * l + i
                    act.activation(prob[:, i, :], row1[:], ACT.Exp, bias=score[:, i, 0:1])
                    if c >= 2:
                        act.wait_ge(S["prob2_taken"], c - 1)
                    act.activation(prob2[:, c % 2, :], row2[:], ACT.Exp, bias=score2[:, i:i + 1]).then_inc(S["exp_ready"], 1)

            def gat_turn(l):
                for k in range(KD):
                    act.wait_ge(S["gatT_filled"], KD * l + k + 1)
                    act.activation(gat_pre[:, k, :], gps[:, 0:NP], ACT.Identity, bias=col("gat_b", l, k)).then_inc(S["gatT_kept"], 1)
                act.wait_ge(S["bn_ready"], l + 1)
                for k in range(KD):
                    act.activation(gat_in[:, k, :], gat_pre[:, k, :], ACT.Relu, bias=bn_shift[:, k:k + 1],
                                   scale=bn_scale[:, k:k + 1]).then_inc(S["gatin_ready"], 1)

            nth = 1
            for i in range(DEPTH):
                nth += 1
                normT_half(nth, normed_T[:, 1, :], col("ln1_g", i, 1), col("ln1_b", i, 1))
                act.wait_ge(S["qv_filled"], 2 * i + 2)
                act.activation(v_tok[:, :, :, 0:P], halves(bank(3, NT * D)), ACT.Copy).then_inc(S["v_kept"], 1)
                act.wait_ge(S["q_shifted"], i + 1)
                act.activation(q_tok[:], q_tok[:], ACT.Exp, scale=QK_SCALE).then_inc(S["q_exped"], 1)
                for k in range(KD):
                    act.wait_ge(S["kmax_ready"], KD * i + k + 1)
                    act.activation(k_exp[:, k, 0:N], bank(2 * k, N), ACT.Exp, bias=k_max[:, k:k + 1], scale=QK_SCALE,
                                   accum_out=k_sum[:, k:k + 1]).then_inc(S["k_exped"], 1)
                if i < GAT:
                    gat_rows(i)
                act.wait_ge(S["qT_filled"], 2 * i + 2)
                act.activation(q_T[:, 1, :], bank(0), ACT.Copy).then_inc(S["qT_act"], 1)
                act.wait_ge(S["kT_filled"], 2 * i + 2)
                act.activation(k_tok[:, :, P:D], tiles(bank(4)), ACT.Copy).then_inc(S["kT_act"], 1)
                act.wait_ge(S["att_filled"], 2 * i + 2)
                act.activation(att_T[:, 1, :], bank(4), ACT.Copy).then_inc(S["att_act"], 1)
                nth += 1
                normT_half(nth, normed_T[:, 1, :], col("ln2_g", i, 1), col("ln2_b", i, 1))
                if i < GAT:
                    exponentials(i)
                for j in range(FF // P):
                    up_tile(FF // P * i + j, hidden[:, j, :], ACT.Gelu, cols[:, COLS["ff_b1", i] + j:COLS["ff_b1", i] + j + 1])
                if i < GAT - 1:
                    gat_turn(i)

            def moe(m, experts, width):
                nonlocal nth
                nth += 1
                normT_half(nth, normed_T[:, 1, :])
                act.wait_ge(S["gdiff_ready"], m + 1)
                act.activation(pair[:, :, 1], pair[:, :, 0], ACT.Exp).then_inc(S["gexp_ready"], 1)
                act.wait_ge(S["combT_filled"], m + 1)
                act.activation(comb_T[0:experts, :], bank(3)[0:experts, :], ACT.Copy).then_inc(S["combT_kept"], 1)
                act.wait_ge(S["small_loaded"], 16 * 5)
                act.wait_ge(S["slots_ready"], m + 1)
                Q = width // P // 4
                at = act.alloc_register("act_chunk%d" % m)

                def copy_chunk():
                    c = act.snap(at, min_val=0, max_val=(chunks_of(experts) - 1) * D)
                    act.activation(x_chunk, x_all[m][:, bass.ds(c, D)], ACT.Copy).then_inc(S["x_copied"], 1)
                    act.reg_add(at, at, D)

                act.reg_mov(at, 0)
                act.wait_ge(S["x_head_loaded"], 16 * (m + 1))
                copy_chunk()
                act.reg_add(turned_no, turned_no, 1)
                act.wait_ge(S["x_rest_loaded"], 16 * (m + 1))
                for e in range(experts):
                    n = act.value_load(chunk_i[0:1, e:e + 1], min_val=1, max_val=NT)
                    with act.Fori(0, n):
                        act.wait_ge(S["x_turned"], act.snap(turned_no))
                        act.reg_add(turned_no, turned_no, 1)
                        copy_chunk()
                        for h in range(2):
                            act.reg_add(halves_no, halves_no, 1)
                            act.wait_ge(S["half_filled"], act.snap(halves_no))
                            for q in range(Q):
                                j = 2 * h * Q + q
                                ins = act.activation(hid_chunk[:, j, :], mps[:, 1024 * h + q * P:1024 * h + (q + 1) * P], ACT.Relu,
                                                     bias=moe_b1[:, m, e * 4 * Q + j:e * 4 * Q + j + 1])
                            ins.then_inc(S["half_act"], 1)

            halves_no = act.alloc_register("act_half")
            turned_no = act.alloc_register("act_turned")
            act.reg_mov(halves_no, 0)
            act.reg_mov(turned_no, 0)
            moe(0, E0, H0)
            nth += 1
            normT_half(nth, normed_T[:, 1, :])
            act.wait_ge(S["qk_min"], 1)
            act.activation(q_T[:], q_T[:], ACT.Exp).then_inc(S["qk_exp"], 1)
            act.wait_ge(S["qk_min"], 2)
            act.activation(k_tok[:], k_tok[:], ACT.Exp).then_inc(S["qk_exp"], 1)
            act.wait_ge(S["qv_filled"], 2 * DEPTH + 2)
            act.activation(v_tok[:, :, :, 0:P], halves(bank(3, NT * D)), ACT.Copy, scale=1.0 / N).then_inc(S["v_kept"], 1)
            act.wait_ge(S["qT_filled"], 2 * DEPTH + 2)
            act.activation(att_T[:, 1, :], bank(2), ACT.Copy).then_inc(S["att_act"], 1)
            nth += 1
            normT_half(nth, att_T[:, 1, :], col("m_g1", 0, 1), col("m_b1", 0, 1))

            def first_exponentials(h):
                act.wait_ge(S["hr1_filled"], h + 1)
                if h == 1:
                    act.wait_ge(S["down_filled"], DEPTH + 1)
                elif h:
                    act.wait_ge(S["hagg_filled"], h - 1)
                for i in range(NT):
                    ins = act.activation(head_prob[h % 2][:, i, :], gps[:, 0:NP], ACT.Exp, bias=su[:, i, h:h + 1])
                ins.then_inc(S["hr1_used"], 1)

            def second_exponentials(h):
                act.wait_ge(S["hr2_filled"], h + 1)
                for i in range(NT):
                    if h:
                        act.wait_ge(S["prob2_taken"], NT * (GAT + h - 1) + i + 1)
                    act.activation(head_prob2[:, i, :], bank(4), ACT.Exp, bias=su2[:, i, h:h + 1]).then_inc(S["exp_ready"], 1)

            for j in range(4):
                up_tile(DEPTH * 8 + j, hidden2[:, j, :], ACT.Relu, 0.0)
                if j == 1:
                    first_exponentials(0)
            second_exponentials(0)
            for h in range(1, HEADS + 1):
                if h < HEADS:
                    first_exponentials(h)
                    second_exponentials(h)
                act.wait_ge(S["hagg_filled"], h)
                if h > 1:
                    act.wait_ge(S["hT_filled"], h - 1)
                act.activation(head_T[:], mps[0:DH + 1, 0:NP], ACT.Copy).then_inc(S["hagg_kept"], 1)
            moe(1, E1, H1)

        @block.vector
        def _(dve):
            steps = [0]

            def link(ins):
                steps[0] += 1
                ins.then_inc(S["dve_step"], 1)
                dve.wait_ge(S["dve_step"], steps[0])

            norms, turns = [0], [0]

            def normalise(src, dst, stats_taken=False):
                norms[0] += 1
                if not stats_taken:
                    for i in range(NT):
                        ins = dve.bn_stats(stats[:, i, :], src[:, i, :])
                    link(ins)
                for i in range(NT):
                    ins = dve.bn_aggr(mv[:, i, :], stats[:, i, :])
                ins.then_inc(S["var_ready"], 1)
                dve.wait_ge(S["rstd_ready"], norms[0])
                for i in range(NT):
                    ins = dve.tensor_scalar(dst[:, i, :], src[:, i, :], mv[:, i, 0:1], rstd[:, i:i + 1],
                                            ALU.subtract, ALU.mult)
                return ins

            def normT_half(dst, g=None, b=None):
                turns[0] += 1
                dve.wait_ge(S["normT_filled"], 2 * turns[0] - 1)
                if g is None:
                    ins = dve.tensor_copy(dst, bank(4))
                else:
                    ins = dve.tensor_scalar(dst, bank(4), g, b, ALU.mult, ALU.add)
                ins.then_inc(S["normT_dve"], 1)

            dve.wait_ge(S["consts_ready"], 1)
            dve.wait_ge(S["edges_loaded"], 32)
            link(dve.tensor_copy(edge_f[:], edge_i[:]))
            for b in range(NT):
                link(dve.tensor_scalar(in_block[:, b, :], edge_f[:, 1, :], float(P * b), None, ALU.is_ge))
                ins = dve.scalar_tensor_tensor(out=in_block[:, b, :], in0=edge_f[:, 1, :], scalar=float(P * (b + 1)),
                                               in1=in_block[:, b, :], op0=ALU.is_lt, op1=ALU.mult)
            link(ins)
            dve.sem_inc(S["in_block_ready"], 1)
            dve.wait_ge(S["block_counts"], 1)
            for h in range(2):
                c = NT * ET // 2
                ins = dve.tensor_reduce(present[0:1, h * c // EG:(h + 1) * c // EG],
                                        gps[0:1, 512 * h:512 * h + c].rearrange("p (g s) -> p g s", s=EG), AX.X, ALU.add)
            link(ins)
            pr = present[:].rearrange("p (b g) -> p b g", b=NT)
            gr = group_f[0:1, None, :].broadcast_to([1, NT, EGN])
            link(dve.tensor_scalar(present[:], present[:], 0.0, None, ALU.is_gt))
            link(dve.tensor_tensor(marked[:].rearrange("p (b g) -> p b g", b=NT), pr, gr, ALU.mult))
            link(dve.tensor_reduce(span_f[:, 1, :], marked[:].rearrange("p (b g) -> p b g", b=NT), AX.X, ALU.max))
            link(dve.tensor_scalar(group_r[:], group_f[:], -1.0, float(EGN + 1), ALU.mult, ALU.add))
            link(dve.tensor_tensor(marked[:].rearrange("p (b g) -> p b g", b=NT), pr,
                                   group_r[0:1, None, :].broadcast_to([1, NT, EGN]), ALU.mult))
            link(dve.tensor_reduce(span_f[:, 0, :], marked[:].rearrange("p (b g) -> p b g", b=NT), AX.X, ALU.max))
            link(dve.tensor_scalar(span_f[:, 0, :], span_f[:, 0, :], -1.0, float(EGN), ALU.mult, ALU.add))
            link(dve.tensor_scalar(span_f[:, 0, :], span_f[:, 0, :], float(EGN - 1), None, ALU.min))
            link(dve.tensor_scalar(span_g[:, 0, :], span_f[:, 0, :], 1.0, None, ALU.add))
            link(dve.tensor_tensor(span_f[:, 1, :], span_f[:, 1, :], span_g[:, 0, :], ALU.max))
            link(dve.tensor_copy(span_i[:], span_f[:]))
            dve.sem_inc(S["span_ready"], 1)

            turn_no = dve.alloc_register("dve_hot_turn")
            dve.reg_mov(turn_no, 0)
            for b in range(NT):
                first = dve.value_load(span_i[0:1, 0, b:b + 1], min_val=0, max_val=EGN - 1)
                last = dve.value_load(span_i[0:1, 1, b:b + 1], min_val=1, max_val=EGN)
                with dve.Fori(first, last) as g:
                    for u in range(2):
                        dve.reg_add(turn_no, turn_no, 1)
                        dve.wait_ge(S["hot_free"], dve.snap(turn_no))
                        for s in range(EG // 2):
                            c = bass.ds(g * EG + u * (EG // 2) + s, 1)
                            dve.tensor_scalar(hot_src[:, u, s, :], iota[0:EP, :], edge_f[:, 0, c], None, ALU.is_equal)
                            ins = dve.tensor_scalar(hot_dst[:, u, s, :], iota[0:EP, P * b:P * (b + 1)], edge_f[:, 1, c],
                                                    None, ALU.is_equal)
                        ins.then_inc(S["hot_ready"], 1)
                dve.wait_ge(S["count_filled"], b + 1)
                dve.tensor_copy(count_dst[:, b, :], bank(2 * (b % 2)))
                dve.tensor_scalar(no_edge[:, b, :], bank(2 * (b % 2)), 0.0, NOEDGE, ALU.is_equal, ALU.mult).then_inc(S["count_kept"], 1)

            dve.wait_ge(S["rows_loaded"], 16)
            dve.wait_ge(S["arows_loaded"], 16)
            dve.wait_ge(S["gatw_loaded"], 16)
            for l in range(GAT):
                for n in range(2):
                    for k in range(KD):
                        s0 = ((l * 2 + n) * KD + k) * D
                        ins = dve.tensor_tensor_reduce(flat(prob[:])[:, s0:s0 + D], gat_w[:, l, k, 0:D], a_rows[:, (2 * l + n) * D:(2 * l + n + 1) * D], 1.0, 0.0, ALU.mult,
                                                       ALU.add, gat_w[:, l, k, D + n:D + n + 1])
            ins.then_inc(S["gatw_ready"], 1)

            dve.wait_ge(S["x_loaded"], 32)
            link(normalise(x_res, x_mix))
            dve.sem_inc(S["norm_ready"], 1)
            normT_half(gat_in[:, 0, :])

            def gat_shift(l):
                dve.wait_ge(S["srow_filled"], l + 1)
                for i in range(NT):
                    ins = dve.tensor_tensor_reduce(prob[:, i, :], gps[:, 0:NP], no_edge[:, i, :], 1.0, NOEDGE * 2, ALU.add,
                                                   ALU.max, score_max[:, i:i + 1])
                ins.then_inc(S["max_done"], 1)
                dve.wait_ge(S["max_done"], l + 1)
                link(dve.scalar_tensor_tensor(out=score_max[:], in0=score_max[:], scalar=NOEDGE / 2, in1=score_max[:],
                                              op0=ALU.is_gt, op1=ALU.mult))
                link(dve.tensor_tensor(tiny[:, 0:NT], score_max[:], score[:, :, 1], ALU.add))
                link(dve.scalar_tensor_tensor(out=tiny2[:, 0:NT], in0=tiny[:, 0:NT], scalar=0.2, in1=tiny[:, 0:NT],
                                              op0=ALU.mult, op1=ALU.max))
                dve.tensor_tensor(shift[:, 0, :], score[:, :, 1], tiny2[:, 0:NT], ALU.subtract)
                dve.tensor_scalar(score2[:], score[:, :, 0], 0.2, None, ALU.mult)
                dve.scalar_tensor_tensor(out=shift[:, 1, :], in0=score[:, :, 1], scalar=0.2, in1=tiny2[:, 0:NT],
                                         op0=ALU.mult, op1=ALU.subtract).then_inc(S["shift_ready"], 1)

            def probabilities(n, p1, p2):
                def larger(i):
                    dve.wait_ge(S["exp_ready"], n + i + 1)
                    dve.tensor_tensor(p1[:, i, :], p1[:, i, :], p2(i), ALU.max).then_inc(S["prob2_taken"], 1)

                def counted(i):
                    dve.wait_ge(S["prob2_taken"], n + i + 1)
                    dve.scalar_tensor_tensor(out=p1[:, i, :], in0=p1[:, i, :], scalar=1.0, in1=count_src[:, i, :],
                                             op0=ALU.min, op1=ALU.mult).then_inc(S["prob_ready"], 1)

                larger(0)
                for i in range(1, NT):
                    larger(i)
                    counted(i - 1)
                counted(NT - 1)

            def gat_aggregate(l):
                probabilities(NT * l, prob, lambda i: prob2[:, (NT * l + i) % 2, :])
                for i in range(NT):
                    dve.wait_ge(S["agg_filled"], NT * l + i + 1)
                    ps = gps[:, (i % 2) * 512:(i % 2) * 512 + D + 1]
                    link(dve.tensor_scalar(tiny[:, 0:1], ps[:, D:D + 1], 1e-16, None, ALU.add))
                    link(dve.reciprocal(tiny[:, 1:2], tiny[:, 0:1]))
                    dve.tensor_scalar(gat_out[:, i, :], ps[:, 0:D], tiny[:, 1:2], None, ALU.mult).then_inc(S["agg_kept"], 1)

            def gat_batchnorm(l):
                for k in range(KD):
                    dve.wait_ge(S["gatT_kept"], KD * l + k + 1)
                    dve.bn_stats(bn_st[:, k, 0, :], gat_pre[:, k, 0:512])
                    ins = dve.bn_stats(bn_st[:, k, 1, :], gat_pre[:, k, 512:N])
                link(ins)
                for k in range(KD):
                    ins = dve.bn_aggr(bn_mv[:, k, :], bn_st[:, k, :, :])
                ins.then_inc(S["bnvar_ready"], 1)
                dve.wait_ge(S["bnrstd_ready"], l + 1)
                c = COLS["gamma", l]
                link(dve.tensor_tensor(bn_scale[:], bn_rstd[:], cols[:, c:c + KD], ALU.mult))
                link(dve.tensor_tensor(bn_shift[:], bn_mv[:, :, 0], bn_scale[:], ALU.mult))
                c = COLS["beta", l]
                dve.tensor_tensor(bn_shift[:], cols[:, c:c + KD], bn_shift[:], ALU.subtract).then_inc(S["bn_ready"], 1)

            def residual(n, ps):
                dve.wait_ge(S["xbias_ready"], n)
                link(dve.tensor_tensor(x_mix[:], ps, x_bias[:], ALU.add))
                dve.sem_inc(S["x_updated"], 1)

            for i in range(DEPTH):
                link(normalise(x_mix, normed))
                dve.sem_inc(S["norm_ready"], 1)
                normT_half(normed_T[:, 0, :], col("ln1_g", i, 0), col("ln1_b", i, 0))
                dve.wait_ge(S["qv_filled"], 2 * i + 1)
                heads = mps[:, 0:NT * D].rearrange("p (g c) -> p g c", c=DH)
                link(dve.tensor_reduce(q_max[:], heads, AX.X, ALU.max))
                qh = q_tok[:].rearrange("p t (g c) -> p (t g) c", c=DH)
                dve.tensor_tensor(qh, heads, q_max[:, :, None].broadcast_to([P, NT * HEADS, DH]),
                                  ALU.subtract).then_inc(S["q_shifted"], 1)
                for k in range(KD):
                    dve.wait_ge(S["k_filled"], KD * i + k + 1)
                    link(dve.tensor_reduce(k_top[:, k:k + 1], bank(2 * k, N), AX.X, ALU.max))
                    dve.tensor_scalar(k_max[:, k:k + 1], k_top[:, k:k + 1], -QK_SCALE, None, ALU.mult).then_inc(S["kmax_ready"], 1)
                dve.wait_ge(S["q_exped"], i + 1)
                link(dve.tensor_reduce(q_max[:], qh, AX.X, ALU.add))
                link(dve.reciprocal(q_inv[:], q_max[:]))
                dve.tensor_tensor(qh, qh, q_inv[:, :, None].broadcast_to([P, NT * HEADS, DH]), ALU.mult).then_inc(S["q_normed"], 1)
                if i < GAT:
                    gat_shift(i)
                dve.wait_ge(S["qT_filled"], 2 * i + 1)
                dve.tensor_copy(q_T[:, 0, :], bank(4)).then_inc(S["qT_dve"], 1)
                dve.wait_ge(S["kT_filled"], 2 * i + 1)
                dve.tensor_copy(k_tok[:, :, 0:P], tiles(bank(2))).then_inc(S["kT_dve"], 1)
                dve.wait_ge(S["k_exped"], KD * i + 2)
                link(dve.reciprocal(k_inv[:], k_sum[:]))
                dve.wait_ge(S["ctx_filled"], i + 1)
                for k in range(KD):
                    ins = dve.scalar_tensor_tensor(out=context[:, k, 0:P], in0=mps[:, k * 256:k * 256 + P], scalar=k_inv[:, k:k + 1],
                                                   in1=headmask[:], op0=ALU.mult, op1=ALU.mult)
                ins.then_inc(S["ctx_kept"], 1)
                dve.wait_ge(S["att_filled"], 2 * i + 1)
                dve.tensor_copy(att_T[:, 0, :], bank(2)).then_inc(S["att_dve"], 1)
                dve.wait_ge(S["proj_filled"], i + 1)
                residual(2 * i + 1, tiles(mps[:, 0:NT * D]))
                link(normalise(x_mix, normed))
                dve.sem_inc(S["norm_ready"], 1)
                normT_half(normed_T[:, 0, :], col("ln2_g", i, 0), col("ln2_b", i, 0))
                if i < GAT:
                    gat_aggregate(i)
                if i < GAT - 1:
                    gat_batchnorm(i)
                dve.wait_ge(S["down_filled"], i + 1)
                residual(2 * i + 2, tiles(mps[:, 0:NT * D]))
            link(dve.tensor_tensor(x_res[:], x_res[:], gat_out[:], ALU.add))
            link(dve.tensor_tensor(x_res[:], x_res[:], row("gat_b2", 0)[:, None, :].broadcast_to([P, NT, D]), ALU.add))
            link(dve.tensor_tensor(x_res[:], x_res[:], x_mix[:], ALU.add))

            def moe(m, experts, width, bias):
                link(normalise(x_res, normed))
                dve.sem_inc(S["norm_ready"], 1)
                normT_half(normed_T[:, 0, :])
                dve.wait_ge(S["gate_filled"], m + 1)
                g = gates[:, :, 0:experts]
                link(dve.tensor_tensor(g, gps[:, 0:NT * experts].rearrange("p (t e) -> p t e", t=NT),
                                       row(bias, 0, experts)[:, None, :].broadcast_to([P, NT, experts]), ALU.add))
                for i in range(NT):
                    ins = dve.max(top[:, i, :], gates[:, i, 0:experts])
                link(ins)
                for i in range(NT):
                    ins = dve.max_index(top_i[:, i, :], top[:, i, :], gates[:, i, 0:experts])
                link(ins)
                dve.tensor_tensor(pair[:, :, 0], top[:, :, 1], top[:, :, 0], ALU.subtract).then_inc(S["gdiff_ready"], 1)
                link(dve.tensor_copy(top_f[:], top_i[:]))
                ch, fh, bo = (a[:, :, 0:experts] for a in (chosen, first_hot, both))
                wide = lambda column: column[:, :, None].broadcast_to([P, NT, experts])
                expert_no = iota_f[:, None, 0:experts].broadcast_to([P, NT, experts])
                dve.tensor_tensor(fh, expert_no, wide(top_f[:, :, 0]), ALU.is_equal)
                link(dve.tensor_tensor(ch, expert_no, wide(top_f[:, :, 1]), ALU.is_equal))
                link(dve.tensor_tensor(bo, ch, fh, ALU.add))
                valid = v_tok[:, NT - 1, 0, P:P + 1]
                link(dve.tensor_scalar(both[:, NT - 1, 0:experts], both[:, NT - 1, 0:experts], valid, None, ALU.mult))
                dve.sem_inc(S["chosen_ready"], 1)
                dve.wait_ge(S["gexp_ready"], m + 1)
                link(dve.tensor_scalar(pair[:, :, 0], pair[:, :, 1], 1.0, None, ALU.add))
                link(dve.reciprocal(pair[:, :, 2], pair[:, :, 0]))
                link(dve.tensor_tensor(pair[:, :, 3], pair[:, :, 1], pair[:, :, 2], ALU.mult))
                cb, sl = comb[:, :, 0:experts], slot[:, :, 0:experts]
                dve.tensor_tensor(cb, fh, wide(pair[:, :, 2]), ALU.mult)
                link(dve.tensor_tensor(sl, ch, wide(pair[:, :, 3]), ALU.mult))
                link(dve.tensor_tensor(cb, cb, sl, ALU.add))
                dve.sem_inc(S["comb_ready"], 1)
                dve.wait_ge(S["ranks_filled"], m + 1)
                link(dve.memset(before[:, 0, :], 0.0))
                within = gps[:, 0:NT * experts].rearrange("p (t e) -> p t e", t=NT)
                totals = gps[:, 512:512 + NT * experts].rearrange("p (t e) -> p t e", t=NT)
                for i in range(NT):
                    link(dve.tensor_tensor(before[:, i + 1, 0:experts], before[:, i, 0:experts], totals[:, i, :], ALU.add))
                n = before[:, NT, 0:experts]
                link(dve.tensor_scalar(chunk_n[:, 0:experts], n, float(P), 1.0, ALU.is_gt, ALU.add))
                for k in range(2, NT):
                    link(dve.scalar_tensor_tensor(out=chunk_n[:, 0:experts], in0=n, scalar=float(P * k), in1=chunk_n[:, 0:experts],
                                                  op0=ALU.is_gt, op1=ALU.add))
                dve.tensor_copy(chunk_i[:, 0:experts], chunk_n[:, 0:experts])
                link(dve.memset(scan_a[:, 0:1], 0.0))
                link(dve.tensor_scalar(scan_a[:, 1:experts], chunk_n[:, 0:experts - 1], float(P), None, ALU.mult))
                a, b, d = scan_a, scan_b, 1
                while d < experts:
                    dve.tensor_copy(b[:, 0:d], a[:, 0:d])
                    link(dve.tensor_tensor(b[:, d:experts], a[:, d:experts], a[:, 0:experts - d], ALU.add))
                    a, b, d = b, a, 2 * d
                link(dve.tensor_tensor(sl, within, before[:, 0:NT, 0:experts], ALU.add))
                link(dve.tensor_tensor(sl, sl, a[:, None, 0:experts].broadcast_to([P, NT, experts]), ALU.add))
                for k, hot in enumerate((fh, ch)):
                    link(dve.tensor_tensor(hot, hot, sl, ALU.mult))
                    link(dve.tensor_reduce(slot_f[:, k, :], hot, AX.X, ALU.add))
                link(dve.tensor_copy(slot_i[:], slot_f[:]))
                dve.sem_inc(S["slots_ready"], 1)
                dve.wait_ge(S["moe_bias_filled"], m + 1)
                base = x_res if m == 0 else normed
                link(dve.tensor_tensor(x_mix[:], tiles(mps[:, 0:NT * D]), base[:], ALU.add))
                dve.sem_inc(S["moe_bias_kept"], 1)
                Q = width // P // 4

                def keep_turned(turn):
                    dve.wait_ge(S["x_turned"], turn)
                    dve.tensor_copy(xT_chunk, gps[:, 0:D].rearrange("p (k n) -> p k n", k=KD)).then_inc(S["xT_kept"], 1)

                at = dve.alloc_register("dve_at%d" % m)
                dve.reg_mov(at, 0)
                dve.reg_add(turned_no, turned_no, 1)
                keep_turned(dve.snap(turned_no))
                for e in range(experts):
                    n = dve.value_load(chunk_i[0:1, e:e + 1], min_val=1, max_val=NT)
                    with dve.Fori(0, n):
                        for h in range(2):
                            dve.reg_add(halves_no, halves_no, 1)
                            dve.wait_ge(S["half_filled"], dve.snap(halves_no))
                            for q in range(Q):
                                j = (2 * h + 1) * Q + q
                                c = 1024 * h + 512 + q * P
                                ins = dve.tensor_scalar(hid_chunk[:, j, :], mps[:, c:c + P],
                                                        moe_b1[:, m, e * 4 * Q + j:e * 4 * Q + j + 1], 0.0, ALU.add, ALU.max)
                            ins.then_inc(S["half_dve"], 1)
                        dve.reg_add(turned_no, turned_no, 1)
                        keep_turned(dve.snap(turned_no))
                        dve.reg_add(chunk_no, chunk_no, 1)
                        dve.wait_ge(S["y_filled"], dve.snap(chunk_no))
                        c = dve.snap(at, min_val=0, max_val=(chunks_of(experts) - 1) * D)
                        dve.tensor_copy(y_all[m][:, bass.ds(c, D)], gps[:, 512:512 + D]).then_inc(S["y_kept"], 1)
                        dve.reg_add(at, at, D)
                for i in range(NT):
                    dve.wait_ge(S["gathered%d" % i], 32 * (m + 1))
                    n = P if i < NT - 1 else LAST
                    for k in range(2):
                        link(dve.scalar_tensor_tensor(out=x_mix[0:n, i, :], in0=picked[m][0:n, k, i, :], scalar=pair[0:n, i, 2 + k:3 + k],
                                                      in1=x_mix[0:n, i, :], op0=ALU.mult, op1=ALU.add))
                    ins = dve.bn_stats(stats[:, i, :], x_mix[:, i, :])
                link(ins)

            halves_no = dve.alloc_register("dve_half")
            turned_no = dve.alloc_register("dve_turned")
            chunk_no = dve.alloc_register("dve_chunk")
            for r in (halves_no, turned_no, chunk_no):
                dve.reg_mov(r, 0)
            moe(0, E0, H0, "bg")

            link(normalise(x_mix, xn_tok, stats_taken=True))
            dve.sem_inc(S["norm_ready"], 1)
            normT_half(normed_T[:, 0, :])

            def head_max(h):
                dve.wait_ge(S["hrow_filled"], h + 1)
                for i in range(NT):
                    ins = dve.tensor_tensor_reduce(prob[:, i, :], gps[:, 0:NP], no_edge[:, i, :], 1.0, NOEDGE * 2, ALU.add,
                                                   ALU.max, hmax[:, i, h:h + 1])
                ins.then_inc(S["hmax_done"], 1)

            dve.wait_ge(S["uv_filled"], 1)
            uv = gps[:, 0:NT * 2 * HEADS].rearrange("p (t c) -> p t c", t=NT)
            dve.tensor_tensor(su[:], uv[:, :, 0:HEADS], row("b_u", 0, HEADS)[:, None, :].broadcast_to([P, NT, HEADS]), ALU.add)
            link(dve.tensor_copy(sv[:], uv[:, :, HEADS:2 * HEADS]))
            dve.sem_inc(S["uv_ready"], 1)
            for k in range(KD):
                dve.wait_ge(S["qk_filled"], k + 1)
                dve.tensor_scalar(q_T[:, k, :], bank(2 * k), 0.0, None, ALU.min)
                ins = dve.tensor_scalar(k_exp[:, k, :], bank(2 * k), 0.0, None, ALU.max)
            link(ins)
            dve.sem_inc(S["qk_min"], 1)
            head_max(0)
            dve.wait_ge(S["qv_filled"], 2 * DEPTH + 1)
            dve.tensor_scalar(k_tok[:], tiles(mps[:, 0:NT * D]), 0.0, None, ALU.min)
            link(dve.tensor_scalar(q_tok[:], tiles(mps[:, 0:NT * D]), 0.0, None, ALU.max))
            dve.sem_inc(S["qk_min"], 1)
            dve.wait_ge(S["qk_exp"], 1)
            dve.tensor_tensor(q_T[:], q_T[:], k_exp[:], ALU.add).then_inc(S["qk_ready"], 1)
            head_max(1)
            dve.wait_ge(S["qk_exp"], 2)
            link(dve.tensor_tensor(k_tok[:], k_tok[:], q_tok[:], ALU.add))
            dve.tensor_scalar(k_tok[:][:, NT - 1, :], k_tok[:][:, NT - 1, :], v_tok[:, NT - 1, 0, P:P + 1], None,
                              ALU.mult).then_inc(S["qk_ready"], 1)
            head_max(2)
            dve.wait_ge(S["ctx_filled"], DEPTH + 1)
            for k in range(KD):
                dve.tensor_tensor(context[:, k, 0:P], mps[:, k * 256:k * 256 + P], headmask[:], ALU.mult)
                ins = dve.tensor_scalar(context[:, k, P:P + 4], headmask[:, 0:P:DH], mps[:, k * 256 + P:k * 256 + P + 1],
                                        None, ALU.mult)
            ins.then_inc(S["ctx_kept"], 1)
            head_max(3)
            dve.wait_ge(S["num_filled"], 1)
            ps = mps[:, 0:NT * 512].rearrange("p (t x) -> p t x", t=NT)
            den, inv = (a[:].rearrange("p (t k h) -> p t k h", t=NT, k=KD) for a in (tiny, tiny2))
            for k in range(KD):
                c = k * (P + 4) + P
                ins = dve.tensor_scalar(den[:, :, k, :], ps[:, :, c:c + 4], ATT_EPS, None, ALU.add)
            link(ins)
            link(dve.reciprocal(tiny2[:], tiny[:]))
            link(dve.tensor_scalar(tiny2[:], tiny2[:], float(N), None, ALU.mult))
            for k in range(KD):
                c = k * (P + 4)
                ins = dve.tensor_tensor(q_tok[:, :, k * P:(k + 1) * P].rearrange("p t (h c) -> p t h c", c=DH),
                                        ps[:, :, c:c + P].rearrange("p t (h c) -> p t h c", c=DH),
                                        inv[:, :, k, :, None].broadcast_to([P, NT, 4, DH]), ALU.mult)
            ins.then_inc(S["num_kept"], 1)
            head_max(4)
            dve.wait_ge(S["qT_filled"], 2 * DEPTH + 1)
            dve.tensor_copy(att_T[:, 0, :], bank(4)).then_inc(S["att_dve"], 1)
            head_max(5)
            dve.wait_ge(S["proj_filled"], DEPTH + 1)
            link(normalise(tiles(mps[:, 0:NT * D]), normed))
            dve.sem_inc(S["norm_ready"], 1)
            head_max(6)
            normT_half(att_T[:, 0, :], col("m_g1", 0, 0), col("m_b1", 0, 0))
            head_max(7)
            dve.wait_ge(S["hmax_done"], HEADS)
            link(dve.scalar_tensor_tensor(out=hmax[:], in0=hmax[:], scalar=NOEDGE / 2, in1=hmax[:], op0=ALU.is_gt, op1=ALU.mult))
            link(dve.tensor_tensor(hmax[:], hmax[:], sv[:], ALU.add))
            link(dve.scalar_tensor_tensor(out=hm_[:], in0=hmax[:], scalar=0.2, in1=hmax[:], op0=ALU.mult, op1=ALU.max))
            dve.tensor_tensor(hs1[:], sv[:], hm_[:], ALU.subtract)
            dve.tensor_scalar(su2[:], su[:], 0.2, None, ALU.mult)
            dve.scalar_tensor_tensor(out=hs2[:], in0=sv[:], scalar=0.2, in1=hm_[:], op0=ALU.mult, op1=ALU.subtract)\
               .then_inc(S["hshift_ready"], 1)

            def keep_head(h):
                dve.wait_ge(S["hT_filled"], h + 1)
                ps = mps[:, 1024 + 512 * (h % 2):1024 + 512 * (h % 2) + NT * (DH + 1)]
                dve.tensor_copy(head_sum[:, :, h, :], ps.rearrange("p (t c) -> p t c", t=NT)).then_inc(S["hT_kept"], 1)

            for h in range(HEADS):
                probabilities(NT * (GAT + h), head_prob[h % 2], lambda i: head_prob2[:, i, :])
                if h == 0:
                    dve.wait_ge(S["down_filled"], DEPTH + 1)
                    normalise(tiles(mps[:, 0:NT * D]), normed).then_inc(S["mix1_kept"], 1)
                if h >= 2:
                    keep_head(h - 2)
            for h in range(HEADS - 2, HEADS):
                keep_head(h)
            dve.wait_ge(S["hT_kept"], HEADS)
            link(dve.tensor_scalar(tiny[:].rearrange("p (t h) -> p t h", t=NT), head_sum[:, :, :, DH], 1e-30, None, ALU.max))
            link(dve.reciprocal(tiny2[:], tiny[:]))
            link(dve.tensor_tensor(head_sum[:, :, :, 0:DH], head_sum[:, :, :, 0:DH],
                                   tiny2[:].rearrange("p (t h) -> p t h", t=NT)[:, :, :, None].broadcast_to([P, NT, HEADS, DH]), ALU.mult))
            dve.wait_ge(S["mix1_added"], 1)
            by_head = lambda ap: ap.rearrange("p t (c h) -> p t h c", h=HEADS)
            link(dve.tensor_tensor(by_head(x_res[:]), head_sum[:, :, :, 0:DH], by_head(normed[:]), ALU.add))

            moe(1, E1, H1, "gate_b")
            norms[0] += 1
            for i in range(NT):
                ins = dve.bn_aggr(mv[:, i, :], stats[:, i, :])
            ins.then_inc(S["var_ready"], 1)
            dve.wait_ge(S["var_ready"], norms[0])
            for i in range(NT):
                ins = dve.scalar_tensor_tensor(out=normed[:, i, :], in0=x_mix[:, i, :], scalar=mv[:, i, 0:1], in1=row("gamma_out", 0),
                                               op0=ALU.subtract, op1=ALU.mult)
            link(ins)
            dve.wait_ge(S["x_beta_ready"], 1)
            dve.wait_ge(S["rstd_ready"], norms[0])
            for i in range(NT):
                dve.scalar_tensor_tensor(out=normed[:, i, :], in0=normed[:, i, :], scalar=rstd[:, i:i + 1], in1=x_res[:, i, :],
                                         op0=ALU.mult, op1=ALU.add).then_inc(S["out_ready"], 1)

        @block.tensor
        def _(pe):
            turns = [0]

            def product(out, pairs):
                ins = None
                width = out.shape[-1]
                for c in range(0, width, 512):
                    w = min(512, width - c)
                    for n, (lhsT, rhs) in enumerate(pairs):
                        ins = pe.matmul(out[:, c:c + w], lhsT, rhs[:, c:c + w], start=(n == 0), stop=(n == len(pairs) - 1))
                return ins

            def turn(src, k, out):
                for i in range(NT):
                    ins = pe.transpose(out[:, i * P:(i + 1) * P], src[:, i, k * P:(k + 1) * P], ident[:])
                return ins

            def turn_norm(src):
                turns[0] += 1
                n = turns[0]
                pe.wait_ge(S["norm_ready"], n)
                if n > 1:
                    pe.wait_ge(S["normT_dve"], n - 1)
                    pe.wait_ge(S["normT_act"], n - 1)
                turn(src, 0, bank(4)).then_inc(S["normT_filled"], 1)
                turn(src, 1, bank(2)).then_inc(S["normT_filled"], 1)

            def norm_turned():
                pe.wait_ge(S["normT_dve"], turns[0])
                pe.wait_ge(S["normT_act"], turns[0])

            def part(src, k, i):
                return src[:, k, i * P:(i + 1) * P]

            def spread(column, out):
                for i in range(NT):
                    ins = pe.matmul(out[:, i * P:(i + 1) * P], column(i).broadcast_to([P, P]), ident[:], start=True, stop=True)
                return ins

            pe.wait_ge(S["consts_ready"], 1)
            pe.wait_ge(S["in_block_ready"], 1)
            blocks = in_block.rearrange("p b t -> p (b t)")
            for h in range(2):
                c = NT * ET // 2
                ins = pe.matmul(gps[0:1, 512 * h:512 * h + c], ones[0:EP, 0:1], blocks[:, h * c:(h + 1) * c], start=True, stop=True)
            ins.then_inc(S["block_counts"], 1)
            pe.wait_ge(S["span_ready"], 1)
            pe.sem_inc(S["hot_free"], 2)

            turn_no = pe.alloc_register("pe_hot_turn")
            pe.reg_mov(turn_no, 0)
            for b in range(NT):
                first = pe.value_load(span_i[0:1, 0, b:b + 1], min_val=0, max_val=EGN - 1)
                last = pe.value_load(span_i[0:1, 1, b:b + 1], min_val=1, max_val=EGN)
                if b >= 2:
                    pe.wait_ge(S["count_kept"], b - 1)
                out = bank(2 * (b % 2))
                for c, w in ((0, 512), (512, P)):
                    pe.matmul(out[:, c:c + w], zero_b[:, 0:P], zero_b[:, 0:w], start=True, stop=False, skip_group_check=True)
                with pe.Fori(first, last) as g:
                    for u in range(2):
                        pe.reg_add(turn_no, turn_no, 1)
                        pe.wait_ge(S["hot_ready"], pe.snap(turn_no))
                        for s in range(EG // 2):
                            for c, w in ((0, 512), (512, P)):
                                ins = pe.matmul(out[:, c:c + w], hot_dst[:, u, s, :], hot_src[:, u, s, c:c + w],
                                                start=False, stop=False, skip_group_check=True)
                        ins.then_inc(S["hot_free"], 1)
                for c, w in ((0, 512), (512, P)):
                    ins = pe.matmul(out[:, c:c + w], zero_b[:, 0:P], zero_b[:, 0:w], start=False, stop=True, skip_group_check=True)
                ins.then_inc(S["count_filled"], 1)
            pe.wait_ge(S["count_kept"], NT)
            for l in range(NT):
                if l >= 2:
                    pe.wait_ge(S["countT_kept"], l - 1)
                for b in range(NT):
                    ins = pe.transpose(mps[:, 1024 * (l % 2) + b * P:1024 * (l % 2) + (b + 1) * P],
                                       count_dst[:, b, l * P:(l + 1) * P], ident[:])
                ins.then_inc(S["countT_filled"], 1)
            pe.wait_ge(S["countT_kept"], NT)
            turn_norm(x_mix)
            norm_turned()
            pe.wait_ge(S["gatw_ready"], 1)

            def gat_scores(l):
                if l > 0:
                    pe.wait_ge(S["gatin_ready"], KD * l)
                for i in range(NT):
                    if i >= 2:
                        pe.wait_ge(S["h_kept"], NT * l + i - 1)
                    c = (i % 2) * 512
                    product(gps[:, c:c + D + 2], [(part(gat_in, k, i), gat_w[:, l, k, :]) for k in range(KD)])\
                        .then_inc(S["h_filled"], 1)
                pe.wait_ge(S["h_kept"], NT * (l + 1))
                spread(lambda i: score[:, i, 0:1], gps[:, 0:NP]).then_inc(S["srow_filled"], 1)
                pe.wait_ge(S["shift_ready"], l + 1)
                for n in range(2):
                    if n:
                        pe.wait_ge(S["r_kept"], 2 * l + 1)
                    spread(lambda i: shift[:, n, i:i + 1], gps[:, 0:NP]).then_inc(S["r_filled"], 1)

            def gat_sum(l):
                pe.wait_ge(S["r_kept"], 2 * l + 2)
                pe.wait_ge(S["prob_ready"], NT * (l + 1))
                for i in range(NT):
                    if i >= 2:
                        pe.wait_ge(S["agg_kept"], NT * l + i - 1)
                    c = (i % 2) * 512
                    product(gps[:, c:c + D + 1], [(part(prob, s, i), gat_h[:, s, :]) for s in range(NT)])\
                        .then_inc(S["agg_filled"], 1)
                if l < GAT - 1:
                    pe.wait_ge(S["agg_kept"], NT * (l + 1))
                    for k in range(KD):
                        if k:
                            pe.wait_ge(S["gatT_kept"], KD * l + 1)
                        turn(gat_out, k, gps[:, 0:NP]).then_inc(S["gatT_filled"], 1)

            def weight(w, n):
                return w[:, n * KD * D:(n + 1) * KD * D].rearrange("p (k d) -> p k d", k=KD)

            def tokens_by(src, w, c0):
                for i in range(NT):
                    ins = product(mps[:, c0 + i * D:c0 + (i + 1) * D], [(part(src, k, i), w[:, k, :]) for k in range(KD)])
                return ins

            def up(u0, tiles_, srcs, w):
                for j in range(tiles_):
                    u = u0 + j
                    if u >= 2:
                        pe.wait_ge(S["up_kept"], u - 1)
                    product(bank(2 * (u % 2)), [(w[:, k, j * P:(j + 1) * P], src) for k, src in enumerate(srcs)])\
                        .then_inc(S["up_filled"], 1)

            for i in range(DEPTH):
                turn_norm(normed)
                norm_turned()
                pe.wait_ge(S["mixw_loaded"], 16 * (i + 1))
                w = mix_w
                tokens_by(normed_T, weight(w, 0), 0).then_inc(S["qv_filled"], 1)
                tokens_by(normed_T, weight(w, 2), 3 * 512).then_inc(S["qv_filled"], 1)
                for m in range(KD):
                    pe.wait_ge(S["q_shifted" if m == 0 else "v_kept"], i + 1)
                    product(bank(2 * m), [(weight(w, 1)[:, k, m * P:(m + 1) * P], normed_T[:, k, :]) for k in range(KD)])\
                        .then_inc(S["k_filled"], 1)
                if i < GAT:
                    gat_scores(i)
                pe.wait_ge(S["q_normed"], i + 1)
                turn(q_tok, 0, bank(4)).then_inc(S["qT_filled"], 1)
                pe.wait_ge(S["k_exped"], KD * i + 1)
                turn(q_tok, 1, bank(0)).then_inc(S["qT_filled"], 1)
                pe.wait_ge(S["k_exped"], KD * i + 2)
                for m, b in ((0, 2), (1, 4)):
                    if m:
                        pe.wait_ge(S["qT_dve"], i + 1)
                    for j in range(NT):
                        ins = pe.transpose(mps[:, b * 512 + j * P:b * 512 + (j + 1) * P], part(k_exp, m, j), ident[:])
                    ins.then_inc(S["kT_filled"], 1)
                pe.wait_ge(S["qT_act"], i + 1)
                pe.wait_ge(S["kT_dve"], i + 1)
                pe.wait_ge(S["kT_act"], i + 1)
                for m in range(KD):
                    ins = product(mps[:, m * 256:m * 256 + P],
                                  [(k_tok[:, j, m * P:(m + 1) * P], v_tok[:, j, m, 0:P]) for j in range(NT)])
                ins.then_inc(S["ctx_filled"], 1)
                pe.wait_ge(S["ctx_kept"], i + 1)
                for m, b in ((0, 2), (1, 4)):
                    product(bank(b), [(context[:, m, 0:P], q_T[:, m, :])]).then_inc(S["att_filled"], 1)
                pe.wait_ge(S["att_dve"], i + 1)
                pe.wait_ge(S["att_act"], i + 1)
                tokens_by(att_T, weight(w, 3), 0).then_inc(S["proj_filled"], 1)
                turn_norm(normed)
                norm_turned()
                pe.wait_ge(S["ffw_loaded%d" % (i % 2)], 32 * (i // 2 + 1))
                up(8 * i, FF // P, [normed_T[:, k, :] for k in range(KD)], expert_up(FF, i % 2))
                if i < GAT:
                    gat_sum(i)
                pe.wait_ge(S["up_kept"], 8 * (i + 1))
                wd = expert_down(FF, i % 2)
                for j in range(NT):
                    ins = product(mps[:, j * D:(j + 1) * D], [(part(hidden, h, j), wd[:, h, :]) for h in range(FF // P)])
                ins.then_inc(S["down_filled"], 1)

            def moe(m, experts, width):
                turn_norm(normed)
                norm_turned()
                if m == 0:
                    pe.wait_ge(S["agg_kept"], NT * GAT)
                else:
                    pe.wait_ge(S["hT_kept"], HEADS)
                pe.wait_ge(S["small_loaded"], 16 * 5)
                w = gate_w[:, :, 0:E0] if m == 0 else gate_w[:, :, E0:E0 + E1]
                for i in range(NT):
                    ins = product(gps[:, i * experts:(i + 1) * experts], [(part(normed_T, k, i), w[:, k, :]) for k in range(KD)])
                ins.then_inc(S["gate_filled"], 1)
                pe.wait_ge(S["chosen_ready"], m + 1)
                pe.matmul(gps[:, 0:NT * experts], below[:], both[:, :, 0:experts],
                          start=True, stop=True)
                pe.matmul(gps[:, 512:512 + NT * experts], ones[:], both[:, :, 0:experts], start=True, stop=True)\
                    .then_inc(S["ranks_filled"], 1)
                pe.wait_ge(S["comb_ready"], m + 1)
                for i in range(NT):
                    ins = pe.transpose(mps[0:experts, 3 * 512 + i * P:3 * 512 + (i + 1) * P], comb[:, i, 0:experts], ident[:])
                ins.then_inc(S["combT_filled"], 1)
                pe.wait_ge(S["combT_kept"], m + 1)
                for i in range(NT):
                    ins = pe.matmul(mps[:, i * D:(i + 1) * D], comb_T[0:experts, i * P:(i + 1) * P], moe_b2[0:experts, m, :],
                                    start=True, stop=True)
                ins.then_inc(S["moe_bias_filled"], 1)
                pe.wait_ge(S["moe_bias_kept"], m + 1)
                J = width // P
                Q = J // 4

                def turn_chunk(n):
                    pe.wait_ge(S["x_copied"], n)
                    for k in range(KD):
                        ins = pe.transpose(gps[:, k * P:(k + 1) * P], x_chunk[:, k * P:(k + 1) * P], ident[:])
                    ins.then_inc(S["x_turned"], 1)

                pe.reg_add(copied_no, copied_no, 1)
                turn_chunk(pe.snap(copied_no))
                pe.reg_add(kept_no, kept_no, 1)
                for e in range(experts):
                    if m == 0:
                        r, u = DEPTH + e, (DEPTH + e) % 2
                        pe.wait_ge(S["ffw_loaded%d" % u], 32 * (r // 2 + 1))
                    else:
                        u = e % 4
                        pe.wait_ge(S["expert_loaded%d" % u], 32 * (e // 4 + 1))
                    wu, wd = expert_up(width, u), expert_down(width, u)
                    n = pe.value_load(chunk_i[0:1, e:e + 1], min_val=1, max_val=NT)
                    with pe.Fori(0, n):
                        pe.wait_ge(S["xT_kept"], pe.snap(kept_no))
                        for h in range(2):
                            pe.reg_add(free_no, free_no, 1)
                            free = pe.snap(free_no)
                            pe.wait_ge(S["half_act"], free)
                            pe.wait_ge(S["half_dve"], free)
                            for q in range(2 * Q):
                                c = 1024 * h + 512 * (q // Q) + (q % Q) * P
                                ins = product(mps[:, c:c + P], [(wu[:, k, (2 * h * Q + q) * P:(2 * h * Q + q + 1) * P], xT_chunk[:, k, :])
                                                                for k in range(KD)])
                            ins.then_inc(S["half_filled"], 1)
                        pe.reg_add(copied_no, copied_no, 1)
                        turn_chunk(pe.snap(copied_no))
                        pe.reg_add(kept_no, kept_no, 1)
                        both_no = pe.snap(free_no) + 2
                        pe.wait_ge(S["half_act"], both_no)
                        pe.wait_ge(S["half_dve"], both_no)
                        product(gps[:, 512:512 + D], [(hid_chunk[:, j, :], wd[:, j, :]) for j in range(J)])\
                            .then_inc(S["y_filled"], 1)

            copied_no = pe.alloc_register("pe_copied")
            kept_no = pe.alloc_register("pe_kept")
            free_no = pe.alloc_register("pe_free")
            pe.sem_inc(S["half_act"], 2)
            pe.sem_inc(S["half_dve"], 2)
            for r in (copied_no, kept_no, free_no):
                pe.reg_mov(r, 0)
            moe(0, E0, H0)

            turn_norm(xn_tok)
            norm_turned()
            pe.wait_ge(S["mixw_loaded"], 16 * (DEPTH + 1))
            w = mix_w
            for i in range(NT):
                ins = product(gps[:, i * 16:(i + 1) * 16], [(part(normed_T, k, i), uv_w[:, k, :]) for k in range(KD)])
            ins.then_inc(S["uv_filled"], 1)

            def head_row(h):
                if h == 0:
                    pe.wait_ge(S["uv_ready"], 1)
                else:
                    pe.wait_ge(S["hmax_done"], h)
                spread(lambda i: su[:, i, h:h + 1], gps[:, 0:NP]).then_inc(S["hrow_filled"], 1)

            for m in range(KD):
                product(bank(2 * m), [(weight(w, 0)[:, k, m * P:(m + 1) * P], normed_T[:, k, :]) for k in range(KD)])\
                    .then_inc(S["qk_filled"], 1)
            head_row(0)
            pe.wait_ge(S["qk_min"], 1)
            tokens_by(normed_T, weight(w, 1), 0).then_inc(S["qv_filled"], 1)
            tokens_by(normed_T, weight(w, 2), 3 * 512).then_inc(S["qv_filled"], 1)
            head_row(1)
            head_row(2)
            pe.wait_ge(S["qk_ready"], 2)
            pe.wait_ge(S["v_kept"], DEPTH + 1)
            for m in range(KD):
                ins = product(mps[:, m * 256:m * 256 + P + 1],
                              [(k_tok[:, j, m * P:(m + 1) * P], v_tok[:, j, m, :]) for j in range(NT)])
            ins.then_inc(S["ctx_filled"], 1)
            head_row(3)
            pe.wait_ge(S["ctx_kept"], DEPTH + 1)
            for i in range(NT):
                for m in range(KD):
                    c = i * 512 + m * (P + 4)
                    ins = product(mps[:, c:c + P + 4], [(part(q_T, m, i), context[:, m, :])])
            ins.then_inc(S["num_filled"], 1)
            head_row(4)
            pe.wait_ge(S["num_kept"], 1)
            turn(q_tok, 0, bank(4)).then_inc(S["qT_filled"], 1)
            turn(q_tok, 1, bank(2)).then_inc(S["qT_filled"], 1)
            head_row(5)
            pe.wait_ge(S["att_dve"], DEPTH + 1)
            pe.wait_ge(S["att_act"], DEPTH + 1)
            tokens_by(att_T, weight(w, 3), 0).then_inc(S["proj_filled"], 1)
            head_row(6)
            turn_norm(normed)
            head_row(7)
            norm_turned()
            pe.wait_ge(S["ffw_loaded0"], 32 * ((DEPTH + E0) // 2 + 1))
            w1 = ff_w1[:, 0, :].rearrange("p (k h) -> p k h", k=4)
            w2 = ff_w2[:, 0, 0:4 * D].rearrange("p (k d) -> p k d", k=4)

            def head_shifts(h):
                pe.wait_ge(S["hr1_used"], h) if h else pe.wait_ge(S["hshift_ready"], 1)
                spread(lambda i: hs1[:, i, h:h + 1], gps[:, 0:NP]).then_inc(S["hr1_filled"], 1)
                if h:
                    pe.wait_ge(S["exp_ready"], NT * (GAT + h))
                spread(lambda i: hs2[:, i, h:h + 1], bank(4)).then_inc(S["hr2_filled"], 1)

            def head_aggregate(h):
                if h == 0:
                    pe.wait_ge(S["mix1_kept"], 1)
                else:
                    pe.wait_ge(S["hagg_kept"], h)
                for s in range(NT):
                    pe.wait_ge(S["prob_ready"], NT * (GAT + h) + s + 1)
                    for c, n in ((0, 512), (512, P)):
                        ins = pe.matmul(mps[0:DH + 1, c:c + n], xh[:, s, h, :], head_prob[h % 2][:, s, c:c + n],
                                        start=(s == 0), stop=(s == NT - 1))
                ins.then_inc(S["hagg_filled"], 1)

            def head_turn(h):
                pe.wait_ge(S["hagg_kept"], h + 1)
                if h >= 2:
                    pe.wait_ge(S["hT_kept"], h - 1)
                for i in range(NT):
                    c = 1024 + 512 * (h % 2) + i * (DH + 1)
                    ins = pe.transpose(mps[:, c:c + DH + 1], head_T[:, i * P:(i + 1) * P], ident[0:DH + 1, 0:DH + 1])
                ins.then_inc(S["hT_filled"], 1)

            u0 = DEPTH * 8
            srcs = [normed_T[:, 0, :], normed_T[:, 1, :], att_T[:, 0, :], att_T[:, 1, :]]
            up(u0, 2, srcs, w1)
            head_shifts(0)
            up(u0 + 2, 2, srcs, w1[:, :, 2 * P:])
            pe.wait_ge(S["up_kept"], u0 + 4)
            for j in range(NT):
                ins = product(mps[:, j * D:(j + 1) * D], [(part(hidden2, h, j), w2[:, h, :]) for h in range(4)])
            ins.then_inc(S["down_filled"], 1)
            pe.wait_ge(S["xh_ready"], 1)
            for h in range(HEADS):
                if h + 1 < HEADS:
                    head_shifts(h + 1)
                if h:
                    head_turn(h - 1)
                head_aggregate(h)
            head_turn(HEADS - 1)
            moe(1, E1, H1)


def kernel(**inputs):
    import numpy as np
    import concourse.bacc as bacc
    from concourse.bass_utils import run_bass_kernel_spmd as run

    a = {k: np.asarray(v) for k, v in inputs.items()}

    def halves(w):
        *lead, r, c = w.shape
        w = w.reshape(*lead, r // P, P, c)
        return np.ascontiguousarray(np.swapaxes(w, -3, -2)).reshape(*lead, P, r // P * c)

    def column(v):
        return v.reshape(-1, P).T

    arrays = {"x": a["x"], "src": a["src"].reshape(ET, EP).T, "dst": a["dst"].reshape(ET, EP).T}
    cols = np.zeros((P, NCOL), np.float32)
    names = {"gat_b": "L0_gnn_b%d", "gamma": "L0_gnn_gamma%d", "beta": "L0_gnn_beta%d"}
    stacked = {"ln1_g": "L0_mix_ln1_g", "ln1_b": "L0_mix_ln1_b", "ln2_g": "L0_mix_ln2_g", "ln2_b": "L0_mix_ln2_b",
               "ff_b1": "L0_mix_b1"}
    for (n, l), c in COLS.items():
        if n in names:
            v = a[names[n] % l]
        elif n in stacked:
            v = a[stacked[n]][l]
        else:
            v = a["L1_mix_" + n[2:]]
        cols[:, c:c + v.size // P] = column(v)
    arrays["cols"] = cols
    rows = np.zeros((1, NROW), np.float32)
    plain = {"gat_b2": "L0_gnn_b2", "bg": "L0_ffn_bg", "b_u": "L1_gnn_b_u", "m_g2": "L1_mix_g2", "m_b2": "L1_mix_b2",
             "gate_b": "L1_ffn_gate_b", "gamma_out": "L1_ffn_gamma", "beta_out": "L1_ffn_beta"}
    for (n, l), c in ROWS.items():
        if n in ("bo", "ff_b2"):
            v = a["L0_mix_" + n[-2:]][l]
        else:
            v = a[plain[n]]
        rows[0, c:c + v.size] = v
    arrays["rows"] = rows
    arrays["gat_w"] = np.stack([halves(a["L0_gnn_W%d" % l]).reshape(P, KD, D) for l in range(GAT)], 1)
    arrays["mix_w"] = np.concatenate([halves(a["L0_mix_" + n]) for n in ("Wq", "Wk", "Wv", "Wo")], -1)
    arrays["ff_w1"], arrays["ff_w2"] = halves(a["L0_mix_W1"]), halves(a["L0_mix_W2"])
    arrays["moe0_w1"] = halves(a["L0_ffn_W1"].transpose(0, 2, 1))
    arrays["moe0_w2"] = halves(a["L0_ffn_W2"].transpose(0, 2, 1))
    arrays["moe1_w1"], arrays["moe1_w2"] = halves(a["L1_ffn_w1"]), halves(a["L1_ffn_w2"])
    arrays["moe0_b2"], arrays["moe1_b2"] = a["L0_ffn_b2"], a["L1_ffn_b2"]
    arrays["moe_b1"] = np.stack([column(a["L0_ffn_b1"].reshape(-1)), column(a["L1_ffn_b1"].reshape(-1))], 1)
    arrays["gate_w"] = np.concatenate([halves(a["L0_ffn_Wg"].T).reshape(P, KD, E0), halves(a["L1_ffn_gate_w"]).reshape(P, KD, E1)], -1)
    arrays["uv_w"] = np.concatenate([halves(a["L1_gnn_W_u"].T).reshape(P, KD, HEADS), halves(a["L1_gnn_W_v"].T).reshape(P, KD, HEADS)], -1)
    arrays["mix1_qkvm"] = np.concatenate([halves(a["L1_mix_" + n]) for n in ("Wq", "Wk", "Wv", "Wm")], -1)
    arrays["mix1_w1"] = halves(a["L1_mix_W1"])
    arrays["mix1_w2"] = halves(a["L1_mix_W2"])
    arrays["a_rows"] = np.concatenate([a["L0_gnn_a_%s%d" % (n, l)] for l in range(GAT) for n in ("src", "dst")])[None, :]

    nc = bacc.Bacc("TRN2", target_bir_lowering=False, num_devices=1)
    t, feed = {}, {}
    for name, v in arrays.items():
        v = np.ascontiguousarray(v)
        feed["in_" + name] = v
        t[name] = nc.dram_tensor("in_" + name, v.shape, mybir.dt.from_np(v.dtype), kind="ExternalInput").ap()
    t["out"] = nc.dram_tensor("out", (N, D), F32, kind="ExternalOutput").ap()
    build(nc, t)
    r = run(nc, [feed], core_ids=[0])
    return r.results[0]["out"]
```

```python
from contextlib import ExitStack

import concourse.bass as bass
from concourse import mybir

F32 = mybir.dt.float32
BF16 = mybir.dt.bfloat16
F16 = mybir.dt.float16
I32 = mybir.dt.int32
U32 = mybir.dt.uint32
ALU = mybir.AluOpType
ACT = mybir.ActivationFunctionType
AX = mybir.AxisListType

P = 128
N = 625
NT = 5
NP = NT * P
LAST = N - (NT - 1) * P
D = 256
KD = D // P
EDGES = 20000
EP = 125
ET = EDGES // EP
EG = 4
EGN = ET // EG
GAT = 3
DEPTH = 4
HEADS = 8
DH = D // HEADS
FF = 1024
E0, H0 = 8, 1024
E1, H1 = 16, 512
EPS = 1e-5
QK_SCALE = float(DH) ** -0.25
NOEDGE = -1.0e30
ATT_EPS = 1e-6
BANKS = -(-NT * D // 512)
HEAD = NT + 1


def chunks_of(experts):
    return (2 * N - experts) // P + experts


CHUNKS = max(chunks_of(E0), chunks_of(E1))

COLS = {}
_at = 0
for _l in range(GAT):
    COLS["gat_b", _l] = _at; _at += KD
for _l in range(GAT - 1):
    COLS["gamma", _l] = _at; _at += KD
    COLS["beta", _l] = _at; _at += KD
for _l in range(DEPTH):
    for _n in ("ln1_g", "ln1_b", "ln2_g", "ln2_b"):
        COLS[_n, _l] = _at; _at += KD
    COLS["ff_b1", _l] = _at; _at += FF // P
COLS["m_g1", 0] = _at; _at += KD
COLS["m_b1", 0] = _at; _at += KD
NCOL = _at
ROWS = {}
_at = 0
for _l in range(DEPTH):
    ROWS["bo", _l] = _at; _at += D
    ROWS["ff_b2", _l] = _at; _at += D
for _n, _k in (("gat_b2", D), ("bg", E0), ("b_u", HEADS), ("m_g2", D), ("m_b2", D), ("gate_b", E1),
               ("gamma_out", D), ("beta_out", D)):
    ROWS[_n, 0] = _at; _at += _k
NROW = _at


def build(nc, t):
    ctx = ExitStack()
    with ctx:
        def sb(name, shape, dt=F32):
            return ctx.enter_context(nc.sbuf_tensor(name, shape, dt))

        def sem(name):
            return ctx.enter_context(nc.semaphore(name))

        ident = sb("ident", [P, P])
        ones = sb("ones", [P, P])
        iota = sb("iota", [P, NP], F16)
        iota_f = sb("iota_f", [P, E1])
        headmask = sb("headmask", [P, P])
        minus_half = sb("minus_half", [P, 16])
        cols = sb("cols", [P, NCOL])
        rows = sb("rows", [P, NROW])
        x_res = sb("x_res", [P, NT, D])
        x_mix = sb("x_mix", [P, NT, D])
        x_bias = sb("x_bias", [P, NT, D])
        normed = sb("normed", [P, NT, D])
        normed_T = sb("normed_T", [P, KD, NP])
        stats = sb("stats", [P, NT, 6])
        mv = sb("mv", [P, NT, 2])
        var_eps = sb("var_eps", [P, NT])
        rstd = sb("rstd", [P, NT])
        edge_i = sb("edge_i", [EP, 2, ET], I32)
        edge_f = sb("edge_f", [EP, 2, ET])
        present = sb("present", [1, NT * EGN])
        span_f = sb("span_f", [1, 2, NT])
        span_g = sb("span_g", [1, 1, NT])
        marked = sb("marked", [1, NT * EGN])
        group_f = sb("group_f", [1, EGN])
        group_r = sb("group_r", [1, EGN])
        zero_b = sb("zero_b", [EP, 512], BF16)
        span_i = sb("span_i", [1, 2, NT], I32)
        graph = sb("graph", [P, 2, NT, NP])
        count_src = graph[:, 0]
        no_edge = graph[:, 1]
        gat_w = sb("gat_w", [P, GAT, KD, D + 2])
        gat_in = sb("gat_in", [P, KD, NP])
        gat_h = sb("gat_h", [P, NT, D + 1])
        score = sb("score", [P, NT, 2])
        gat_out = sb("gat_out", [P, NT, D + 1])
        score_max = sb("score_max", [P, NT])
        shift = sb("shift", [P, 2, NT])
        score2 = sb("score2", [P, NT])
        tiny = sb("tiny", [P, 8 * NT])
        tiny2 = sb("tiny2", [P, 8 * NT])
        row1 = sb("row1", [P, NP])
        arena = sb("arena", [P, NT + 2 + FF // P, NP])
        prob = arena[:, 0:NT, :]
        prob2 = arena[:, NT:NT + 2, :]
        bn_st = sb("bn_st", [P, KD, 2, 6])
        bn_mv = sb("bn_mv", [P, KD, 2])
        bn_rstd = sb("bn_rstd", [P, KD])
        bn_eps = sb("bn_eps", [P, KD])
        bn_scale = sb("bn_scale", [P, KD])
        bn_shift = sb("bn_shift", [P, KD])
        WQKVO = KD * D
        mix_w = sb("mix_w", [P, 4 * WQKVO])
        ff_w1 = sb("ff_w1", [P, 2, KD * FF])
        ff_w2 = sb("ff_w2", [P, 2, KD * FF])
        q_max = sb("q_max", [P, NT * HEADS])
        v_tok = sb("v_tok", [P, NT, KD, P + 1])
        k_exp = sb("k_exp", [P, KD, NP])
        q_T = sb("q_T", [P, KD, NP])
        k_max = sb("k_max", [P, KD])
        k_top = sb("k_top", [P, KD])
        k_inv = sb("k_inv", [P, KD])
        q_inv = sb("q_inv", [P, NT * HEADS])
        k_sum = sb("k_sum", [P, KD])
        context = sb("context", [P, KD, P + 4])
        att_T = sb("att_T", [P, KD, NP])
        hidden = arena[:, NT + 2:, :]
        gate_w = sb("gate_w", [P, KD, E0 + E1])
        gates = sb("gates", [P, NT, E1])
        top = sb("top", [P, NT, 8])
        top_i = sb("top_i", [P, NT, 8], U32)
        top_f = sb("top_f", [P, NT, 8])
        pair = sb("pair", [P, NT, 4])
        comb = sb("comb", [P, NT, E1])
        first_hot = sb("first_hot", [P, NT, E1])
        chosen = sb("chosen", [P, NT, E1])
        both = sb("both", [P, NT, E1])
        before = sb("before", [P, NT, E1])
        tokens_n = sb("tokens_n", [P, E1])
        chunk_ends = sb("chunk_ends", [P, NT - 1])
        exceeds = sb("exceeds", [P, E1, NT - 1])
        chunk_n = sb("chunk_n", [P, E1])
        scan_a = sb("scan_a", [P, E1])
        scan_b = sb("scan_b", [P, E1])
        chunk_i = sb("chunk_i", [P, E1], I32)
        slot = sb("slot", [P, NT, E1])
        slot_f = sb("slot_f", [P, 2, NT])
        slot_i = sb("slot_i", [P, 2, NT], I32)
        below = sb("below", [P, P])
        moe_b2 = sb("moe_b2", [E1, 2, D])
        moe_b1 = sb("moe_b1", [P, 2, 64])
        uv_w = sb("uv_w", [P, KD, 2 * HEADS])
        su = sb("su", [P, NT, HEADS])
        su2 = sb("su2", [P, NT, HEADS])
        sv = sb("sv", [P, NT, HEADS])
        hmax = sb("hmax", [P, NT, HEADS])
        hm_ = sb("hm_", [P, NT, HEADS])
        hs1 = sb("hs1", [P, NT, HEADS])
        hs2 = sb("hs2", [P, NT, HEADS])
        flat = lambda ap: ap.rearrange("p a b -> p (a b)")
        count_dst = prob[:]
        a_rows = flat(hidden[:, NT:, :])[:, 0:GAT * 2 * D]
        count_room = flat(count_src)[0:EP]
        in_block = count_room[:, 0:NT * ET].rearrange("p (b t) -> p b t", b=NT)
        hot_src, hot_dst = (count_room[:, c:c + EG * n // 2].bitcast(BF16).rearrange("p (s n) -> p s n", s=EG)
                            for c, n in ((NT * ET, NP), (NT * ET + EG * NP // 2, P)))
        unused = [k_exp[:, 0, 0:N], k_exp[:, 1, 0:N], q_T[:, 0, 0:N], q_T[:, 1, 0:N], row1[:, 0:N]]
        squares = count_room[:, NT * ET + EG * (NP + P) // 2:][:, 0:P].bitcast(BF16).rearrange("p (u n) -> p u n", u=2)
        minus_dst = count_room[:, NT * ET + EG * (NP + P) // 2 + P:][:, 0:ET]
        gat_pre = prob[:, 0:KD, :]
        xn_tok = gat_out[:, :, 0:D]
        zero_x = prob2[:, 0, 0:D]
        q_tok = normed
        k_tok = flat(att_T[:]).rearrange("p (t d) -> p t d", t=NT)
        comb_T = row1
        head_T = k_exp[0:DH + 1, 0, :]
        x_chunk = flat(q_T[:])[:, 0:D]
        xT_chunk = flat(q_T[:])[:, D:2 * D].rearrange("p (k n) -> p k n", k=KD)
        hid_chunk = flat(att_T[:])[:, 0:FF].rearrange("p (j n) -> p j n", n=P)
        x_all = [flat(hidden[:]), flat(graph[:].rearrange("p a b c -> p (a b) c"))]
        y_all = [flat(arena[:]), flat(arena[:])]
        picked = [a[:, 0:2 * NT * D].rearrange("p (s t d) -> p s t d", s=2, t=NT) for a in x_all]
        head_prob = [arena[:, 0:NT, :], arena[:, NT:2 * NT, :]]
        head_prob2 = arena[:, 2 * NT:3 * NT, :]
        hidden2 = arena[:, NT:NT + 4, :]
        heads = lambda ap: ap[:, 0:NT * HEADS * (DH + 1)].rearrange("p (t h c) -> p t h c", t=NT, h=HEADS)
        xh = heads(gat_w[:].rearrange("p l k d -> p (l k d)"))
        head_sum = heads(mix_w)
        mps = ctx.enter_context(nc.psum_tensor("mps", [P, 6 * 512], F32))
        gps = ctx.enter_context(nc.psum_tensor("gps", [P, 2 * 512], F32))

        def bank(b, n=NP):
            return mps[:, b * 512:b * 512 + n]

        def bank_tiles(p):
            return range(2 * p, min(2 * p + 2, NT))

        def count_bank(l):
            return gps[:, 0:NP] if l % 2 == 0 else bank(4)

        def col(name, l, k):
            c = COLS[name, l] + k
            return cols[:, c:c + 1]

        def row(name, l, n=D):
            return rows[:, ROWS[name, l]:ROWS[name, l] + n]

        def tiles(ap):
            return ap.rearrange("p (t c) -> p t c", t=NT)

        def halves(ap):
            return ap.rearrange("p (t k c) -> p t k c", t=NT, k=KD)

        def expert_up(h, u):
            c = u // 2 * KD * h
            return ff_w1[:, u % 2, c:c + KD * h].rearrange("p (k h) -> p k h", k=KD)

        def expert_down(h, u):
            c = u // 2 * KD * h
            return ff_w2[:, u % 2, c:c + h // P * D].rearrange("p (j d) -> p j d", j=h // P)

        LAYER2_NORM = 2 * DEPTH + 3

        xs = nc.dram_tensor("expert_in", (CHUNKS * P, D), F32, kind="Internal").ap()
        ys = nc.dram_tensor("expert_out", (CHUNKS * P, D), F32, kind="Internal").ap()

        names = ("x_loaded xpad_zero consts_ready cols_loaded rows_loaded edges_loaded gatw_loaded mixw_loaded "
                 "arows_loaded ffw_loaded0 ffw_loaded1 small_loaded var_ready rstd_ready norm_ready normT_filled "
                 "normT_dve normT_act in_block_ready block_counts span_ready hot_ready squared hot_act "
                 "hot_free count_filled count_kept countT_filled countT_kept gatw_ready "
                 "h_filled h_kept srow_filled max_done shift_ready r1_filled r2_filled exp_ready agg_copied "
                 "prob_ready agg_filled agg_kept gatT_filled gatT_kept bnvar_ready bnrstd_ready bn_ready gatin_ready "
                 "qv_filled q_shifted q_exped q_normed v_kept k_filled kmax_ready k_exped qT_filled qT_dve qT_act "
                 "kT_filled kT_dve kT_act ctx_filled ctx_kept att_filled att_dve att_act proj_filled xbias_ready "
                 "x_updated up_filled up_kept down_filled gate_filled gdiff_ready gexp_ready "
                 "comb_ready combT_filled combT_kept moe_bias_filled out_ready dve_step act_step pool_step "
                 "uv_filled uv_ready hrow_filled hmax_done hshift_ready hr1_filled hr2_filled hr1_used xh_ready prob2_taken "
                 "down_kept mix1_normed mix1_added hagg_filled hagg_kept hT_filled hT_kept qk_min qk_exp qk_ready qk_filled num_filled "
                 "num_kept moe_bias_kept "
                 "chosen_ready ranks_filled slots_ready scattered x_first_loaded x_head_loaded x_rest_loaded x_copied x_turned xT_kept "
                 "half_filled "
                 "half_act half_dve y_filled y_kept slots_written expert_done "
                 "expert_loaded0 expert_loaded1 expert_loaded2 expert_loaded3 x_beta_ready "
                 "gathered0 gathered1 gathered2 gathered3 gathered4 stored").split()
        S = {n: sem("s_" + n) for n in names}

        block = ctx.enter_context(nc.Block())

        @block.sync
        def _(sp):
            sp.wait_ge(S["xpad_zero"], 1)
            sp.dma_start(x_res[:, 0:NT - 1, :], t["x"][0:(NT - 1) * P].rearrange("(t p) d -> p t d", p=P)).then_inc(S["x_loaded"], 16)
            sp.dma_start(x_res[0:LAST, NT - 1, :], t["x"][(NT - 1) * P:N]).then_inc(S["x_loaded"], 16)
            sp.dma_start(edge_i[:, 0, :], t["src"]).then_inc(S["edges_loaded"], 16)
            sp.dma_start(edge_i[:, 1, :], t["dst"]).then_inc(S["edges_loaded"], 16)
            sp.dma_start(cols[:], t["cols"]).then_inc(S["cols_loaded"], 16)

            def load_mix(i):
                if i >= 1:
                    sp.wait_ge(S["proj_filled"], BANKS * i)
                sp.dma_start(mix_w[:], t["mix1_qkvm"] if i == DEPTH else t["mix_w"][i]).then_inc(S["mixw_loaded"], 16)

            def load_ff(n, up, down):
                if 2 <= n < 2 + DEPTH:
                    sp.wait_ge(S["down_filled"], BANKS * (n - 1))
                sp.dma_start(ff_w1[:, n % 2, 0:up.shape[1]], up).then_inc(S["ffw_loaded%d" % (n % 2)], 16)
                sp.dma_start(ff_w2[:, n % 2, 0:down.shape[1]], down).then_inc(S["ffw_loaded%d" % (n % 2)], 16)

            load_mix(0)
            sp.dma_start(rows[:], t["rows"].broadcast_to([P, NROW])).then_inc(S["rows_loaded"], 16)
            sp.dma_start(gat_w[:, :, :, 0:D], t["gat_w"]).then_inc(S["gatw_loaded"], 16)
            load_ff(0, t["ff_w1"][0], t["ff_w2"][0])
            sp.dma_start(a_rows, t["a_rows"].broadcast_to([P, GAT * 2 * D])).then_inc(S["arows_loaded"], 16)
            sp.dma_start(xs.rearrange("(c p) d -> p c d", p=P), zero_x[:, None, :].broadcast_to([P, CHUNKS, D]))\
              .then_inc(S["slots_written"], 16)
            sp.dma_start(ys.rearrange("(c p) d -> p c d", p=P), zero_x[:, None, :].broadcast_to([P, CHUNKS, D]))\
              .then_inc(S["slots_written"], 16)
            load_ff(1, t["ff_w1"][1], t["ff_w2"][1])
            sp.dma_start(gate_w[:], t["gate_w"]).then_inc(S["small_loaded"], 16)
            sp.dma_start(uv_w[:], t["uv_w"]).then_inc(S["small_loaded"], 16)
            sp.dma_start(moe_b2[0:E0, 0, :], t["moe0_b2"]).then_inc(S["small_loaded"], 16)
            sp.dma_start(moe_b2[0:E1, 1, :], t["moe1_b2"]).then_inc(S["small_loaded"], 16)
            sp.dma_start(moe_b1[:], t["moe_b1"]).then_inc(S["small_loaded"], 16)
            load_mix(1)
            for i in range(2, DEPTH):
                load_mix(i)
                load_ff(i, t["ff_w1"][i], t["ff_w2"][i])
            load_mix(DEPTH)
            for e in range(2):
                load_ff(DEPTH + e, t["moe0_w1"][e], t["moe0_w2"][e])

            def load_expert(e):
                half = slice(e % 4 // 2 * KD * H1, (e % 4 // 2 + 1) * KD * H1)
                sp.dma_start(ff_w1[:, e % 2, half], t["moe1_w1"][e]).then_inc(S["expert_loaded%d" % (e % 4)], 16)
                sp.dma_start(ff_w2[:, e % 2, half], t["moe1_w2"][e]).then_inc(S["expert_loaded%d" % (e % 4)], 16)

            no, written = (sp.alloc_register("sp_" + n) for n in ("chunk", "written"))
            sp.reg_mov(no, 0)
            sp.reg_mov(written, 32)

            def moe(m, experts):
                sp.wait_ge(S["scattered"], 16 * 2 * NT * (m + 1))
                n = chunks_of(experts)
                for c0, c1, name in ((0, 1, "x_first_loaded"), (1, HEAD, "x_head_loaded"), (HEAD, n, "x_rest_loaded")):
                    sp.dma_start(x_all[m][:, c0 * D:c1 * D].rearrange("p (c d) -> p c d", d=D),
                                 xs[c0 * P:c1 * P].rearrange("(c p) d -> p c d", p=P)).then_inc(S[name], 16)
                at = sp.alloc_register("sp_slot%d" % m)
                sp.reg_mov(at, 0)
                for e in range(experts):
                    n = sp.value_load(chunk_i[0:1, e:e + 1], min_val=1, max_val=NT)
                    with sp.Fori(0, n):
                        sp.reg_add(no, no, 1)
                        sp.reg_add(written, written, 16)
                        sp.wait_ge(S["y_kept"], sp.snap(no))
                        here = sp.snap(at, min_val=0, max_val=(CHUNKS - 1) * P)
                        sp.dma_start(ys[bass.ds(here, P), :], y_all[m][:, bass.ds(here * (D // P), D)]).then_inc(S["slots_written"], 16)
                        sp.reg_add(at, at, P)
                    if m == 0 and e + 2 < E0:
                        load_ff(DEPTH + e + 2, t["moe0_w1"][e + 2], t["moe0_w2"][e + 2])
                    elif m == 0 and e + 2 == E0:
                        load_ff(DEPTH + E0, t["mix1_w1"], t["mix1_w2"])
                    elif m == 1 and e + 4 < E1:
                        load_expert(e + 4)
                sp.wait_ge(S["slots_written"], sp.snap(written))
                sp.sem_inc(S["expert_done"], 1)

            moe(0, E0)
            sp.wait_ge(S["gathered%d" % (NT - 1)], 32)
            load_expert(1)
            load_expert(3)
            sp.wait_ge(S["down_filled"], BANKS * (DEPTH + 1))
            load_expert(0)
            load_expert(2)
            moe(1, E1)
            sp.wait_ge(S["out_ready"], NT - 1)
            sp.dma_start(t["out"][0:(NT - 1) * P].rearrange("(t p) d -> p t d", p=P), normed[:, 0:NT - 1, :]).then_inc(S["stored"], 16)
            sp.wait_ge(S["out_ready"], NT)
            sp.dma_start(t["out"][(NT - 1) * P:N], normed[0:LAST, NT - 1, :]).then_inc(S["stored"], 16)
            sp.wait_ge(S["stored"], 32)

        @block.gpsimd
        def _(pool):
            steps = [0]

            def link(ins):
                steps[0] += 1
                ins.then_inc(S["pool_step"], 1)
                pool.wait_ge(S["pool_step"], steps[0])

            def rsqrt(dst, var, eps, n, ready, count):
                pool.wait_ge(S[ready], count)
                link(pool.tensor_scalar(eps, var, EPS, None, ALU.add))
                return pool.tensor_tensor(dst, eps, minus_half[:, 0:n], ALU.pow)

            def norm(n):
                rsqrt(rstd[:], mv[:, :, 1], var_eps[:], NT, "var_ready", n).then_inc(S["rstd_ready"], 1)

            pool.memset(zero_x, 0.0)
            link(pool.memset(x_res[:, NT - 1, :], 0.0))
            pool.sem_inc(S["xpad_zero"], 1)
            pool.memset(ones[:], 1.0)
            pool.memset(minus_half[:], -0.5)
            link(pool.memset(ident[:], 0.0))
            pool.affine_select(out=ident[:], in_=ident[:], compare_op=ALU.not_equal, fill=1.0, base=0,
                               pattern=[[-1, P]], channel_multiplier=1)
            pool.iota(iota[:], pattern=[[1, NP]], base=0, channel_multiplier=0, allow_small_or_imprecise_dtypes=True)
            pool.iota(iota_f[:], pattern=[[1, E1]], base=0, channel_multiplier=0, allow_small_or_imprecise_dtypes=True)
            pool.iota(chunk_ends[:], pattern=[[P, NT - 1]], base=P, channel_multiplier=0, allow_small_or_imprecise_dtypes=True)
            pool.iota(group_f[0:1, :], pattern=[[1, EGN]], base=1, channel_multiplier=0, allow_small_or_imprecise_dtypes=True)
            link(pool.memset(below[:], 1.0))
            pool.affine_select(out=below[:], in_=below[:], compare_op=ALU.is_gt, fill=0.0, base=0,
                               pattern=[[1, P]], channel_multiplier=-1)
            link(pool.memset(headmask[:], 1.0))
            hm = headmask[:].rearrange("p (h e) -> p h e", e=DH)
            link(pool.affine_select(out=hm, in_=hm, compare_op=ALU.is_ge, fill=0.0, base=0,
                                    pattern=[[-DH, P // DH], [0, DH]], channel_multiplier=1))
            link(pool.affine_select(out=hm, in_=hm, compare_op=ALU.is_ge, fill=0.0, base=DH - 1,
                                    pattern=[[DH, P // DH], [0, DH]], channel_multiplier=-1))
            pool.memset(gat_h[:, :, D:D + 1], 1.0)
            pool.memset(k_exp[:, :, N:NP], 0.0)
            pool.memset(zero_b[:], 0.0)
            link(pool.memset(v_tok[:, :, :, P:P + 1], 1.0))
            key_sum = v_tok[:, NT - 1, :, P]
            pool.affine_select(out=key_sum, in_=key_sum, compare_op=ALU.is_ge,
                               fill=0.0, base=LAST - 1, pattern=[[0, KD]], channel_multiplier=-1).then_inc(S["consts_ready"], 1)
            norm(1)
            nth = 1
            for i in range(DEPTH):
                nth += 1
                norm(nth)
                if i == 0:
                    pool.wait_ge(S["rows_loaded"], 16)
                if i > 0:
                    pool.wait_ge(S["x_updated"], 2 * i)
                pool.tensor_tensor(x_bias[:], x_mix[:], row("bo", i)[:, None, :].broadcast_to([P, NT, D]),
                                   ALU.add).then_inc(S["xbias_ready"], 1)
                if 1 <= i < GAT:
                    rsqrt(bn_rstd[:], bn_mv[:, :, 1], bn_eps[:], KD, "bnvar_ready", i).then_inc(S["bnrstd_ready"], 1)
                nth += 1
                norm(nth)
                pool.wait_ge(S["x_updated"], 2 * i + 1)
                ins = pool.tensor_tensor(x_bias[:], x_mix[:], row("ff_b2", i)[:, None, :].broadcast_to([P, NT, D]), ALU.add)
                if i == DEPTH - 1:
                    link(ins)
                    pool.wait_ge(S["agg_kept"], GAT)
                    link(pool.tensor_tensor(x_res[:], x_res[:], gat_out[:, :, 0:D], ALU.add))
                    link(pool.tensor_tensor(x_res[:], x_res[:], row("gat_b2", 0)[:, None, :].broadcast_to([P, NT, D]), ALU.add))
                    ins = pool.tensor_tensor(x_bias[:], x_bias[:], x_res[:], ALU.add)
                ins.then_inc(S["xbias_ready"], 1)

            def exchange(m):
                pool.wait_ge(S["slots_written"], 32)
                pool.wait_ge(S["slots_ready"], m + 1)
                for s in range(2):
                    for i in range(NT):
                        n = P if i < NT - 1 else LAST
                        pool.indirect_dma_start(xs, bass.IndirectOffsetOnAxis(ap=slot_i[0:n, s, i:i + 1], axis=0), normed[0:n, i, :],
                                                None).then_inc(S["scattered"], 16)
                if m == 1:
                    pool.tensor_tensor(x_res[:], x_res[:], row("beta_out", 0)[:, None, :].broadcast_to([P, NT, D]), ALU.add)\
                        .then_inc(S["x_beta_ready"], 1)
                pool.wait_ge(S["expert_done"], m + 1)
                for i in range(NT):
                    for s in range(2):
                        n = P if i < NT - 1 else LAST
                        pool.indirect_dma_start(picked[m][0:n, s, i, :], None, ys,
                                                bass.IndirectOffsetOnAxis(ap=slot_i[0:n, s, i:i + 1], axis=0)).then_inc(S["gathered%d" % i], 16)

            nth += 1
            norm(nth)
            exchange(0)
            nth += 1
            norm(nth)
            pool.wait_ge(S["norm_ready"], LAYER2_NORM)
            pool.memset(xh[:, :, :, DH:DH + 1], 1.0)
            pool.tensor_copy(xh[:, :, :, 0:DH], xn_tok[:].rearrange("p t (c h) -> p t h c", h=HEADS)).then_inc(S["xh_ready"], 1)
            for _ in range(2):
                nth += 1
                norm(nth)
            pool.wait_ge(S["mix1_normed"], 1)
            link(pool.tensor_tensor(normed[:], normed[:], row("m_g2", 0)[:, None, :].broadcast_to([P, NT, D]), ALU.mult))
            link(pool.tensor_tensor(normed[:], normed[:], row("m_b2", 0)[:, None, :].broadcast_to([P, NT, D]), ALU.add))
            link(pool.tensor_tensor(normed[:], normed[:], xn_tok[:], ALU.add))
            pool.tensor_tensor(normed[:], normed[:], x_mix[:], ALU.add).then_inc(S["mix1_added"], 1)
            nth += 1
            norm(nth)
            exchange(1)
            nth += 1
            norm(nth)

        @block.scalar
        def _(act):
            steps = [0]

            def link(ins):
                steps[0] += 1
                ins.then_inc(S["act_step"], 1)
                act.wait_ge(S["act_step"], steps[0])

            def normT_half(n, dst, g=None, b=None):
                act.wait_ge(S["normT_filled"], 2 * n)
                if g is None:
                    ins = act.activation(dst, bank(2), ACT.Copy)
                else:
                    ins = act.activation(dst, bank(2), ACT.Identity, bias=b, scale=g)
                ins.then_inc(S["normT_act"], 1)

            def up_tile(u, dst, func, bias):
                act.wait_ge(S["up_filled"], u + 1)
                act.activation(dst, bank(2 * (u % 2)), func, bias=bias).then_inc(S["up_kept"], 1)

            act.wait_ge(S["consts_ready"], 1)
            act.wait_ge(S["cols_loaded"], 16)
            normT_half(1, gat_in[:, 1, :])

            turn_no = act.alloc_register("act_hot_turn")
            pair_no = act.alloc_register("act_hot_pair")
            act.reg_mov(turn_no, 0)
            act.reg_mov(pair_no, 0)

            def count_block(b):
                if b == 0:
                    act.wait_ge(S["span_ready"], 1)
                first = act.value_load(span_i[0:1, 0, b:b + 1], min_val=0, max_val=EGN - 1)
                last = act.value_load(span_i[0:1, 1, b:b + 1], min_val=1, max_val=EGN)
                with act.Fori(first, last) as g:
                    for u in range(2):
                        c = bass.ds(g * EG + 2 * u + 1, 1)
                        act.activation(squares[:, u, :], iota[0:EP, P * b:P * (b + 1)], ACT.Square, bias=minus_dst[:, c])\
                            .then_inc(S["squared"], 1)
                    for u in range(2):
                        act.reg_add(turn_no, turn_no, 2)
                        act.reg_add(pair_no, pair_no, 1)
                        free, now = act.snap(turn_no), act.snap(pair_no)
                        act.wait_ge(S["hot_free"], free)
                        act.wait_ge(S["squared"], now)
                        act.activation(hot_dst[:, 2 * u + 1, :], squares[:, u, :], ACT.Relu, scale=-1.0, bias=ones[0:EP, 0:1])\
                            .then_inc(S["hot_act"], 1)
                    act.wait_ge(S["hot_act"], now)

            def counts_turned():
                for l in range(NT):
                    act.wait_ge(S["countT_filled"], l + 1)
                    act.activation(count_src[:, l, :], count_bank(l), ACT.Copy).then_inc(S["countT_kept"], 1)

            def gat_rows(l):
                for i in range(NT):
                    act.wait_ge(S["h_filled"], NT * l + i + 1)
                    if i == 0 and l > 0:
                        act.wait_ge(S["agg_filled"], NT * l)
                    ps = gps[:, (i % 2) * 512:(i % 2) * 512 + D + 2]
                    act.activation(gat_h[:, i, 0:D], ps[:, 0:D], ACT.Copy)
                    act.activation(score[:, i, :], ps[:, D:D + 2], ACT.Copy).then_inc(S["h_kept"], 1)

            def gat_sums(l):
                for i in range(NT):
                    act.wait_ge(S["agg_filled"], NT * l + i + 1)
                    act.activation(gat_out[:, i, :], gps[:, (i % 2) * 512:(i % 2) * 512 + D + 1], ACT.Copy).then_inc(S["agg_copied"], 1)

            def exponentials(l):
                act.wait_ge(S["r1_filled"], l + 1)
                act.wait_ge(S["r2_filled"], l + 1)
                if l == 0:
                    act.wait_ge(S["slots_written"], 32)
                for i in range(NT):
                    c = NT * l + i
                    act.activation(prob[:, i, :], gps[:, 0:NP], ACT.Exp, bias=score[:, i, 0:1])
                    if c >= 2:
                        act.wait_ge(S["prob2_taken"], c - 1)
                    act.activation(prob2[:, c % 2, :], bank(4), ACT.Exp, bias=score2[:, i:i + 1]).then_inc(S["exp_ready"], 1)

            def gat_turn(l):
                for k in range(KD):
                    act.wait_ge(S["gatT_filled"], KD * l + k + 1)
                    act.activation(gat_pre[:, k, :], gps[:, 0:NP], ACT.Identity, bias=col("gat_b", l, k)).then_inc(S["gatT_kept"], 1)

            def gat_relu(l):
                act.wait_ge(S["bn_ready"], l + 1)
                for k in range(KD):
                    act.activation(gat_in[:, k, :], gat_pre[:, k, :], ACT.Relu, bias=bn_shift[:, k:k + 1],
                                   scale=bn_scale[:, k:k + 1]).then_inc(S["gatin_ready"], 1)

            nth = 1
            for i in range(DEPTH):
                if i >= 1:
                    gat_sums(i - 1)
                nth += 1
                normT_half(nth, normed_T[:, 1, :], col("ln1_g", i, 1), col("ln1_b", i, 1))
                if i == 0:
                    count_block(0)
                act.wait_ge(S["q_shifted"], i + 1)
                act.activation(q_tok[:], q_tok[:], ACT.Exp, scale=QK_SCALE).then_inc(S["q_exped"], 1)
                act.wait_ge(S["qv_filled"], 2 * i + 2)
                act.activation(v_tok[:, :, :, 0:P], halves(bank(3, NT * D)), ACT.Copy).then_inc(S["v_kept"], 1)
                for k in range(KD):
                    act.wait_ge(S["kmax_ready"], KD * i + k + 1)
                    act.activation(k_exp[:, k, 0:N], bank(2 * k, N), ACT.Exp, bias=k_max[:, k:k + 1], scale=QK_SCALE,
                                   accum_out=k_sum[:, k:k + 1]).then_inc(S["k_exped"], 1)
                if i == 0:
                    count_block(1)
                elif i < GAT:
                    gat_turn(i - 1)
                act.wait_ge(S["qT_filled"], 2 * i + 2)
                act.activation(q_T[:, 1, :], bank(0), ACT.Copy).then_inc(S["qT_act"], 1)
                act.wait_ge(S["kT_filled"], 2 * i + 2)
                act.activation(k_tok[:, :, P:D], tiles(bank(4)), ACT.Copy).then_inc(S["kT_act"], 1)
                if i == 0:
                    for b in range(2, NT):
                        count_block(b)
                if 1 <= i < GAT:
                    gat_relu(i - 1)
                act.wait_ge(S["att_filled"], 2 * i + 2)
                act.activation(att_T[:, 1, :], bank(4), ACT.Copy).then_inc(S["att_act"], 1)
                if i < GAT:
                    gat_rows(i)
                nth += 1
                normT_half(nth, normed_T[:, 1, :], col("ln2_g", i, 1), col("ln2_b", i, 1))
                for j in range(FF // P):
                    if i == 0 and j == 4:
                        counts_turned()
                    up_tile(FF // P * i + j, hidden[:, j, :], ACT.Gelu, cols[:, COLS["ff_b1", i] + j:COLS["ff_b1", i] + j + 1])
                if i < GAT:
                    exponentials(i)

            def moe(m, experts, width):
                nonlocal nth
                nth += 1
                normT_half(nth, normed_T[:, 1, :])
                act.wait_ge(S["gdiff_ready"], m + 1)
                act.activation(pair[:, :, 1], pair[:, :, 0], ACT.Exp).then_inc(S["gexp_ready"], 1)
                act.wait_ge(S["combT_filled"], m + 1)
                act.activation(comb_T[0:experts, :], bank(3)[0:experts, :], ACT.Copy).then_inc(S["combT_kept"], 1)
                act.wait_ge(S["small_loaded"], 16 * 5)
                act.wait_ge(S["slots_ready"], m + 1)
                Q = width // P // 4
                at = act.alloc_register("act_chunk%d" % m)

                def copy_chunk():
                    c = act.snap(at, min_val=0, max_val=(chunks_of(experts) - 1) * D)
                    act.activation(x_chunk, x_all[m][:, bass.ds(c, D)], ACT.Copy).then_inc(S["x_copied"], 1)
                    act.reg_add(at, at, D)
                    act.reg_alu(at, at, (chunks_of(experts) - 1) * D, ALU.min)

                act.reg_mov(at, 0)
                act.wait_ge(S["x_first_loaded"], 16 * (m + 1))
                copy_chunk()
                act.reg_add(turned_no, turned_no, 1)
                for e in range(experts):
                    if e < 2:
                        act.wait_ge(S["x_rest_loaded" if e else "x_head_loaded"], 16 * (m + 1))
                    n = act.value_load(chunk_i[0:1, e:e + 1], min_val=1, max_val=NT)
                    with act.Fori(0, n):
                        act.wait_ge(S["x_turned"], act.snap(turned_no))
                        act.reg_add(turned_no, turned_no, 1)
                        copy_chunk()
                        for h in range(2):
                            act.reg_add(halves_no, halves_no, 1)
                            act.wait_ge(S["half_filled"], act.snap(halves_no))
                            for q in range(Q):
                                j = 2 * h * Q + q
                                ins = act.activation(hid_chunk[:, j, :], mps[:, 1024 * h + q * P:1024 * h + (q + 1) * P], ACT.Relu,
                                                     bias=moe_b1[:, m, e * 4 * Q + j:e * 4 * Q + j + 1])
                            ins.then_inc(S["half_act"], 1)

            halves_no = act.alloc_register("act_half")
            turned_no = act.alloc_register("act_turned")
            act.reg_mov(halves_no, 0)
            act.reg_mov(turned_no, 0)
            moe(0, E0, H0)
            nth += 1
            normT_half(nth, normed_T[:, 1, :])
            act.wait_ge(S["qk_min"], 1)
            act.activation(q_T[:], q_T[:], ACT.Exp).then_inc(S["qk_exp"], 1)
            act.wait_ge(S["qk_min"], 2)
            act.activation(k_tok[:], k_tok[:], ACT.Exp).then_inc(S["qk_exp"], 1)
            act.wait_ge(S["qv_filled"], 2 * DEPTH + 2)
            act.activation(v_tok[:, :, :, 0:P], halves(bank(3, NT * D)), ACT.Copy, scale=1.0 / N).then_inc(S["v_kept"], 1)
            act.wait_ge(S["qT_filled"], 2 * DEPTH + 2)
            act.activation(att_T[:, 1, :], bank(2), ACT.Copy).then_inc(S["att_act"], 1)
            nth += 1
            normT_half(nth, att_T[:, 1, :], col("m_g1", 0, 1), col("m_b1", 0, 1))

            def first_exponentials(h):
                act.wait_ge(S["hr1_filled"], h + 1)
                if h == 1:
                    act.wait_ge(S["down_filled"], BANKS * (DEPTH + 1))
                elif h:
                    act.wait_ge(S["hagg_filled"], h - 1)
                for i in range(NT):
                    ins = act.activation(head_prob[h % 2][:, i, :], gps[:, 0:NP], ACT.Exp, bias=su[:, i, h:h + 1])
                ins.then_inc(S["hr1_used"], 1)

            def second_exponentials(h):
                act.wait_ge(S["hr2_filled"], h + 1)
                for i in range(NT):
                    if h:
                        act.wait_ge(S["prob2_taken"], NT * (GAT + h - 1) + i + 1)
                    act.activation(head_prob2[:, i, :], bank(4), ACT.Exp, bias=su2[:, i, h:h + 1]).then_inc(S["exp_ready"], 1)

            for j in range(4):
                up_tile(DEPTH * 8 + j, hidden2[:, j, :], ACT.Relu, 0.0)
                if j == 2:
                    first_exponentials(0)
            second_exponentials(0)
            act.wait_ge(S["down_filled"], BANKS * (DEPTH + 1))
            act.activation(normed[:], tiles(mps[:, 0:NT * D]), ACT.Copy).then_inc(S["down_kept"], 1)
            for h in range(1, HEADS + 1):
                if h < HEADS:
                    first_exponentials(h)
                    second_exponentials(h)
                act.wait_ge(S["hagg_filled"], h)
                if h > 1:
                    act.wait_ge(S["hT_filled"], h - 1)
                act.activation(head_T[:], mps[0:DH + 1, 0:NP], ACT.Copy).then_inc(S["hagg_kept"], 1)
            moe(1, E1, H1)

        @block.vector
        def _(dve):
            steps = [0]

            def link(ins):
                steps[0] += 1
                ins.then_inc(S["dve_step"], 1)
                dve.wait_ge(S["dve_step"], steps[0])

            norms, turns = [0], [0]

            def normalise(src, dst, stats_taken=False):
                norms[0] += 1
                if not stats_taken:
                    for i in range(NT):
                        ins = dve.bn_stats(stats[:, i, :], src[:, i, :])
                    link(ins)
                for i in range(NT):
                    ins = dve.bn_aggr(mv[:, i, :], stats[:, i, :])
                ins.then_inc(S["var_ready"], 1)
                dve.wait_ge(S["rstd_ready"], norms[0])
                for i in range(NT):
                    ins = dve.tensor_scalar(dst[:, i, :], src[:, i, :], mv[:, i, 0:1], rstd[:, i:i + 1],
                                            ALU.subtract, ALU.mult)
                return ins

            def normT_half(dst, g=None, b=None):
                turns[0] += 1
                dve.wait_ge(S["normT_filled"], 2 * turns[0] - 1)
                if g is None:
                    ins = dve.tensor_copy(dst, bank(4))
                else:
                    ins = dve.tensor_scalar(dst, bank(4), g, b, ALU.mult, ALU.add)
                ins.then_inc(S["normT_dve"], 1)

            dve.wait_ge(S["consts_ready"], 1)
            dve.wait_ge(S["edges_loaded"], 32)
            link(dve.tensor_copy(edge_f[:], edge_i[:]))
            dve.tensor_scalar(minus_dst, edge_f[:, 1, :], -1.0, None, ALU.mult)
            for b in range(NT):
                link(dve.tensor_scalar(in_block[:, b, :], edge_f[:, 1, :], float(P * b), None, ALU.is_ge))
                ins = dve.scalar_tensor_tensor(out=in_block[:, b, :], in0=edge_f[:, 1, :], scalar=float(P * (b + 1)),
                                               in1=in_block[:, b, :], op0=ALU.is_lt, op1=ALU.mult)
            link(ins)
            dve.sem_inc(S["in_block_ready"], 1)
            def spans():
                dve.wait_ge(S["block_counts"], 1)
                for h in range(2):
                    c = NT * ET // 2
                    ins = dve.tensor_reduce(present[0:1, h * c // EG:(h + 1) * c // EG],
                                            gps[0:1, 512 * h:512 * h + c].rearrange("p (g s) -> p g s", s=EG), AX.X, ALU.add)
                link(ins)
                pr = present[:].rearrange("p (b g) -> p b g", b=NT)
                gr = group_f[0:1, None, :].broadcast_to([1, NT, EGN])
                link(dve.tensor_scalar(present[:], present[:], 0.0, None, ALU.is_gt))
                link(dve.tensor_tensor(marked[:].rearrange("p (b g) -> p b g", b=NT), pr, gr, ALU.mult))
                link(dve.tensor_reduce(span_f[:, 1, :], marked[:].rearrange("p (b g) -> p b g", b=NT), AX.X, ALU.max))
                link(dve.tensor_scalar(group_r[:], group_f[:], -1.0, float(EGN + 1), ALU.mult, ALU.add))
                link(dve.tensor_tensor(marked[:].rearrange("p (b g) -> p b g", b=NT), pr,
                                       group_r[0:1, None, :].broadcast_to([1, NT, EGN]), ALU.mult))
                link(dve.tensor_reduce(span_f[:, 0, :], marked[:].rearrange("p (b g) -> p b g", b=NT), AX.X, ALU.max))
                link(dve.tensor_scalar(span_f[:, 0, :], span_f[:, 0, :], -1.0, float(EGN), ALU.mult, ALU.add))
                link(dve.tensor_scalar(span_f[:, 0, :], span_f[:, 0, :], float(EGN - 1), None, ALU.min))
                link(dve.tensor_scalar(span_g[:, 0, :], span_f[:, 0, :], 1.0, None, ALU.add))
                link(dve.tensor_tensor(span_f[:, 1, :], span_f[:, 1, :], span_g[:, 0, :], ALU.max))
                link(dve.tensor_copy(span_i[:], span_f[:]))
                dve.sem_inc(S["span_ready"], 1)

            turn_no = dve.alloc_register("dve_hot_turn")
            dve.reg_mov(turn_no, 0)

            def count_block(b):
                first = dve.value_load(span_i[0:1, 0, b:b + 1], min_val=0, max_val=EGN - 1)
                last = dve.value_load(span_i[0:1, 1, b:b + 1], min_val=1, max_val=EGN)
                with dve.Fori(first, last) as g:
                    for s in range(EG):
                        dve.reg_add(turn_no, turn_no, 1)
                        dve.wait_ge(S["hot_free"], dve.snap(turn_no))
                        c = bass.ds(g * EG + s, 1)
                        if s % 2 == 0:
                            dve.tensor_scalar(hot_dst[:, s, :], iota[0:EP, P * b:P * (b + 1)], edge_f[:, 1, c],
                                              None, ALU.is_equal)
                        dve.tensor_scalar(hot_src[:, s, :], iota[0:EP, :], edge_f[:, 0, c], None, ALU.is_equal)\
                           .then_inc(S["hot_ready"], 1)
                score_weights(b)
                dve.wait_ge(S["count_filled"], b + 1)
                dve.tensor_copy(count_dst[:, b, :], gps[:, 0:NP])
                dve.tensor_scalar(no_edge[:, b, :], gps[:, 0:NP], 0.0, NOEDGE, ALU.is_equal, ALU.mult).then_inc(S["count_kept"], 1)

            dve.wait_ge(S["x_loaded"], 32)
            link(normalise(x_res, x_mix))
            dve.sem_inc(S["norm_ready"], 1)
            normT_half(gat_in[:, 0, :])

            score_jobs = [(l, n, k) for l in range(GAT) for n in range(2) for k in range(KD)]

            def score_weights(b):
                if b == 0:
                    dve.wait_ge(S["arows_loaded"], 16)
                    dve.wait_ge(S["gatw_loaded"], 16)
                for l, n, k in score_jobs[b::NT]:
                    s0 = ((l * 2 + n) * KD + k) * D
                    a = a_rows[:, (2 * l + n) * D:(2 * l + n + 1) * D]
                    dve.tensor_tensor_reduce(flat(hidden[:, 0:NT, :])[:, s0:s0 + D], gat_w[:, l, k, 0:D], a, 1.0, 0.0, ALU.mult,
                                             ALU.add, gat_w[:, l, k, D + n:D + n + 1]).then_inc(S["gatw_ready"], 1)

            def gat_shift(l):
                dve.wait_ge(S["srow_filled"], l + 1)
                for i in range(NT):
                    ins = dve.tensor_tensor_reduce(unused[i], gps[:, 0:N], no_edge[:, i, 0:N], 1.0, NOEDGE * 2, ALU.add,
                                                   ALU.max, score_max[:, i:i + 1])
                ins.then_inc(S["max_done"], 1)
                dve.wait_ge(S["max_done"], l + 1)
                link(dve.scalar_tensor_tensor(out=score_max[:], in0=score_max[:], scalar=NOEDGE / 2, in1=score_max[:],
                                              op0=ALU.is_gt, op1=ALU.mult))
                link(dve.tensor_tensor(tiny[:, 0:NT], score_max[:], score[:, :, 1], ALU.add))
                link(dve.scalar_tensor_tensor(out=tiny2[:, 0:NT], in0=tiny[:, 0:NT], scalar=0.2, in1=tiny[:, 0:NT],
                                              op0=ALU.mult, op1=ALU.max))
                dve.tensor_tensor(shift[:, 0, :], score[:, :, 1], tiny2[:, 0:NT], ALU.subtract)
                dve.tensor_scalar(score2[:], score[:, :, 0], 0.2, None, ALU.mult)
                dve.scalar_tensor_tensor(out=shift[:, 1, :], in0=score[:, :, 1], scalar=0.2, in1=tiny2[:, 0:NT],
                                         op0=ALU.mult, op1=ALU.subtract).then_inc(S["shift_ready"], 1)

            def probabilities(n, p1, p2):
                def larger(i):
                    dve.wait_ge(S["exp_ready"], n + i + 1)
                    dve.tensor_tensor(p1[:, i, :], p1[:, i, :], p2(i), ALU.max).then_inc(S["prob2_taken"], 1)

                def counted(i):
                    dve.wait_ge(S["prob2_taken"], n + i + 1)
                    dve.scalar_tensor_tensor(out=p1[:, i, :], in0=p1[:, i, :], scalar=1.0, in1=count_src[:, i, :],
                                             op0=ALU.min, op1=ALU.mult).then_inc(S["prob_ready"], 1)

                larger(0)
                for i in range(1, NT):
                    larger(i)
                    counted(i - 1)
                counted(NT - 1)

            def gat_normalise(l):
                dve.wait_ge(S["agg_copied"], NT * (l + 1))
                link(dve.tensor_scalar(tiny[:, 0:NT], gat_out[:, :, D], 1e-16, None, ALU.add))
                link(dve.reciprocal(tiny2[:, 0:NT], tiny[:, 0:NT]))
                dve.tensor_tensor(gat_out[:, :, 0:D], gat_out[:, :, 0:D], tiny2[:, 0:NT, None].broadcast_to([P, NT, D]),
                                  ALU.mult).then_inc(S["agg_kept"], 1)

            def gat_batchnorm(l):
                for k in range(KD):
                    dve.wait_ge(S["gatT_kept"], KD * l + k + 1)
                    dve.bn_stats(bn_st[:, k, 0, :], gat_pre[:, k, 0:512])
                    ins = dve.bn_stats(bn_st[:, k, 1, :], gat_pre[:, k, 512:N])
                link(ins)
                for k in range(KD):
                    ins = dve.bn_aggr(bn_mv[:, k, :], bn_st[:, k, :, :])
                ins.then_inc(S["bnvar_ready"], 1)
                dve.wait_ge(S["bnrstd_ready"], l + 1)
                c = COLS["gamma", l]
                link(dve.tensor_tensor(bn_scale[:], bn_rstd[:], cols[:, c:c + KD], ALU.mult))
                link(dve.tensor_tensor(bn_shift[:], bn_mv[:, :, 0], bn_scale[:], ALU.mult))
                c = COLS["beta", l]
                dve.tensor_tensor(bn_shift[:], cols[:, c:c + KD], bn_shift[:], ALU.subtract).then_inc(S["bn_ready"], 1)

            def stats_by_bank(name, n, value):
                for p in range(BANKS):
                    dve.wait_ge(S[name], BANKS * n + p + 1)
                    i0, i1 = bank_tiles(p)[0], bank_tiles(p)[-1] + 1
                    x = value(i0, i1)
                    for i in range(i0, i1):
                        ins = dve.bn_stats(stats[:, i, :], x[:, i, :])
                link(ins)

            def residual(n, name, layer, out):
                dve.wait_ge(S["xbias_ready"], n)

                def add(i0, i1):
                    link(dve.tensor_tensor(out[:, i0:i1, :], tiles(mps[:, 0:NT * D])[:, i0:i1, :], x_bias[:, i0:i1, :], ALU.add))
                    return out

                stats_by_bank(name, layer, add)
                dve.sem_inc(S["x_updated"], 1)

            for i in range(DEPTH):
                link(normalise(x_mix, normed, stats_taken=i > 0))
                dve.sem_inc(S["norm_ready"], 1)
                normT_half(normed_T[:, 0, :], col("ln1_g", i, 0), col("ln1_b", i, 0))
                if i == 0:
                    spans()
                    count_block(0)
                else:
                    gat_normalise(i - 1)
                dve.wait_ge(S["qv_filled"], 2 * i + 1)
                heads = mps[:, 0:NT * D].rearrange("p (g c) -> p g c", c=DH)
                link(dve.tensor_reduce(q_max[:], heads, AX.X, ALU.max))
                qh = q_tok[:].rearrange("p t (g c) -> p (t g) c", c=DH)
                dve.tensor_tensor(qh, heads, q_max[:, :, None].broadcast_to([P, NT * HEADS, DH]),
                                  ALU.subtract).then_inc(S["q_shifted"], 1)
                dve.wait_ge(S["q_exped"], i + 1)
                link(dve.tensor_reduce(q_max[:], qh, AX.X, ALU.add))
                link(dve.reciprocal(q_inv[:], q_max[:]))
                dve.tensor_tensor(qh, qh, q_inv[:, :, None].broadcast_to([P, NT * HEADS, DH]), ALU.mult).then_inc(S["q_normed"], 1)
                for k in range(KD):
                    dve.wait_ge(S["k_filled"], KD * i + k + 1)
                    link(dve.tensor_reduce(k_top[:, k:k + 1], bank(2 * k, N), AX.X, ALU.max))
                    dve.tensor_scalar(k_max[:, k:k + 1], k_top[:, k:k + 1], -QK_SCALE, None, ALU.mult).then_inc(S["kmax_ready"], 1)
                if i == 0:
                    count_block(1)
                dve.wait_ge(S["qT_filled"], 2 * i + 1)
                dve.tensor_copy(q_T[:, 0, :], bank(4)).then_inc(S["qT_dve"], 1)
                if i == 0:
                    count_block(2)
                dve.wait_ge(S["kT_filled"], 2 * i + 1)
                dve.tensor_copy(k_tok[:, :, 0:P], tiles(bank(2))).then_inc(S["kT_dve"], 1)
                dve.wait_ge(S["k_exped"], KD * i + 2)
                link(dve.reciprocal(k_inv[:], k_sum[:]))
                if i == 0:
                    count_block(3)
                elif i < GAT:
                    gat_batchnorm(i - 1)
                dve.wait_ge(S["ctx_filled"], i + 1)
                for k in range(KD):
                    ins = dve.scalar_tensor_tensor(out=context[:, k, 0:P], in0=mps[:, k * 256:k * 256 + P], scalar=k_inv[:, k:k + 1],
                                                   in1=headmask[:], op0=ALU.mult, op1=ALU.mult)
                ins.then_inc(S["ctx_kept"], 1)
                if i == 0:
                    count_block(4)
                dve.wait_ge(S["att_filled"], 2 * i + 1)
                dve.tensor_copy(att_T[:, 0, :], bank(2)).then_inc(S["att_dve"], 1)
                residual(2 * i + 1, "proj_filled", i, x_mix)
                link(normalise(x_mix, normed, stats_taken=True))
                dve.sem_inc(S["norm_ready"], 1)
                normT_half(normed_T[:, 0, :], col("ln2_g", i, 0), col("ln2_b", i, 0))
                if i < GAT:
                    gat_shift(i)
                    probabilities(NT * i, prob, lambda j: prob2[:, (NT * i + j) % 2, :])
                residual(2 * i + 2, "down_filled", i, x_mix if i < DEPTH - 1 else x_res)
            def moe(m, experts, width, bias):
                link(normalise(x_res, normed, stats_taken=m == 0))
                dve.sem_inc(S["norm_ready"], 1)
                normT_half(normed_T[:, 0, :])
                dve.wait_ge(S["gate_filled"], m + 1)
                g = gates[:, :, 0:experts]
                link(dve.tensor_tensor(g, gps[:, 0:NT * experts].rearrange("p (t e) -> p t e", t=NT),
                                       row(bias, 0, experts)[:, None, :].broadcast_to([P, NT, experts]), ALU.add))
                for i in range(NT):
                    ins = dve.max(top[:, i, :], gates[:, i, 0:experts])
                link(ins)
                for i in range(NT):
                    ins = dve.max_index(top_i[:, i, :], top[:, i, :], gates[:, i, 0:experts])
                link(ins)
                dve.tensor_tensor(pair[:, :, 0], top[:, :, 1], top[:, :, 0], ALU.subtract).then_inc(S["gdiff_ready"], 1)
                link(dve.tensor_copy(top_f[:], top_i[:]))
                ch, fh, bo = (a[:, :, 0:experts] for a in (chosen, first_hot, both))
                wide = lambda column: column[:, :, None].broadcast_to([P, NT, experts])
                expert_no = iota_f[:, None, 0:experts].broadcast_to([P, NT, experts])
                dve.tensor_tensor(fh, expert_no, wide(top_f[:, :, 0]), ALU.is_equal)
                link(dve.tensor_tensor(ch, expert_no, wide(top_f[:, :, 1]), ALU.is_equal))
                link(dve.tensor_tensor(bo, ch, fh, ALU.add))
                valid = v_tok[:, NT - 1, 0, P:P + 1]
                link(dve.tensor_scalar(both[:, NT - 1, 0:experts], both[:, NT - 1, 0:experts], valid, None, ALU.mult))
                dve.sem_inc(S["chosen_ready"], 1)
                dve.wait_ge(S["gexp_ready"], m + 1)
                link(dve.tensor_scalar(pair[:, :, 0], pair[:, :, 1], 1.0, None, ALU.add))
                link(dve.reciprocal(pair[:, :, 2], pair[:, :, 0]))
                link(dve.tensor_tensor(pair[:, :, 3], pair[:, :, 1], pair[:, :, 2], ALU.mult))
                cb, sl = comb[:, :, 0:experts], slot[:, :, 0:experts]
                dve.tensor_tensor(cb, fh, wide(pair[:, :, 2]), ALU.mult)
                link(dve.tensor_tensor(sl, ch, wide(pair[:, :, 3]), ALU.mult))
                link(dve.tensor_tensor(cb, cb, sl, ALU.add))
                dve.sem_inc(S["comb_ready"], 1)
                dve.wait_ge(S["ranks_filled"], m + 1)
                within = gps[:, 0:NT * experts].rearrange("p (t e) -> p t e", t=NT)
                totals = gps[:, 512:512 + NT * experts].rearrange("p (t e) -> p t e", t=NT)
                dve.memset(before[:, 0, :], 0.0)
                dve.tensor_copy(before[:, 1, 0:experts], totals[:, 0, :])
                link(dve.tensor_reduce(tokens_n[:, 0:experts], totals.rearrange("p t e -> p e t"), AX.X, ALU.add))
                link(dve.tensor_tensor(before[:, 2, 0:experts], before[:, 1, 0:experts], totals[:, 1, :], ALU.add))
                link(dve.tensor_tensor(exceeds[:, 0:experts, :], tokens_n[:, 0:experts, None].broadcast_to([P, experts, NT - 1]),
                                       chunk_ends[:, None, :].broadcast_to([P, experts, NT - 1]), ALU.is_gt))
                dve.tensor_tensor(before[:, 3, 0:experts], before[:, 2, 0:experts], totals[:, 2, :], ALU.add)
                link(dve.tensor_reduce(chunk_n[:, 0:experts], exceeds[:, 0:experts, :], AX.X, ALU.add))
                dve.tensor_tensor(before[:, 4, 0:experts], before[:, 3, 0:experts], totals[:, 3, :], ALU.add)
                dve.tensor_scalar(chunk_i[:, 0:experts], chunk_n[:, 0:experts], 1.0, None, ALU.add)
                dve.memset(scan_a[:, 0:1], 0.0)
                link(dve.tensor_scalar(scan_a[:, 1:experts], chunk_n[:, 0:experts - 1], 1.0, float(P), ALU.add, ALU.mult))
                dve.tensor_tensor(sl, within, before[:, 0:NT, 0:experts], ALU.add)
                a, b, d = scan_a, scan_b, 1
                while d < experts:
                    dve.tensor_copy(b[:, 0:d], a[:, 0:d])
                    link(dve.tensor_tensor(b[:, d:experts], a[:, d:experts], a[:, 0:experts - d], ALU.add))
                    a, b, d = b, a, 2 * d
                link(dve.tensor_tensor(sl, sl, a[:, None, 0:experts].broadcast_to([P, NT, experts]), ALU.add))
                dve.tensor_tensor(fh, fh, sl, ALU.mult)
                link(dve.tensor_tensor(ch, ch, sl, ALU.mult))
                dve.tensor_reduce(slot_f[:, 0, :], fh, AX.X, ALU.add)
                link(dve.tensor_reduce(slot_f[:, 1, :], ch, AX.X, ALU.add))
                link(dve.tensor_copy(slot_i[:], slot_f[:]))
                dve.sem_inc(S["slots_ready"], 1)
                dve.wait_ge(S["moe_bias_filled"], m + 1)
                base = x_res if m == 0 else normed
                link(dve.tensor_tensor(x_mix[:], tiles(mps[:, 0:NT * D]), base[:], ALU.add))
                dve.sem_inc(S["moe_bias_kept"], 1)
                Q = width // P // 4

                def keep_turned(turn):
                    dve.wait_ge(S["x_turned"], turn)
                    dve.tensor_copy(xT_chunk, gps[:, 0:D].rearrange("p (k n) -> p k n", k=KD)).then_inc(S["xT_kept"], 1)

                at = dve.alloc_register("dve_at%d" % m)
                dve.reg_mov(at, 0)
                dve.reg_add(turned_no, turned_no, 1)
                keep_turned(dve.snap(turned_no))
                for e in range(experts):
                    n = dve.value_load(chunk_i[0:1, e:e + 1], min_val=1, max_val=NT)
                    with dve.Fori(0, n):
                        for h in range(2):
                            dve.reg_add(halves_no, halves_no, 1)
                            dve.wait_ge(S["half_filled"], dve.snap(halves_no))
                            for q in range(Q):
                                j = (2 * h + 1) * Q + q
                                c = 1024 * h + 512 + q * P
                                ins = dve.tensor_scalar(hid_chunk[:, j, :], mps[:, c:c + P],
                                                        moe_b1[:, m, e * 4 * Q + j:e * 4 * Q + j + 1], 0.0, ALU.add, ALU.max)
                            ins.then_inc(S["half_dve"], 1)
                        dve.reg_add(turned_no, turned_no, 1)
                        keep_turned(dve.snap(turned_no))
                        dve.reg_add(chunk_no, chunk_no, 1)
                        dve.wait_ge(S["y_filled"], dve.snap(chunk_no))
                        c = dve.snap(at, min_val=0, max_val=(chunks_of(experts) - 1) * D)
                        dve.tensor_copy(y_all[m][:, bass.ds(c, D)], gps[:, 512:512 + D]).then_inc(S["y_kept"], 1)
                        dve.reg_add(at, at, D)
                for i in range(NT):
                    dve.wait_ge(S["gathered%d" % i], 32 * (m + 1))
                    n = P if i < NT - 1 else LAST
                    for k in range(2):
                        link(dve.scalar_tensor_tensor(out=x_mix[0:n, i, :], in0=picked[m][0:n, k, i, :], scalar=pair[0:n, i, 2 + k:3 + k],
                                                      in1=x_mix[0:n, i, :], op0=ALU.mult, op1=ALU.add))
                    ins = dve.bn_stats(stats[:, i, :], x_mix[:, i, :])
                link(ins)

            halves_no = dve.alloc_register("dve_half")
            turned_no = dve.alloc_register("dve_turned")
            chunk_no = dve.alloc_register("dve_chunk")
            for r in (halves_no, turned_no, chunk_no):
                dve.reg_mov(r, 0)
            moe(0, E0, H0, "bg")

            link(normalise(x_mix, xn_tok, stats_taken=True))
            dve.sem_inc(S["norm_ready"], 1)
            normT_half(normed_T[:, 0, :])

            def head_max(h):
                dve.wait_ge(S["hrow_filled"], h + 1)
                for i in range(NT):
                    ins = dve.tensor_tensor_reduce(prob[:, i, :], gps[:, 0:NP], no_edge[:, i, :], 1.0, NOEDGE * 2, ALU.add,
                                                   ALU.max, hmax[:, i, h:h + 1])
                ins.then_inc(S["hmax_done"], 1)

            dve.wait_ge(S["uv_filled"], 1)
            uv = gps[:, 0:NT * 2 * HEADS].rearrange("p (t c) -> p t c", t=NT)
            dve.tensor_tensor(su[:], uv[:, :, 0:HEADS], row("b_u", 0, HEADS)[:, None, :].broadcast_to([P, NT, HEADS]), ALU.add)
            link(dve.tensor_copy(sv[:], uv[:, :, HEADS:2 * HEADS]))
            dve.sem_inc(S["uv_ready"], 1)
            for k in range(KD):
                dve.wait_ge(S["qk_filled"], k + 1)
                dve.tensor_scalar(q_T[:, k, :], bank(2 * k), 0.0, None, ALU.min)
                ins = dve.tensor_scalar(k_exp[:, k, :], bank(2 * k), 0.0, None, ALU.max)
            link(ins)
            dve.sem_inc(S["qk_min"], 1)
            head_max(0)
            dve.wait_ge(S["qv_filled"], 2 * DEPTH + 1)
            dve.tensor_scalar(k_tok[:], tiles(mps[:, 0:NT * D]), 0.0, None, ALU.min)
            link(dve.tensor_scalar(q_tok[:], tiles(mps[:, 0:NT * D]), 0.0, None, ALU.max))
            dve.sem_inc(S["qk_min"], 1)
            dve.wait_ge(S["qk_exp"], 1)
            dve.tensor_tensor(q_T[:], q_T[:], k_exp[:], ALU.add).then_inc(S["qk_ready"], 1)
            dve.wait_ge(S["qk_exp"], 2)
            link(dve.tensor_tensor(k_tok[:], k_tok[:], q_tok[:], ALU.add))
            dve.tensor_scalar(k_tok[:][:, NT - 1, :], k_tok[:][:, NT - 1, :], v_tok[:, NT - 1, 0, P:P + 1], None,
                              ALU.mult).then_inc(S["qk_ready"], 1)
            head_max(1)
            dve.wait_ge(S["ctx_filled"], DEPTH + 1)
            for k in range(KD):
                dve.tensor_tensor(context[:, k, 0:P], mps[:, k * 256:k * 256 + P], headmask[:], ALU.mult)
                ins = dve.tensor_scalar(context[:, k, P:P + 4], headmask[:, 0:P:DH], mps[:, k * 256 + P:k * 256 + P + 1],
                                        None, ALU.mult)
            ins.then_inc(S["ctx_kept"], 1)
            head_max(2)
            dve.wait_ge(S["num_filled"], 1)
            ps = mps[:, 0:NT * 512].rearrange("p (t x) -> p t x", t=NT)
            den, inv = (a[:].rearrange("p (t k h) -> p t k h", t=NT, k=KD) for a in (tiny, tiny2))
            for k in range(KD):
                c = k * (P + 4) + P
                ins = dve.tensor_scalar(den[:, :, k, :], ps[:, :, c:c + 4], ATT_EPS, None, ALU.add)
            link(ins)
            link(dve.reciprocal(tiny2[:], tiny[:]))
            link(dve.tensor_scalar(tiny2[:], tiny2[:], float(N), None, ALU.mult))
            for k in range(KD):
                c = k * (P + 4)
                ins = dve.tensor_tensor(q_tok[:, :, k * P:(k + 1) * P].rearrange("p t (h c) -> p t h c", c=DH),
                                        ps[:, :, c:c + P].rearrange("p t (h c) -> p t h c", c=DH),
                                        inv[:, :, k, :, None].broadcast_to([P, NT, 4, DH]), ALU.mult)
            ins.then_inc(S["num_kept"], 1)
            head_max(3)
            dve.wait_ge(S["qT_filled"], 2 * DEPTH + 1)
            dve.tensor_copy(att_T[:, 0, :], bank(4)).then_inc(S["att_dve"], 1)
            head_max(4)
            message = tiles(mps[:, 0:NT * D])
            stats_by_bank("proj_filled", DEPTH, lambda i0, i1: message)
            link(normalise(message, normed, stats_taken=True))
            dve.sem_inc(S["norm_ready"], 1)
            normT_half(att_T[:, 0, :], col("m_g1", 0, 0), col("m_b1", 0, 0))
            for h in range(5, HEADS):
                head_max(h)
            dve.wait_ge(S["hmax_done"], HEADS)
            link(dve.scalar_tensor_tensor(out=hmax[:], in0=hmax[:], scalar=NOEDGE / 2, in1=hmax[:], op0=ALU.is_gt, op1=ALU.mult))
            link(dve.tensor_tensor(hmax[:], hmax[:], sv[:], ALU.add))
            link(dve.scalar_tensor_tensor(out=hm_[:], in0=hmax[:], scalar=0.2, in1=hmax[:], op0=ALU.mult, op1=ALU.max))
            dve.tensor_tensor(hs1[:], sv[:], hm_[:], ALU.subtract)
            dve.tensor_scalar(su2[:], su[:], 0.2, None, ALU.mult)
            dve.scalar_tensor_tensor(out=hs2[:], in0=sv[:], scalar=0.2, in1=hm_[:], op0=ALU.mult, op1=ALU.subtract)\
               .then_inc(S["hshift_ready"], 1)

            def keep_head(h):
                dve.wait_ge(S["hT_filled"], h + 1)
                ps = mps[:, 1024 + 512 * (h % 2):1024 + 512 * (h % 2) + NT * (DH + 1)]
                dve.tensor_copy(head_sum[:, :, h, :], ps.rearrange("p (t c) -> p t c", t=NT)).then_inc(S["hT_kept"], 1)

            for h in range(HEADS):
                probabilities(NT * (GAT + h), head_prob[h % 2], lambda i: head_prob2[:, i, :])
                if h == 0:
                    dve.wait_ge(S["down_kept"], 1)
                    normalise(normed, normed).then_inc(S["mix1_normed"], 1)
                if h >= 2:
                    keep_head(h - 2)
            for h in range(HEADS - 2, HEADS):
                keep_head(h)
            dve.wait_ge(S["hT_kept"], HEADS)
            link(dve.tensor_scalar(tiny[:].rearrange("p (t h) -> p t h", t=NT), head_sum[:, :, :, DH], 1e-30, None, ALU.max))
            link(dve.reciprocal(tiny2[:], tiny[:]))
            link(dve.tensor_tensor(head_sum[:, :, :, 0:DH], head_sum[:, :, :, 0:DH],
                                   tiny2[:].rearrange("p (t h) -> p t h", t=NT)[:, :, :, None].broadcast_to([P, NT, HEADS, DH]), ALU.mult))
            dve.wait_ge(S["mix1_added"], 1)
            by_head = lambda ap: ap.rearrange("p t (c h) -> p t h c", h=HEADS)
            link(dve.tensor_tensor(by_head(x_res[:]), head_sum[:, :, :, 0:DH], by_head(normed[:]), ALU.add))

            moe(1, E1, H1, "gate_b")
            norms[0] += 1
            for i in range(NT):
                ins = dve.bn_aggr(mv[:, i, :], stats[:, i, :])
            ins.then_inc(S["var_ready"], 1)
            dve.wait_ge(S["var_ready"], norms[0])
            for i in range(NT):
                ins = dve.scalar_tensor_tensor(out=normed[:, i, :], in0=x_mix[:, i, :], scalar=mv[:, i, 0:1], in1=row("gamma_out", 0),
                                               op0=ALU.subtract, op1=ALU.mult)
            link(ins)
            dve.wait_ge(S["x_beta_ready"], 1)
            dve.wait_ge(S["rstd_ready"], norms[0])
            for i in range(NT):
                dve.scalar_tensor_tensor(out=normed[:, i, :], in0=normed[:, i, :], scalar=rstd[:, i:i + 1], in1=x_res[:, i, :],
                                         op0=ALU.mult, op1=ALU.add).then_inc(S["out_ready"], 1)

        @block.tensor
        def _(pe):
            turns = [0]

            def product(out, pairs):
                ins = None
                width = out.shape[-1]
                for c in range(0, width, 512):
                    w = min(512, width - c)
                    for n, (lhsT, rhs) in enumerate(pairs):
                        ins = pe.matmul(out[:, c:c + w], lhsT, rhs[:, c:c + w], start=(n == 0), stop=(n == len(pairs) - 1))
                return ins

            def turn(src, k, out):
                for i in range(NT):
                    ins = pe.transpose(out[:, i * P:(i + 1) * P], src[:, i, k * P:(k + 1) * P], ident[:])
                return ins

            def keep_warm(n):
                for _ in range(n):
                    pe.matmul(mps[:, 5 * 512:6 * 512], zero_b[:, 0:P], zero_b[:], start=True, stop=True)

            def turn_norm(src, warm=0):
                turns[0] += 1
                n = turns[0]
                if n > 1:
                    pe.wait_ge(S["normT_dve"], n - 1)
                    pe.wait_ge(S["normT_act"], n - 1)
                keep_warm(warm)
                pe.wait_ge(S["norm_ready"], n)
                turn(src, 0, bank(4)).then_inc(S["normT_filled"], 1)
                turn(src, 1, bank(2)).then_inc(S["normT_filled"], 1)

            def norm_turned():
                pe.wait_ge(S["normT_dve"], turns[0])
                pe.wait_ge(S["normT_act"], turns[0])

            def part(src, k, i):
                return src[:, k, i * P:(i + 1) * P]

            def spread(column, out):
                for i in range(NT):
                    ins = pe.matmul(out[:, i * P:(i + 1) * P], column(i).broadcast_to([P, P]), ident[:], start=True, stop=True)
                return ins

            pe.wait_ge(S["consts_ready"], 1)
            pe.wait_ge(S["in_block_ready"], 1)
            blocks = in_block.rearrange("p b t -> p (b t)")
            for h in range(2):
                c = NT * ET // 2
                ins = pe.matmul(gps[0:1, 512 * h:512 * h + c], ones[0:EP, 0:1], blocks[:, h * c:(h + 1) * c], start=True, stop=True)
            ins.then_inc(S["block_counts"], 1)
            pe.sem_inc(S["hot_free"], EG)

            turn_no = pe.alloc_register("pe_hot_turn")
            pair_no = pe.alloc_register("pe_hot_pair")
            pe.reg_mov(turn_no, 0)
            pe.reg_mov(pair_no, 0)

            def count_block(b):
                first = pe.value_load(span_i[0:1, 0, b:b + 1], min_val=0, max_val=EGN - 1)
                last = pe.value_load(span_i[0:1, 1, b:b + 1], min_val=1, max_val=EGN)
                if b:
                    pe.wait_ge(S["count_kept"], b)
                for c, w in ((0, 512), (512, P)):
                    pe.matmul(gps[:, c:c + w], zero_b[:, 0:P], zero_b[:, 0:w], start=True, stop=False, skip_group_check=True)
                with pe.Fori(first, last) as g:
                    for s in range(EG):
                        pe.reg_add(turn_no, turn_no, 1)
                        ready = pe.snap(turn_no)
                        if s % 2:
                            pe.reg_add(pair_no, pair_no, 1)
                            by_act = pe.snap(pair_no)
                        pe.wait_ge(S["hot_ready"], ready)
                        if s % 2:
                            pe.wait_ge(S["hot_act"], by_act)
                        for c, w in ((0, 512), (512, P)):
                            ins = pe.matmul(gps[:, c:c + w], hot_dst[:, s, :], hot_src[:, s, c:c + w],
                                            start=False, stop=False, skip_group_check=True)
                        ins.then_inc(S["hot_free"], 1)
                for c, w in ((0, 512), (512, P)):
                    ins = pe.matmul(gps[:, c:c + w], zero_b[:, 0:P], zero_b[:, 0:w], start=False, stop=True, skip_group_check=True)
                ins.then_inc(S["count_filled"], 1)

            def turn_counts():
                pe.wait_ge(S["shift_ready"], 1)
                for l in range(NT):
                    if l >= 2:
                        pe.wait_ge(S["countT_kept"], l - 1)
                    for b in range(NT):
                        ins = pe.transpose(count_bank(l)[:, b * P:(b + 1) * P], count_dst[:, b, l * P:(l + 1) * P], ident[:])
                    ins.then_inc(S["countT_filled"], 1)
                pe.wait_ge(S["countT_kept"], NT)

            turn_norm(x_mix, warm=7)

            def gat_scores(l):
                if l > 0:
                    pe.wait_ge(S["gatin_ready"], KD * l)
                else:
                    pe.wait_ge(S["gatw_ready"], GAT * 2 * KD)
                    pe.wait_ge(S["count_kept"], NT)
                for i in range(NT):
                    if i >= 2:
                        pe.wait_ge(S["h_kept"], NT * l + i - 1)
                    c = (i % 2) * 512
                    product(gps[:, c:c + D + 2], [(part(gat_in, k, i), gat_w[:, l, k, :]) for k in range(KD)])\
                        .then_inc(S["h_filled"], 1)
                pe.wait_ge(S["h_kept"], NT * (l + 1))
                spread(lambda i: score[:, i, 0:1], gps[:, 0:NP]).then_inc(S["srow_filled"], 1)

            def gat_shifts(l):
                pe.wait_ge(S["shift_ready"], l + 1)
                spread(lambda i: shift[:, 0, i:i + 1], gps[:, 0:NP]).then_inc(S["r1_filled"], 1)
                spread(lambda i: shift[:, 1, i:i + 1], bank(4)).then_inc(S["r2_filled"], 1)

            def gat_sum(l):
                pe.wait_ge(S["prob_ready"], NT * (l + 1))
                for i in range(NT):
                    if i >= 2:
                        pe.wait_ge(S["agg_copied"], NT * l + i - 1)
                    c = (i % 2) * 512
                    product(gps[:, c:c + D + 1], [(part(prob, s, i), gat_h[:, s, :]) for s in range(NT)])\
                        .then_inc(S["agg_filled"], 1)

            def gat_turn(l, k):
                pe.wait_ge(S["agg_kept"], l + 1)
                if k:
                    pe.wait_ge(S["gatT_kept"], KD * l + 1)
                turn(gat_out, k, gps[:, 0:NP]).then_inc(S["gatT_filled"], 1)

            def weight(w, n):
                return w[:, n * KD * D:(n + 1) * KD * D].rearrange("p (k d) -> p k d", k=KD)

            def tokens_by(src, w, c0, filled=None):
                for i in range(NT):
                    ins = product(mps[:, c0 + i * D:c0 + (i + 1) * D], [(part(src, k, i), w[:, k, :]) for k in range(KD)])
                    if filled and (i % 2 or i == NT - 1):
                        ins.then_inc(S[filled], 1)
                return ins

            def up(u0, tiles_, srcs, w):
                for j in range(tiles_):
                    u = u0 + j
                    if u >= 2:
                        pe.wait_ge(S["up_kept"], u - 1)
                    product(bank(2 * (u % 2)), [(w[:, k, j * P:(j + 1) * P], src) for k, src in enumerate(srcs)])\
                        .then_inc(S["up_filled"], 1)

            for i in range(DEPTH):
                if i >= 1:
                    gat_sum(i - 1)
                turn_norm(normed, warm=12 if i == 0 else 0)
                norm_turned()
                pe.wait_ge(S["mixw_loaded"], 16 * (i + 1))
                w = mix_w
                tokens_by(normed_T, weight(w, 0), 0).then_inc(S["qv_filled"], 1)
                if i == 0:
                    pe.wait_ge(S["span_ready"], 1)
                    count_block(0)
                tokens_by(normed_T, weight(w, 2), 3 * 512).then_inc(S["qv_filled"], 1)
                for m in range(KD):
                    pe.wait_ge(S["q_shifted" if m == 0 else "v_kept"], i + 1)
                    product(bank(2 * m), [(weight(w, 1)[:, k, m * P:(m + 1) * P], normed_T[:, k, :]) for k in range(KD)])\
                        .then_inc(S["k_filled"], 1)
                if i == 0:
                    count_block(1)
                elif i < GAT:
                    gat_turn(i - 1, 0)
                pe.wait_ge(S["q_normed"], i + 1)
                turn(q_tok, 0, bank(4)).then_inc(S["qT_filled"], 1)
                if 1 <= i < GAT:
                    gat_turn(i - 1, 1)
                pe.wait_ge(S["k_exped"], KD * i + 1)
                turn(q_tok, 1, bank(0)).then_inc(S["qT_filled"], 1)
                pe.wait_ge(S["k_exped"], KD * i + 2)
                for m, b in ((0, 2), (1, 4)):
                    if m:
                        pe.wait_ge(S["qT_dve"], i + 1)
                    for j in range(NT):
                        ins = pe.transpose(mps[:, b * 512 + j * P:b * 512 + (j + 1) * P], part(k_exp, m, j), ident[:])
                    ins.then_inc(S["kT_filled"], 1)
                if i == 0:
                    count_block(2)
                pe.wait_ge(S["qT_act"], i + 1)
                pe.wait_ge(S["kT_dve"], i + 1)
                pe.wait_ge(S["kT_act"], i + 1)
                for m in range(KD):
                    ins = product(mps[:, m * 256:m * 256 + P],
                                  [(k_tok[:, j, m * P:(m + 1) * P], v_tok[:, j, m, 0:P]) for j in range(NT)])
                ins.then_inc(S["ctx_filled"], 1)
                if i == 0:
                    count_block(3)
                pe.wait_ge(S["ctx_kept"], i + 1)
                for m, b in ((0, 2), (1, 4)):
                    product(bank(b), [(context[:, m, 0:P], q_T[:, m, :])]).then_inc(S["att_filled"], 1)
                if i == 0:
                    count_block(4)
                pe.wait_ge(S["att_dve"], i + 1)
                pe.wait_ge(S["att_act"], i + 1)
                tokens_by(att_T, weight(w, 3), 0, "proj_filled")
                if i < GAT:
                    gat_scores(i)
                turn_norm(normed, warm=6 if i < GAT else 20)
                norm_turned()
                pe.wait_ge(S["ffw_loaded%d" % (i % 2)], 32 * (i // 2 + 1))
                srcs, wu = [normed_T[:, k, :] for k in range(KD)], expert_up(FF, i % 2)
                up(8 * i, 4, srcs, wu)
                if i == 0:
                    turn_counts()
                if i < GAT:
                    gat_shifts(i)
                up(8 * i + 4, 4, srcs, wu[:, :, 4 * P:])
                pe.wait_ge(S["up_kept"], 8 * (i + 1))
                wd = expert_down(FF, i % 2)
                for j in range(NT):
                    ins = product(mps[:, j * D:(j + 1) * D], [(part(hidden, h, j), wd[:, h, :]) for h in range(FF // P)])
                    if j % 2 or j == NT - 1:
                        ins.then_inc(S["down_filled"], 1)

            def moe(m, experts, width):
                turn_norm(normed, warm=18 if m == 0 else 30)
                norm_turned()
                if m == 0:
                    pe.wait_ge(S["agg_kept"], GAT)
                else:
                    pe.wait_ge(S["hT_kept"], HEADS)
                pe.wait_ge(S["small_loaded"], 16 * 5)
                w = gate_w[:, :, 0:E0] if m == 0 else gate_w[:, :, E0:E0 + E1]
                for i in range(NT):
                    ins = product(gps[:, i * experts:(i + 1) * experts], [(part(normed_T, k, i), w[:, k, :]) for k in range(KD)])
                ins.then_inc(S["gate_filled"], 1)
                pe.wait_ge(S["chosen_ready"], m + 1)
                pe.matmul(gps[:, 0:NT * experts], below[:], both[:, :, 0:experts],
                          start=True, stop=True)
                pe.matmul(gps[:, 512:512 + NT * experts], ones[:], both[:, :, 0:experts], start=True, stop=True)\
                    .then_inc(S["ranks_filled"], 1)
                pe.wait_ge(S["comb_ready"], m + 1)
                for i in range(NT):
                    ins = pe.transpose(mps[0:experts, 3 * 512 + i * P:3 * 512 + (i + 1) * P], comb[:, i, 0:experts], ident[:])
                ins.then_inc(S["combT_filled"], 1)
                pe.wait_ge(S["combT_kept"], m + 1)
                for i in range(NT):
                    ins = pe.matmul(mps[:, i * D:(i + 1) * D], comb_T[0:experts, i * P:(i + 1) * P], moe_b2[0:experts, m, :],
                                    start=True, stop=True)
                ins.then_inc(S["moe_bias_filled"], 1)
                pe.wait_ge(S["moe_bias_kept"], m + 1)
                pe.wait_ge(S["scattered"], 16 * 2 * NT * (m + 1))
                keep_warm(4)
                J = width // P
                Q = J // 4

                def turn_chunk(n):
                    pe.wait_ge(S["x_copied"], n)
                    for k in range(KD):
                        ins = pe.transpose(gps[:, k * P:(k + 1) * P], x_chunk[:, k * P:(k + 1) * P], ident[:])
                    ins.then_inc(S["x_turned"], 1)

                pe.reg_add(copied_no, copied_no, 1)
                turn_chunk(pe.snap(copied_no))
                pe.reg_add(kept_no, kept_no, 1)
                for e in range(experts):
                    if m == 0:
                        r, u = DEPTH + e, (DEPTH + e) % 2
                        pe.wait_ge(S["ffw_loaded%d" % u], 32 * (r // 2 + 1))
                    else:
                        u = e % 4
                        pe.wait_ge(S["expert_loaded%d" % u], 32 * (e // 4 + 1))
                    wu, wd = expert_up(width, u), expert_down(width, u)
                    n = pe.value_load(chunk_i[0:1, e:e + 1], min_val=1, max_val=NT)
                    with pe.Fori(0, n):
                        pe.wait_ge(S["xT_kept"], pe.snap(kept_no))
                        for h in range(2):
                            pe.reg_add(free_no, free_no, 1)
                            free = pe.snap(free_no)
                            pe.wait_ge(S["half_act"], free)
                            pe.wait_ge(S["half_dve"], free)
                            for q in range(2 * Q):
                                c = 1024 * h + 512 * (q // Q) + (q % Q) * P
                                ins = product(mps[:, c:c + P], [(wu[:, k, (2 * h * Q + q) * P:(2 * h * Q + q + 1) * P], xT_chunk[:, k, :])
                                                                for k in range(KD)])
                            ins.then_inc(S["half_filled"], 1)
                        pe.reg_add(copied_no, copied_no, 1)
                        turn_chunk(pe.snap(copied_no))
                        pe.reg_add(kept_no, kept_no, 1)
                        for h in range(2):
                            kept = pe.snap(free_no) + 1 + h
                            pe.wait_ge(S["half_act"], kept)
                            pe.wait_ge(S["half_dve"], kept)
                            for j in range(2 * h * Q, 2 * (h + 1) * Q):
                                ins = pe.matmul(gps[:, 512:512 + D], hid_chunk[:, j, :], wd[:, j, :], start=(j == 0), stop=(j == J - 1))
                        ins.then_inc(S["y_filled"], 1)

            copied_no = pe.alloc_register("pe_copied")
            kept_no = pe.alloc_register("pe_kept")
            free_no = pe.alloc_register("pe_free")
            pe.sem_inc(S["half_act"], 2)
            pe.sem_inc(S["half_dve"], 2)
            for r in (copied_no, kept_no, free_no):
                pe.reg_mov(r, 0)
            moe(0, E0, H0)

            pe.wait_ge(S["gathered%d" % (NT - 1)], 32)
            turn_norm(xn_tok, warm=18)
            norm_turned()
            pe.wait_ge(S["mixw_loaded"], 16 * (DEPTH + 1))
            w = mix_w
            for i in range(NT):
                ins = product(gps[:, i * 16:(i + 1) * 16], [(part(normed_T, k, i), uv_w[:, k, :]) for k in range(KD)])
            ins.then_inc(S["uv_filled"], 1)

            def head_row(h):
                if h == 0:
                    pe.wait_ge(S["uv_ready"], 1)
                else:
                    pe.wait_ge(S["hmax_done"], h)
                spread(lambda i: su[:, i, h:h + 1], gps[:, 0:NP]).then_inc(S["hrow_filled"], 1)

            for m in range(KD):
                product(bank(2 * m), [(weight(w, 0)[:, k, m * P:(m + 1) * P], normed_T[:, k, :]) for k in range(KD)])\
                    .then_inc(S["qk_filled"], 1)
            head_row(0)
            pe.wait_ge(S["qk_min"], 1)
            tokens_by(normed_T, weight(w, 1), 0).then_inc(S["qv_filled"], 1)
            tokens_by(normed_T, weight(w, 2), 3 * 512).then_inc(S["qv_filled"], 1)
            head_row(1)
            pe.wait_ge(S["qk_ready"], 2)
            pe.wait_ge(S["v_kept"], DEPTH + 1)
            for m in range(KD):
                ins = product(mps[:, m * 256:m * 256 + P + 1],
                              [(k_tok[:, j, m * P:(m + 1) * P], v_tok[:, j, m, :]) for j in range(NT)])
            ins.then_inc(S["ctx_filled"], 1)
            head_row(2)
            pe.wait_ge(S["ctx_kept"], DEPTH + 1)
            for i in range(NT):
                for m in range(KD):
                    c = i * 512 + m * (P + 4)
                    ins = product(mps[:, c:c + P + 4], [(part(q_T, m, i), context[:, m, :])])
            ins.then_inc(S["num_filled"], 1)
            head_row(3)
            pe.wait_ge(S["num_kept"], 1)
            turn(q_tok, 0, bank(4)).then_inc(S["qT_filled"], 1)
            turn(q_tok, 1, bank(2)).then_inc(S["qT_filled"], 1)
            head_row(4)
            pe.wait_ge(S["att_dve"], DEPTH + 1)
            pe.wait_ge(S["att_act"], DEPTH + 1)
            tokens_by(att_T, weight(w, 3), 0, "proj_filled")
            head_row(5)
            turn_norm(normed, warm=8)
            norm_turned()
            pe.wait_ge(S["ffw_loaded0"], 32 * ((DEPTH + E0) // 2 + 1))
            w1 = ff_w1[:, 0, :].rearrange("p (k h) -> p k h", k=4)
            w2 = ff_w2[:, 0, 0:4 * D].rearrange("p (k d) -> p k d", k=4)

            def head_shifts(h):
                pe.wait_ge(S["hr1_used"], h) if h else pe.wait_ge(S["hshift_ready"], 1)
                spread(lambda i: hs1[:, i, h:h + 1], gps[:, 0:NP]).then_inc(S["hr1_filled"], 1)
                if h:
                    pe.wait_ge(S["exp_ready"], NT * (GAT + h))
                spread(lambda i: hs2[:, i, h:h + 1], bank(4)).then_inc(S["hr2_filled"], 1)

            def head_aggregate(h):
                if h == 0:
                    pe.wait_ge(S["down_kept"], 1)
                else:
                    pe.wait_ge(S["hagg_kept"], h)
                for s in range(NT):
                    pe.wait_ge(S["prob_ready"], NT * (GAT + h) + s + 1)
                    for c, n in ((0, 512), (512, P)):
                        ins = pe.matmul(mps[0:DH + 1, c:c + n], xh[:, s, h, :], head_prob[h % 2][:, s, c:c + n],
                                        start=(s == 0), stop=(s == NT - 1))
                ins.then_inc(S["hagg_filled"], 1)

            def head_turn(h):
                pe.wait_ge(S["hagg_kept"], h + 1)
                if h >= 2:
                    pe.wait_ge(S["hT_kept"], h - 1)
                for i in range(NT):
                    c = 1024 + 512 * (h % 2) + i * (DH + 1)
                    ins = pe.transpose(mps[:, c:c + DH + 1], head_T[:, i * P:(i + 1) * P], ident[0:DH + 1, 0:DH + 1])
                ins.then_inc(S["hT_filled"], 1)

            u0 = DEPTH * 8
            srcs = [normed_T[:, 0, :], normed_T[:, 1, :], att_T[:, 0, :], att_T[:, 1, :]]
            up(u0, 1, srcs, w1)
            head_row(6)
            up(u0 + 1, 1, srcs, w1[:, :, P:])
            head_row(7)
            up(u0 + 2, 1, srcs, w1[:, :, 2 * P:])
            head_shifts(0)
            up(u0 + 3, 1, srcs, w1[:, :, 3 * P:])
            pe.wait_ge(S["up_kept"], u0 + 4)
            for j in range(NT):
                ins = product(mps[:, j * D:(j + 1) * D], [(part(hidden2, h, j), w2[:, h, :]) for h in range(4)])
                if j % 2 or j == NT - 1:
                    ins.then_inc(S["down_filled"], 1)
            pe.wait_ge(S["xh_ready"], 1)
            for h in range(HEADS):
                if h + 1 < HEADS:
                    head_shifts(h + 1)
                if h:
                    head_turn(h - 1)
                head_aggregate(h)
            head_turn(HEADS - 1)
            moe(1, E1, H1)


def kernel(**inputs):
    import numpy as np
    import concourse.bacc as bacc
    from concourse.bass_utils import run_bass_kernel_spmd as run

    a = {k: np.asarray(v) for k, v in inputs.items()}

    def halves(w):
        *lead, r, c = w.shape
        w = w.reshape(*lead, r // P, P, c)
        return np.ascontiguousarray(np.swapaxes(w, -3, -2)).reshape(*lead, P, r // P * c)

    def column(v):
        return v.reshape(-1, P).T

    arrays = {"x": a["x"], "src": a["src"].reshape(ET, EP).T, "dst": a["dst"].reshape(ET, EP).T}
    cols = np.zeros((P, NCOL), np.float32)
    names = {"gat_b": "L0_gnn_b%d", "gamma": "L0_gnn_gamma%d", "beta": "L0_gnn_beta%d"}
    stacked = {"ln1_g": "L0_mix_ln1_g", "ln1_b": "L0_mix_ln1_b", "ln2_g": "L0_mix_ln2_g", "ln2_b": "L0_mix_ln2_b",
               "ff_b1": "L0_mix_b1"}
    for (n, l), c in COLS.items():
        if n in names:
            v = a[names[n] % l]
        elif n in stacked:
            v = a[stacked[n]][l]
        else:
            v = a["L1_mix_" + n[2:]]
        cols[:, c:c + v.size // P] = column(v)
    arrays["cols"] = cols
    rows = np.zeros((1, NROW), np.float32)
    plain = {"gat_b2": "L0_gnn_b2", "bg": "L0_ffn_bg", "b_u": "L1_gnn_b_u", "m_g2": "L1_mix_g2", "m_b2": "L1_mix_b2",
             "gate_b": "L1_ffn_gate_b", "gamma_out": "L1_ffn_gamma", "beta_out": "L1_ffn_beta"}
    for (n, l), c in ROWS.items():
        if n in ("bo", "ff_b2"):
            v = a["L0_mix_" + n[-2:]][l]
        else:
            v = a[plain[n]]
        rows[0, c:c + v.size] = v
    arrays["rows"] = rows
    arrays["gat_w"] = np.stack([halves(a["L0_gnn_W%d" % l]).reshape(P, KD, D) for l in range(GAT)], 1)
    arrays["mix_w"] = np.concatenate([halves(a["L0_mix_" + n]) for n in ("Wq", "Wk", "Wv", "Wo")], -1)
    arrays["ff_w1"], arrays["ff_w2"] = halves(a["L0_mix_W1"]), halves(a["L0_mix_W2"])
    arrays["moe0_w1"] = halves(a["L0_ffn_W1"].transpose(0, 2, 1))
    arrays["moe0_w2"] = halves(a["L0_ffn_W2"].transpose(0, 2, 1))
    arrays["moe1_w1"], arrays["moe1_w2"] = halves(a["L1_ffn_w1"]), halves(a["L1_ffn_w2"])
    arrays["moe0_b2"], arrays["moe1_b2"] = a["L0_ffn_b2"], a["L1_ffn_b2"]
    arrays["moe_b1"] = np.stack([column(a["L0_ffn_b1"].reshape(-1)), column(a["L1_ffn_b1"].reshape(-1))], 1)
    arrays["gate_w"] = np.concatenate([halves(a["L0_ffn_Wg"].T).reshape(P, KD, E0), halves(a["L1_ffn_gate_w"]).reshape(P, KD, E1)], -1)
    arrays["uv_w"] = np.concatenate([halves(a["L1_gnn_W_u"].T).reshape(P, KD, HEADS), halves(a["L1_gnn_W_v"].T).reshape(P, KD, HEADS)], -1)
    arrays["mix1_qkvm"] = np.concatenate([halves(a["L1_mix_" + n]) for n in ("Wq", "Wk", "Wv", "Wm")], -1)
    arrays["mix1_w1"] = halves(a["L1_mix_W1"])
    arrays["mix1_w2"] = halves(a["L1_mix_W2"])
    arrays["a_rows"] = np.concatenate([a["L0_gnn_a_%s%d" % (n, l)] for l in range(GAT) for n in ("src", "dst")])[None, :]

    nc = bacc.Bacc("TRN2", target_bir_lowering=False, num_devices=1)
    t, feed = {}, {}
    for name, v in arrays.items():
        v = np.ascontiguousarray(v)
        feed["in_" + name] = v
        t[name] = nc.dram_tensor("in_" + name, v.shape, mybir.dt.from_np(v.dtype), kind="ExternalInput").ap()
    t["out"] = nc.dram_tensor("out", (N, D), F32, kind="ExternalOutput").ap()
    build(nc, t)
    r = run(nc, [feed], core_ids=[0])
    return r.results[0]["out"]
```
